# Optimizing a Trainium2 kernel written in Bass

```python
import numpy as np
import jax
import jax.numpy as jnp

def _softmax(x, axis=-1):
    return jax.nn.softmax(x, axis=axis)

def _gelu(x):
    return jax.nn.gelu(x, approximate=True)

def _silu(x):
    return jax.nn.silu(x)

def _sigmoid(x):
    return jax.nn.sigmoid(x)

def _layernorm(x, axis=-1, eps=1e-05):
    m = jnp.mean(x, axis=axis, keepdims=True)
    v = jnp.var(x, axis=axis, keepdims=True)
    return (x - m) / jnp.sqrt(v + eps)

def _scatter_add(tgt, idx, src, axis=0):
    return tgt.at[idx].add(src)

def _segment_sum(src, seg, n):
    return jax.ops.segment_sum(src, seg, n)
kernel_name = 'mk_conv_seq_d4_conv_nchw512_r2_53d69e'

def setup_inputs(seed: int=0):
    np.random.seed(seed)
    _w = jnp.asarray

    def _rec_inputs():
        import jax
        import jax.numpy as jnp
        _gk = jax.random.key(seed)
        x = -0.0003929 + 0.9999 * jax.random.normal(jax.random.fold_in(_gk, 1), (8, 256, 32, 32), jnp.float32)
        return x
    x = _rec_inputs()

    def _L0_conv_setup():
        import jax, jax.numpy as jnp
        import numpy as np
        LATENT_CH = 32

        def conv1x1(x, w):
            gain = 1.0 / np.sqrt(w.shape[1])
            return jnp.einsum('bchw,oc->bohw', x, w * gain)

        def casual_attention(q, k, v):
            score = jnp.einsum('bcn,bcm->bnm', q, k)
            score = jax.nn.softmax(score, axis=-1)
            return jnp.einsum('bnm,bcm->bnc', score, v)
        key = jax.random.key(seed)
        ks = jax.random.split(key, 8)
        B, C, H, W = (8, 256, 32, 32)
        L, P = (LATENT_CH, 128)
        return {'feature_map': jax.random.normal(ks[0], (B, C, H, W), jnp.float32), 'concepts': jax.random.normal(ks[1], (P, L), jnp.float32), 'w_theta': jax.random.normal(ks[2], (L, C), jnp.float32), 'w_phi': jax.random.normal(ks[3], (L, C), jnp.float32), 'w_g': jax.random.normal(ks[4], (L, C), jnp.float32), 'w_o': jax.random.normal(ks[5], (C, L), jnp.float32), 'gamma_sa': jnp.float32(0.1), 'gamma_moca': jnp.float32(0.1)}
    _L0_conv_all = _L0_conv_setup()
    _L0_conv_in = {k: v for k, v in _L0_conv_all.items() if k in ('concepts', 'w_theta', 'w_phi', 'w_g', 'w_o', 'gamma_sa', 'gamma_moca')}
    del _L0_conv_all

    def _L1_conv_setup():
        import jax, jax.numpy as jnp
        import numpy as np
        key = jax.random.key(seed)
        ks = jax.random.split(key, 5)
        B, C, H, W = (16, 256, 32, 32)
        K = 10
        return {'x': jax.random.normal(ks[0], (B, C, H, W), dtype=jnp.float32), 'conv_w': jax.random.normal(ks[1], (K, C), dtype=jnp.float32) * (1.0 / np.sqrt(C)), 'conv_b': jax.random.normal(ks[2], (K,), dtype=jnp.float32) * 0.01, 'lin1_w': jax.random.normal(ks[3], (4 * K, K), dtype=jnp.float32) * (1.0 / np.sqrt(K)), 'lin2_w': jax.random.normal(ks[4], (K, 4 * K), dtype=jnp.float32) * (1.0 / np.sqrt(4 * K)), 'gamma': jnp.ones((1,), dtype=jnp.float32)}
    _L1_conv_all = _L1_conv_setup()
    _L1_conv_in = {k: v for k, v in _L1_conv_all.items() if k in ('conv_w', 'conv_b', 'lin1_w', 'lin2_w', 'gamma')}
    del _L1_conv_all

    def _L2_conv_setup():
        import jax, jax.numpy as jnp
        import numpy as np
        N_GROUPS = 32
        N_HEADS = 8
        EPS = 1e-05

        def group_norm(x, scale, bias):
            B, C, T = x.shape
            xg = x.reshape(B, N_GROUPS, C // N_GROUPS, T).astype(jnp.float32)
            mean = xg.mean(axis=(2, 3), keepdims=True)
            var = xg.var(axis=(2, 3), keepdims=True)
            xn = ((xg - mean) * jax.lax.rsqrt(var + EPS)).reshape(B, C, T)
            return (xn * scale[None, :, None] + bias[None, :, None]).astype(x.dtype)
        key = jax.random.key(seed)
        ks = jax.random.split(key, 5)
        B, C, H, W = (8, 256, 32, 32)
        x = jax.random.normal(ks[0], (B, C, H, W), dtype=jnp.float32)
        gn_scale = jnp.ones((C,), dtype=jnp.float32)
        gn_bias = jnp.zeros((C,), dtype=jnp.float32)
        w_qkv = jax.random.normal(ks[1], (3 * C, C), dtype=jnp.float32) * C ** (-0.5)
        b_qkv = jax.random.normal(ks[2], (3 * C,), dtype=jnp.float32) * 0.02
        w_proj = jax.random.normal(ks[3], (C, C), dtype=jnp.float32) * C ** (-0.5)
        b_proj = jax.random.normal(ks[4], (C,), dtype=jnp.float32) * 0.02
        return {'x': x, 'gn_scale': gn_scale, 'gn_bias': gn_bias, 'w_qkv': w_qkv, 'b_qkv': b_qkv, 'w_proj': w_proj, 'b_proj': b_proj}
    _L2_conv_all = _L2_conv_setup()
    _L2_conv_in = {k: v for k, v in _L2_conv_all.items() if k in ('gn_scale', 'gn_bias', 'w_qkv', 'b_qkv', 'w_proj', 'b_proj')}
    del _L2_conv_all

    def _L3_conv_setup():
        import jax, jax.numpy as jnp
        import numpy as np
        NUM_HEADS = 8
        GROUPS = 32
        EPS = 1e-05
        key = jax.random.key(seed)
        k1, k2, k3 = jax.random.split(key, 3)
        B, C, H, W = (16, 256, 32, 32)
        x = jax.random.normal(k1, (B, C, H, W), dtype=jnp.float32)
        scale = C ** (-0.5)
        return {'x': x, 'norm_w': jnp.ones((C,), jnp.float32), 'norm_b': jnp.zeros((C,), jnp.float32), 'qkv_w': jax.random.normal(k2, (3 * C, C), dtype=jnp.float32) * scale, 'qkv_b': jnp.zeros((3 * C,), jnp.float32), 'proj_w': jax.random.normal(k3, (C, C), dtype=jnp.float32) * scale, 'proj_b': jnp.zeros((C,), jnp.float32)}
    _L3_conv_all = _L3_conv_setup()
    _L3_conv_in = {k: v for k, v in _L3_conv_all.items() if k in ('norm_w', 'norm_b', 'qkv_w', 'qkv_b', 'proj_w', 'proj_b')}
    del _L3_conv_all
    return {'x': x, 'L0_conv_concepts': _L0_conv_in['concepts'], 'L0_conv_w_theta': _L0_conv_in['w_theta'], 'L0_conv_w_phi': _L0_conv_in['w_phi'], 'L0_conv_w_g': _L0_conv_in['w_g'], 'L0_conv_w_o': _L0_conv_in['w_o'], 'L0_conv_gamma_sa': _L0_conv_in['gamma_sa'], 'L0_conv_gamma_moca': _L0_conv_in['gamma_moca'], 'L1_conv_conv_w': _L1_conv_in['conv_w'], 'L1_conv_conv_b': _L1_conv_in['conv_b'], 'L1_conv_lin1_w': _L1_conv_in['lin1_w'], 'L1_conv_lin2_w': _L1_conv_in['lin2_w'], 'L1_conv_gamma': _L1_conv_in['gamma'], 'L2_conv_gn_scale': _L2_conv_in['gn_scale'], 'L2_conv_gn_bias': _L2_conv_in['gn_bias'], 'L2_conv_w_qkv': _L2_conv_in['w_qkv'], 'L2_conv_b_qkv': _L2_conv_in['b_qkv'], 'L2_conv_w_proj': _L2_conv_in['w_proj'], 'L2_conv_b_proj': _L2_conv_in['b_proj'], 'L3_conv_norm_w': _L3_conv_in['norm_w'], 'L3_conv_norm_b': _L3_conv_in['norm_b'], 'L3_conv_qkv_w': _L3_conv_in['qkv_w'], 'L3_conv_qkv_b': _L3_conv_in['qkv_b'], 'L3_conv_proj_w': _L3_conv_in['proj_w'], 'L3_conv_proj_b': _L3_conv_in['proj_b']}

def reference(x, L0_conv_concepts, L0_conv_w_theta, L0_conv_w_phi, L0_conv_w_g, L0_conv_w_o, L0_conv_gamma_sa, L0_conv_gamma_moca, L1_conv_conv_w, L1_conv_conv_b, L1_conv_lin1_w, L1_conv_lin2_w, L1_conv_gamma, L2_conv_gn_scale, L2_conv_gn_bias, L2_conv_w_qkv, L2_conv_b_qkv, L2_conv_w_proj, L2_conv_b_proj, L3_conv_norm_w, L3_conv_norm_b, L3_conv_qkv_w, L3_conv_qkv_b, L3_conv_proj_w, L3_conv_proj_b):
    import jax
    import jax.numpy as jnp

    def _L0_conv_ref(feature_map, concepts, w_theta, w_phi, w_g, w_o, gamma_sa, gamma_moca):
        import jax, jax.numpy as jnp
        import numpy as np
        LATENT_CH = 32

        def conv1x1(x, w):
            gain = 1.0 / np.sqrt(w.shape[1])
            return jnp.einsum('bchw,oc->bohw', x, w * gain)

        def casual_attention(q, k, v):
            score = jnp.einsum('bcn,bcm->bnm', q, k)
            score = jax.nn.softmax(score, axis=-1)
            return jnp.einsum('bnm,bcm->bnc', score, v)
        B, C, H, W = feature_map.shape
        L = LATENT_CH
        HW = H * W
        th = conv1x1(feature_map, w_theta).reshape(B, L, HW)
        ph = conv1x1(feature_map, w_phi).reshape(B, L, HW)
        g = conv1x1(feature_map, w_g).reshape(B, L, HW)
        lat = casual_attention(th, ph, g).reshape(B, L, H, W)
        sa_out = gamma_sa * conv1x1(lat, w_o) + feature_map
        enc = conv1x1(sa_out, w_theta).reshape(B, L, HW)
        phi_c = concepts.T[None]
        phi_c = jnp.broadcast_to(phi_c, (B, L, concepts.shape[0]))
        lat2 = casual_attention(enc, phi_c, phi_c).reshape(B, L, H, W)
        out = gamma_moca * conv1x1(lat2, w_o) + sa_out
        return out

    def _L1_conv_ref(x, conv_w, conv_b, lin1_w, lin2_w, gamma):
        import jax, jax.numpy as jnp
        import numpy as np
        out_map = jnp.einsum('bchw,kc->bkhw', x, conv_w) + conv_b[None, :, None, None]
        prob = jax.lax.stop_gradient(out_map)
        wgt = jax.lax.stop_gradient(conv_w)
        norm_map = jnp.linalg.norm(prob, axis=1)
        norm_wgt = jnp.linalg.norm(wgt, axis=1)
        prob = prob / norm_wgt[None, :, None, None] / norm_map[:, None, :, :]
        pooled = prob.mean(axis=(2, 3))
        h = jax.nn.relu(pooled @ lin1_w.T)
        ratio = jax.nn.sigmoid(h @ lin2_w.T)
        out = jnp.einsum('bkhw,kc,bk->bchw', prob, wgt, ratio)
        return gamma[0] * out + x

    def _L2_conv_ref(x, gn_scale, gn_bias, w_qkv, b_qkv, w_proj, b_proj):
        import jax, jax.numpy as jnp
        import numpy as np
        N_GROUPS = 32
        N_HEADS = 8
        EPS = 1e-05

        def group_norm(x, scale, bias):
            B, C, T = x.shape
            xg = x.reshape(B, N_GROUPS, C // N_GROUPS, T).astype(jnp.float32)
            mean = xg.mean(axis=(2, 3), keepdims=True)
            var = xg.var(axis=(2, 3), keepdims=True)
            xn = ((xg - mean) * jax.lax.rsqrt(var + EPS)).reshape(B, C, T)
            return (xn * scale[None, :, None] + bias[None, :, None]).astype(x.dtype)
        B, C, H, W = x.shape
        T = H * W
        x2 = x.reshape(B, C, T)
        xn = group_norm(x2, gn_scale, gn_bias)
        qkv = jnp.einsum('oc,bct->bot', w_qkv, xn) + b_qkv[None, :, None]
        ch = C // N_HEADS
        qkv = qkv.reshape(B * N_HEADS, 3 * ch, T)
        q, k, v = (qkv[:, :ch], qkv[:, ch:2 * ch], qkv[:, 2 * ch:])
        scale = ch ** (-0.25)
        weight = jnp.einsum('bct,bcs->bts', q * scale, k * scale)
        weight = jax.nn.softmax(weight.astype(jnp.float32), axis=-1).astype(weight.dtype)
        a = jnp.einsum('bts,bcs->bct', weight, v)
        h = a.reshape(B, C, T)
        h = jnp.einsum('oc,bct->bot', w_proj, h) + b_proj[None, :, None]
        return (x2 + h).reshape(B, C, H, W)

    def _L3_conv_ref(x, norm_w, norm_b, qkv_w, qkv_b, proj_w, proj_b):
        import jax, jax.numpy as jnp
        import numpy as np
        NUM_HEADS = 8
        GROUPS = 32
        EPS = 1e-05
        B, C, H, W = x.shape
        N = H * W
        nh = NUM_HEADS
        hd = C // nh
        xg = x.reshape(B, GROUPS, C // GROUPS, N)
        mu = xg.mean(axis=(2, 3), keepdims=True)
        var = xg.var(axis=(2, 3), keepdims=True)
        h = ((xg - mu) * jax.lax.rsqrt(var + EPS)).reshape(B, C, N)
        h = h * norm_w[None, :, None] + norm_b[None, :, None]
        h = h.transpose(0, 2, 1)
        qkv = (h @ qkv_w.T + qkv_b).reshape(B, N, 3, nh, hd)
        q, k, v = (qkv[:, :, 0], qkv[:, :, 1], qkv[:, :, 2])
        attn = jnp.einsum('bnhd,bngd->bnhg', q, k) * hd ** (-0.5)
        attn = jax.nn.softmax(attn, axis=-1)
        o = jnp.einsum('bnhg,bngd->bnhd', attn, v).reshape(B, N, C)
        o = o @ proj_w.T + proj_b
        return x + o.transpose(0, 2, 1).reshape(B, C, H, W)

    def _gn(v, G=32, eps=1e-05):
        B_, C_, H_, W_ = v.shape
        g = v.reshape(B_, G, C_ // G, H_, W_)
        m = jnp.mean(g, axis=(2, 3, 4), keepdims=True)
        s = jnp.var(g, axis=(2, 3, 4), keepdims=True)
        return ((g - m) / jnp.sqrt(s + eps)).reshape(v.shape)

    def _ln_c(v, eps=1e-06):
        m = jnp.mean(v, axis=1, keepdims=True)
        s = jnp.var(v, axis=1, keepdims=True)
        return (v - m) / jnp.sqrt(s + eps)

    def _ln_t(v, eps=1e-05):
        m = jnp.mean(v, axis=-1, keepdims=True)
        s = jnp.var(v, axis=-1, keepdims=True)
        return (v - m) / jnp.sqrt(s + eps)

    def _to_tokens(v):
        B_, C_, H_, W_ = v.shape
        return v.reshape(B_, C_, H_ * W_).transpose(0, 2, 1)

    def _from_tokens(t, like):
        B_, C_, H_, W_ = like.shape
        return t.transpose(0, 2, 1).reshape(B_, C_, H_, W_)
    x = _L0_conv_ref(x, L0_conv_concepts, L0_conv_w_theta, L0_conv_w_phi, L0_conv_w_g, L0_conv_w_o, L0_conv_gamma_sa, L0_conv_gamma_moca)
    x = _L1_conv_ref(x, L1_conv_conv_w, L1_conv_conv_b, L1_conv_lin1_w, L1_conv_lin2_w, L1_conv_gamma)
    x = _L2_conv_ref(x, L2_conv_gn_scale, L2_conv_gn_bias, L2_conv_w_qkv, L2_conv_b_qkv, L2_conv_w_proj, L2_conv_b_proj)
    x = _L3_conv_ref(x, L3_conv_norm_w, L3_conv_norm_b, L3_conv_qkv_w, L3_conv_qkv_b, L3_conv_proj_w, L3_conv_proj_b)
    return x

_drawn_inputs = setup_inputs


def setup_inputs(seed=0):
    import zlib

    import numpy as np

    out = dict(_drawn_inputs(seed))
    spreads = {'L2_conv_gn_scale': (1.0, 0.2),
     'L2_conv_gn_bias': (0.0, 0.1),
     'L3_conv_norm_w': (1.0, 0.2),
     'L3_conv_norm_b': (0.0, 0.1),
     'L3_conv_qkv_b': (0.0, 0.1),
     'L3_conv_proj_b': (0.0, 0.1)}
    factors = {'L1_conv_conv_b': 37.052, 'L1_conv_lin1_w': 31.683, 'L1_conv_lin2_w': 31.539}
    for name, (base, spread) in spreads.items():
        noise = np.random.default_rng([zlib.crc32(name.encode()), seed]).standard_normal(out[name].shape)
        drawn = base * np.exp(spread * noise) if base else spread * noise
        out[name] = jnp.asarray(drawn.astype(out[name].dtype))
    for name, factor in factors.items():
        out[name] = (out[name] * factor).astype(out[name].dtype)
    return out
```

```python
from contextlib import ExitStack

import concourse.bass as bass
from concourse import mybir

B, C, N, P = 8, 256, 1024, 128
CT = C // P
HALF = 512
MT = N // P
D = 32
H = P // D
K = 10
STEPS = 2 * MT
PAIRS = 2 * STEPS
POOL_TILES = (0, 1, 3, 5)
POOL_SUMS = len(POOL_TILES) - 1
FIRST_SUMMED = 2
NORM_PARTS = 4
NHEAD = C // D
EPS = 1e-5
QK_COLS = CT * 2 * 2 * P
V_COLS = CT * C
P_COLS = CT * C
W3_COLS = CT * 3 * C


class Tally:

    def __init__(self):
        self.base, self.k = 0, 0

    def add(self, n=1):
        self.k += n
        return self.base + self.k

    def now(self):
        return self.base + self.k

    def slot(self):
        return (self.k - 1) % 2

    def enter(self, turn, per):
        self.start, self.per = self.base + self.k, per
        self.base, self.k = self.start + turn * per, 0

    def leave(self, turns):
        assert self.k == self.per
        self.base, self.k = self.start + turns * self.per, 0


def wait(eng, sem, value):
    if isinstance(value, int) and value <= 0:
        return
    eng.wait_ge(sem, value)


def wait_apart(eng, sem, value, passed):
    if isinstance(value, int) and value <= 0:
        return
    eng.wait_ge(sem, value)
    if not isinstance(value, int):
        eng.sem_inc(passed, 1)


DVE_COST = {"v": 7, "post": 6, "stats": 25, "gn": 6, "qk": 15, "max": 6}


def window_jobs(post=False, prep=False, nxt=True, gn=False):
    jobs = [[] for _ in range(STEPS)]
    if nxt:
        jobs[0] += [("v", 0), ("v", 1)]
    if gn:
        jobs[1].append(("stats",))
        jobs[3].append(("gn", 0))
        jobs[5].append(("gn", 1))
    if post:
        for n in range(4):
            jobs[6 + n // 2].append(("post", n // 2, n % 2))
    if prep:
        for n in range(4):
            jobs[9 + 2 * (n // 2) + n % 2].append(("qk", n // 2, n % 2))
    if nxt:
        tiles = [("max", h, t, half) for h in range(H) for t in range(MT) for half in range(2)]
        load = [sum(DVE_COST[j[0]] for j in step) + 9 * (s % MT in range(1, 1 + NORM_PARTS))
                for s, step in enumerate(jobs)]
        steps = range(2, STEPS - 1)
        room = min(r for r in range(200)
                   if sum(max(0, r - load[s]) // DVE_COST["max"] for s in steps) >= len(tiles))
        for s in steps:
            n = max(0, room - load[s]) // DVE_COST["max"]
            jobs[s] += tiles[:n]
            tiles = tiles[n:]
        assert not tiles
    return jobs


def program(nc, x, w_l0, w_o, concepts, concepts_t, gammas, conv_w, conv_wt, conv_b, lin1_t, lin2_t,
            qk_pack, v_pack, p_pack, w3_pack, b3_row, p3_pack, consts, out):
    f32, f32r = mybir.dt.float32, mybir.dt.float32r
    ALU, ACT, AX = mybir.AluOpType, mybir.ActivationFunctionType, mybir.AxisListType

    x_d = x.rearrange("b (t p) n -> b p t n", p=P)
    out_d = out.rearrange("b (t p) n -> b p t n", p=P)

    ctx = ExitStack()
    with ctx:
        def sb(name, shape, dt=f32):
            return ctx.enter_context(nc.sbuf_tensor(name, shape, dt))

        def sem(name):
            return ctx.enter_context(nc.semaphore(name))

        X = sb("X", [P, B, CT, N])
        QS = [sb(f"QS{i}", [3 * D + 2, H, N], f32r) for i in range(2)]
        KS = [sb(f"KS{i}", [3 * D + 2, H, N], f32r) for i in range(2)]
        HI = sb("HI", [P, 2, N], f32r)
        LO = sb("LO", [P, 2, N], f32r)
        VT = [sb(f"VT{i}", [P, MT, P]) for i in range(2)]
        PR = sb("PR", [P, 4, 2 * HALF])
        ACC = sb("ACC", [P, 2, 2 * HALF])
        OHU = [sb(f"OHU{i}", [P, 2, HALF]) for i in range(2)]
        OH = [[OHU[i][:, h, :] for h in range(2)] for i in range(2)]
        RC = sb("RC", [P, HALF])
        MX = sb("MX", [P, H, MT, 2])
        NM = sb("NM", [P, H, MT])
        NMH = sb("NMH", [P, H, MT], f32r)
        NML = sb("NML", [P, H, MT], f32r)
        ONES = sb("ONES", [P, P])
        XIN, XRES, XN = X[:, 0], X[:, 1], X[:, 2]
        WREG = X[:, 3].rearrange("p t n -> p (t n)")
        WREG2 = X[:, 4].rearrange("p t n -> p (t n)")
        WREG3 = X[:, 6].rearrange("p t n -> p (t n)")
        WQK_ALL = WREG[:, 0:QK_COLS + 8]
        WQK = WQK_ALL[:, 0:QK_COLS].rearrange("p (t u w c) -> p t u w c", t=CT, u=2, w=2)
        BQK = WQK_ALL[:, QK_COLS:QK_COLS + 4].rearrange("p (u w) -> p u w", u=2)
        GNS = WQK_ALL[:, QK_COLS + 4:QK_COLS + 6]
        GNB = WQK_ALL[:, QK_COLS + 6:QK_COLS + 8]
        WV_ALL = WREG[:, 1152:1152 + V_COLS + C]
        WV = WV_ALL[:, 0:V_COLS].rearrange("p (t c) -> p t c", t=CT)
        BV = WV_ALL[:, V_COLS:V_COLS + C]
        WP_ALL = WREG2[:, 0:P_COLS + CT]
        WP = WP_ALL[:, 0:P_COLS].rearrange("p (t c) -> p t c", t=CT)
        BP = WP_ALL[:, P_COLS:P_COLS + CT]
        P3_ALL = WREG2[:, 1024:1024 + P_COLS + 3 * CT]
        WP3 = P3_ALL[:, 0:P_COLS].rearrange("p (t c) -> p t c", t=CT)
        BP3 = P3_ALL[:, P_COLS:P_COLS + CT]
        GNS3 = P3_ALL[:, P_COLS + CT:P_COLS + 2 * CT]
        GNB3 = P3_ALL[:, P_COLS + 2 * CT:P_COLS + 3 * CT]
        W3_ALL = WREG3[:, 0:W3_COLS]
        W3 = W3_ALL.rearrange("p (t c) -> p t c", t=CT)
        B3 = X[0:1, 7].rearrange("p t n -> p (t n)")[:, 0:3 * C]
        PQ = X[:, 5].rearrange("p t n -> p (t n)")
        PV = [PR[:, 2 * n:2 * n + 2, :].rearrange("p a q -> p (a q)") for n in range(2)]
        QC = [HI[:, 0, C * n:C * n + C].bitcast(f32) for n in range(2)]
        VC = [HI[:, 1, C * n:C * n + C].bitcast(f32) for n in range(4)]
        S3 = [sb(f"S3{n}", [P, NHEAD, NHEAD]) for n in range(2)]
        M3 = sb("M3", [P, NHEAD])
        R3 = sb("R3", [P, 2, NHEAD])
        O3 = [LO[:, 1, C * n:C * n + C].bitcast(f32) for n in range(2)]
        OT = ACC[:, :, :]
        BN6 = sb("BN6", [P, CT, 2, 6])
        MV = sb("MV", [P, CT, 2])
        MG = sb("MG", [P, CT])
        DEV = sb("DEV", [P, CT])
        S2 = sb("S2", [P, CT])
        VE = sb("VE", [P, CT])
        RSTD = sb("RSTD", [P, CT])
        GA = sb("GA", [P, CT])
        GT = sb("GT", [P, CT])
        GB = sb("GB", [P, CT])
        MHALF = sb("MHALF", [P, CT])
        CST = sb("CST", [P, 3 * P + H])
        IDENT, GROUP, BLOCK, BMASK = (CST[:, 0:P], CST[:, P:2 * P], CST[:, 2 * P:3 * P], CST[:, 3 * P:3 * P + H])
        WL0 = sb("WL0", [P, CT, 3 * D])
        WO = sb("WO", [P, H, C])
        CON = sb("CON", [P, D])
        CONT = sb("CONT", [P, H, P])
        GAM = sb("GAM", [P, 3])
        CW = sb("CW", [P, C])
        CW3 = sb("CW3", [P, C])
        CWT = sb("CWT", [P, CT, D])
        CB = sb("CB", [P, 1])
        L1T = sb("L1T", [P, 4 * K])
        L2T = sb("L2T", [4 * K, D])
        ZB = sb("ZB", [P, P])
        RW = sb("RW", [P, 1])
        RWS = sb("RWS", [P, 1])
        ENC = RC[:, :]
        E = PR[:, 0:2, :].rearrange("p a (j q) -> p (a j) q", q=P)
        PT = PR[:, 2:4, :].rearrange("p a (j q) -> p (a j) q", q=HALF)
        CM4 = sb("CM4", [P, 4, H])
        CS = sb("CS", [P, 4 * H])
        CR = sb("CR", [P, 4 * H])
        LAT1 = HI[:, 0, :].bitcast(f32)
        LATC = HI[:, 1, :].bitcast(f32)
        LAT2 = LO[:, 0, :].bitcast(f32)
        OM = ACC[:, 0, :]
        SQ = ACC[:, 1, :]
        NRM = PR[:, 0, :]
        NRI = PR[:, 1, :]
        PRB = PR[:, 2, :]
        PSM = sb("PSM", [P, 2])
        POOLED = sb("POOLED", [P, 1])
        PM = sb("PM", [P, H])
        HID = sb("HID", [4 * K, H])
        ZE = sb("ZE", [P, 1])
        RG = sb("RG", [P, 1])

        ST = ctx.enter_context(nc.psum_tensor("ST", [P, 2, 2 * HALF], f32))
        RING = ctx.enter_context(nc.psum_tensor("RING", [P, 2, HALF], f32))
        AV = ctx.enter_context(nc.psum_tensor("AV", [P, HALF], f32))
        SUM = ctx.enter_context(nc.psum_tensor("SUM", [P, HALF], f32))

        x_in = [sem(f"x_in{b}") for b in range(2)]
        w_in = sem("w_in")
        zeroed = sem("zeroed")
        scaled = sem("scaled")
        ring_full = sem("ring_full")
        ring_free = sem("ring_free")
        dve_step = sem("dve_step")
        stage_ready = sem("stage_ready")
        stk = [sem(f"stk{h}") for h in range(H)]
        v_ready = sem("v_ready")
        negmax_ready = sem("negmax_ready")
        rows_in = sem("rows_in")
        st_full = sem("st_full")
        exp_done = sem("exp_done")
        pool_used = sem("pool_used")
        av_done = sem("av_done")
        half_done = sem("half_done")
        half_kept = sem("half_kept")
        norm_done = sem("norm_done")
        cs_ready = sem("cs_ready")
        act_done = sem("act_done")
        pe_ready = sem("pe_ready")
        x_final = sem("x_final")
        x_out = sem("x_out")
        xin_in = sem("xin_in")
        xres_in = sem("xres_in")
        wqk_in = sem("wqk_in")
        wv_in = sem("wv_in")
        wp_in = sem("wp_in")
        gn_ready = sem("gn_ready")
        var_ready = sem("var_ready")
        pool_gn = sem("pool_gn")
        xn_ready = sem("xn_ready")
        y_ready = sem("y_ready")
        passed = sem("passed")
        y_out = sem("y_out")

        w3_in = sem("w3_in")
        qkv3 = sem("qkv3")
        copied3 = sem("copied3")
        k_used3 = sem("k_used3")
        s_ready3 = sem("s_ready3")
        e_done3 = sem("e_done3")
        p_ready3 = sem("p_ready3")
        pv_done3 = sem("pv_done3")
        o_ready3 = sem("o_ready3")
        tr_done3 = sem("tr_done3")
        ot_done3 = sem("ot_done3")

        block = ctx.enter_context(nc.Block())

        def iteration(i, window, tallies, turns=None):
            u = 2 * i + 2
            last = isinstance(i, int) and i == B - 1
            first = isinstance(i, int) and i == 0
            window(u, 0, window_jobs(post=not first, prep=not last, gn=not last), i)
            window(u + 1, 1, window_jobs(prep=not last, nxt=not last), i)

        RING_PER = 2 + 4 + 2 + 4 + 64 + 2 + 4 + 64
        TURNS = B - 2

        def tile_slots(b, slot):
            for t in range(MT):
                slot(b, t)

        @block.sync
        def _(sp):
            def load(dst, src, s):
                sp.dma_start(dst, src).then_inc(s, 16)

            def stacks(u, par):
                wait_apart(sp, stage_ready, u + 1, passed)
                wait(sp, st_full, PAIRS * (u - 1))
                for h in range(H):
                    rows = slice(D * h, D * h + D)
                    for j, (q, k) in enumerate(((HI, HI), (LO, HI), (HI, LO))):
                        load(QS[par][D * j:D * j + D, h, :].bitcast(f32), q[rows, 0, :].bitcast(f32), stk[h])
                        load(KS[par][D * j:D * j + D, h, :].bitcast(f32), k[rows, 1, :].bitcast(f32), stk[h])

            def rows(u, par):
                for h in range(H):
                    wait(sp, negmax_ready, H * u + h + 1)
                    for r, src in ((3 * D, NMH), (3 * D + 1, NML)):
                        load(QS[par][r:r + 1, h, :].rearrange("o (p t) -> o p t", t=MT).bitcast(f32),
                             src[:, h, :].bitcast(f32), rows_in)

            load(CST[:, :], consts, w_in)
            load(WL0[:, :, :], w_l0.rearrange("(t p) o -> p t o", p=P), w_in)
            for b in range(H):
                load(X[:, b], x_d[b], x_in[0])
            load(GAM[:, :], gammas.broadcast_to([P, 3]), w_in)
            load(CON[:, :], concepts, w_in)
            sp.wait_ge(zeroed, 1)
            load(CWT[:, :, 0:K], conv_wt.rearrange("(t p) o -> p t o", p=P), w_in)
            load(L2T[:, 0:K], lin2_t, w_in)
            for j in range(H):
                load(WO[D * j:D * j + D, j, :], w_o, w_in)
                load(CONT[D * j:D * j + D, j, :], concepts_t, w_in)
                load(CW[D * j:D * j + K, :], conv_w, w_in)
                load(CB[D * j:D * j + K, :], conv_b, w_in)
                load(L1T[D * j:D * j + K, :], lin1_t, w_in)
            for b in range(H, B):
                load(X[:, b], x_d[b], x_in[1])
            stacks(0, 0)
            rows(0, 0)
            stacks(1, 1)
            rows(1, 1)
            for g in range(2):
                sp.wait_ge(x_final, g + 1)
                for b in range(H * g, H * g + H):
                    load(out_d[b], X[:, b], x_out)
            sp.wait_ge(x_out, 16 * B)
            load(XIN, out_d[0], xin_in)
            load(WQK_ALL, qk_pack, wqk_in)
            load(WV_ALL, v_pack, wv_in)
            stacks(2, 0)
            load(WP_ALL, p_pack, wp_in)
            load(P3_ALL, p3_pack, w3_in)
            load(W3_ALL, w3_pack, w3_in)
            load(B3, b3_row, w3_in)
            rows(2, 0)

            def sp_iteration(i):
                u = 2 * i + 2
                first, last = isinstance(i, int) and i == 0, isinstance(i, int) and i == B - 1
                if not last:
                    wait_apart(sp, xn_ready, CT * (i + 1), passed)
                    load(XIN, out_d[i + 1] if isinstance(i, int) else out_d[bass.ds(i + 1, 1)][0], xin_in)
                stacks(u + 1, 1)
                if not first:
                    wait_apart(sp, y_ready, i, passed)
                    load(out_d[i - 1] if isinstance(i, int) else out_d[bass.ds(i - 1, 1)][0], XRES, y_out)
                rows(u + 1, 1)
                if not last:
                    stacks(u + 2, 0)
                wait_apart(sp, y_out, 16 * i, passed)
                load(XRES, out_d[i] if isinstance(i, int) else out_d[bass.ds(i, 1)][0], xres_in)
                if not last:
                    rows(u + 2, 0)

            sp_iteration(0)
            with sp.Fori(1, B - 1) as i:
                sp_iteration(i)
            sp_iteration(B - 1)
            sp.wait_ge(xn_ready, CT * B)
            load(XIN, out_d[0], xin_in)
            sp.wait_ge(y_ready, B)
            load(out_d[B - 1], XRES, y_out)
            sp.wait_ge(y_out, 16 * B)
            load(XRES, out_d[0], xres_in)

            def sp_batch(b):
                wait_apart(sp, xn_ready, CT * (B + b + 1), passed)
                load(XIN, out_d[b + 1] if isinstance(b, int) else out_d[bass.ds(b + 1, 1)][0], xin_in)

            def sp_store(b):
                wait_apart(sp, y_ready, B + b + 1, passed)
                load(out_d[b] if isinstance(b, int) else out_d[bass.ds(b, 1)][0], XRES, y_out)
                wait_apart(sp, y_out, 16 * (B + b + 1), passed)
                load(XRES, out_d[b + 1] if isinstance(b, int) else out_d[bass.ds(b + 1, 1)][0], xres_in)

            sp_batch(0)
            with sp.Fori(1, B - 1) as b:
                sp_store(b - 1)
                sp_batch(b)
            sp_store(B - 2)
            sp.wait_ge(y_ready, 2 * B)
            load(out_d[B - 1], XRES, y_out)
            sp.wait_ge(y_out, 16 * 2 * B)

        @block.tensor
        def _(pe):
            ring = Tally()
            pe_need = Tally()
            mm = nc.tensor.matmul

            def bank():
                wait(pe, ring_free, ring.add() - 2)
                return RING[:, ring.slot(), :]

            def all_read():
                wait(pe, ring_free, ring.now())

            def qk_l0(g, which, half):
                dst = bank()
                for t in range(CT):
                    for j in range(H):
                        last = mm(dst[D * j:D * j + D, :], WL0[:, t, D * which:D * which + D],
                                  X[:, H * g + j, t, HALF * half:HALF * half + HALF],
                                  start=(t == 0), stop=(t == CT - 1))
                last.then_inc(ring_full, 1)

            def v_l0(g, part):
                dst = bank()
                for m in range(4):
                    mt = 4 * part + m
                    for j in range(H):
                        for t in range(CT):
                            last = mm(dst[:, P * m + D * j:P * m + D * j + D],
                                      X[:, H * g + j, t, P * mt:P * mt + P], WL0[:, t, 2 * D:3 * D],
                                      start=(t == 0), stop=(t == CT - 1))
                last.then_inc(ring_full, 1)

            def max_scores(u, par, h, t, half):
                if t == 0 and half == 0:
                    wait(pe, stk[h], 96 * (u + 1))
                mm(bank(), QS[par][0:3 * D, h, t:N:MT], KS[par][0:3 * D, h, HALF * half:HALF * half + HALF],
                   start=True, stop=True).then_inc(ring_full, 1)

            def scores(u, par, s, pair):
                half, mt = s // MT, s % MT
                if s == 0 and pair == 0:
                    wait(pe, rows_in, 2 * H * 16 * (u + 1))
                wait(pe, exp_done, PAIRS * u + 2 * s + pair - 1)
                for h in range(2):
                    head = 2 * pair + h
                    last = mm(ST[:, pair, HALF * h:HALF * h + HALF],
                              KS[par][:, head, P * mt:P * mt + P],
                              QS[par][:, head, HALF * half:HALF * half + HALF], start=True, stop=True)
                last.then_inc(st_full, 1)

            def values(u, par, s):
                half, mt = s // MT, s % MT
                if mt == 0:
                    wait(pe, half_kept, 2 * (2 * u + half))
                    wait(pe, v_ready, 2 * (u + 1))
                wait(pe, exp_done, PAIRS * u + 2 * s + 2)
                for h in range(H):
                    last = mm(AV[D * h:D * h + D, :], VT[par][:, mt, D * h:D * h + D],
                              PR[:, (2 * s + h // 2) % 4, HALF * (h % 2):HALF * (h % 2) + HALF],
                              start=(mt == 0), stop=(mt == MT - 1))
                if mt in POOL_TILES:
                    last.then_inc(av_done, 1)

            def sums(u, s):
                half, mt = s // MT, s % MT
                if mt not in POOL_TILES:
                    for h in range(H):
                        last = mm(SUM[D * h:D * h + D, :], ONES[:, 0:D],
                                  PR[:, (2 * s + h // 2) % 4, HALF * (h % 2):HALF * (h % 2) + HALF],
                                  start=(mt == FIRST_SUMMED), stop=False)
                    last.then_inc(av_done, 1)
                if mt == MT - 1:
                    wait(pe, pool_used, 2 * POOL_SUMS * (2 * u + half + 1))
                    for h in range(H):
                        last = mm(SUM[D * h:D * h + D, :], ONES[:, 0:D],
                                  ACC[:, h // 2, HALF * (h % 2):HALF * (h % 2) + HALF], start=False, stop=True)
                    last.then_inc(half_done, 1)

            def v_product(u, part, batch, unit):
                dst = bank()
                if part == 0:
                    pe.wait_ge(wv_in, 16)
                for m in range(4):
                    mt = 4 * part + m
                    for t in range(CT):
                        last = mm(dst[:, P * m:P * m + P], XN[:, t, P * mt:P * mt + P],
                                  WV[:, t, P * unit:P * unit + P], start=(t == 0), stop=(t == CT - 1))
                last.then_inc(ring_full, 1)

            def qk_product(which, half, batch, unit):
                dst = bank()
                if which == 0 and half == 0:
                    pe.wait_ge(wqk_in, 16)
                    wait(pe, xn_ready, CT * (batch + 1))
                for t in range(CT):
                    last = mm(dst, WQK[:, t, unit, which, :], XN[:, t, HALF * half:HALF * half + HALF],
                              start=(t == 0), stop=(t == CT - 1))
                last.then_inc(ring_full, 1)

            def group_sums(k, batch):
                dst = bank()
                wait(pe, gn_ready, 2 * batch + k + 1)
                mm(dst[:, 0:CT], GROUP, MV[:, :, 0] if k == 0 else S2[:, :],
                   start=True, stop=True).then_inc(ring_full, 1)

            def output_product(o, half, batch):
                dst = bank()
                if o == 0 and half == 0:
                    pe.wait_ge(wp_in, 16)
                    wait(pe, norm_done, 2 * NORM_PARTS * (2 * batch + 4))
                for t in range(CT):
                    last = mm(dst, WP[:, t, P * o:P * o + P], OH[t][half],
                              start=(t == 0), stop=(t == CT - 1))
                last.then_inc(ring_full, 1)

            def window(u, par, jobs, i, trail=True):
                def run(todo):
                    for job in todo:
                        if job[0] == "max":
                            max_scores(u + 1, 1 - par, *job[1:])
                        elif job[0] == "v" and i is None:
                            v_l0(1, job[1])
                        elif job[0] == "v":
                            v_product(u + 1, job[1], i + par, 1 - par)
                        elif job[0] == "qk":
                            qk_product(*job[1:], i + 1, par)
                        elif job[0] == "gn":
                            group_sums(job[1], i + 1)
                        elif job[0] == "post":
                            output_product(*job[1:], i - 1)

                for s in range(STEPS):
                    scores(u, par, s, 0)
                    run(jobs[s][0:1])
                    scores(u, par, s, 1)
                    run(jobs[s][1:2])
                    if s:
                        values(u, par, s - 1)
                    elif trail:
                        values(u - 1, 1 - par, STEPS - 1)
                    run(jobs[s][2:3])
                    if s:
                        sums(u, s - 1)
                    elif trail:
                        sums(u - 1, STEPS - 1)
                    run(jobs[s][3:])

            pe.wait_ge(scaled, 1)
            pe.wait_ge(x_in[0], 16 * H)
            for which in range(2):
                for half in range(2):
                    qk_l0(0, which, half)
            for part in range(2):
                v_l0(0, part)
            for h in range(H):
                for t in range(MT):
                    for half in range(2):
                        max_scores(0, 0, h, t, half)
            pe.wait_ge(x_in[1], 16 * H)
            for which in range(2):
                for half in range(2):
                    qk_l0(1, which, half)
            window(0, 0, window_jobs(), None, trail=False)
            window(1, 1, window_jobs(nxt=False), None)
            values(1, 1, STEPS - 1)
            sums(1, STEPS - 1)
            pe.wait_ge(norm_done, 4 * NORM_PARTS)
            for g in range(2):
                pe.wait_ge(pe_ready, pe_need.add())
                for half in range(2):
                    cols = slice(HALF * half, HALF * half + HALF)
                    for j in range(H):
                        for t in range(CT):
                            mm(bank(), WO[:, j, P * t:P * t + P], LAT1[:, cols],
                               start=True, stop=True).then_inc(ring_full, 1)
                    all_read()
                    qk_l0(g, 0, half)
                    all_read()
                    for n in range(4):
                        mm(bank(), ENC[:, P * n:P * n + P], CONT[:, :, :].rearrange("p j q -> p (j q)"),
                           start=True, stop=True).then_inc(ring_full, 1)
                    pe.wait_ge(pe_ready, pe_need.add())
                    for n in range(4):
                        dst = bank()
                        for j in range(H):
                            last = nc.tensor.transpose(dst[:, P * j:P * j + P], E[:, H * n + j, :], IDENT)
                        last.then_inc(ring_full, 1)
                    all_read()
                    dst = bank()
                    for j in range(H):
                        last = mm(dst[D * j:D * j + D, :], CON[:, :], PT[:, j, :], start=True, stop=True)
                    last.then_inc(ring_full, 1)
                pe.wait_ge(pe_ready, pe_need.add())
                for half in range(2):
                    for j in range(H):
                        for t in range(CT):
                            mm(bank(), WO[:, j, P * t:P * t + P], LAT2[:, HALF * half:HALF * half + HALF],
                               start=True, stop=True).then_inc(ring_full, 1)
                all_read()
                for half in range(2):
                    cols = slice(HALF * half, HALF * half + HALF)
                    dst = bank()
                    for t in range(CT):
                        for j in range(H):
                            last = mm(dst[D * j:D * j + D, :], CWT[:, t, :], X[:, H * g + j, t, cols],
                                      start=(t == 0), stop=(t == CT - 1))
                    last.then_inc(ring_full, 1)
                pe.wait_ge(pe_ready, pe_need.add())
                for half in range(2):
                    mm(bank(), BLOCK, SQ[:, HALF * half:HALF * half + HALF],
                       start=True, stop=True).then_inc(ring_full, 1)
                pe.wait_ge(pe_ready, pe_need.add())
                mm(bank()[0:4 * K, 0:H], L1T[:, :], PM[:, :], start=True, stop=True).then_inc(ring_full, 1)
                all_read()
                dst = bank()
                for j in range(H):
                    last = mm(dst[D * j:D * j + D, 0:1], L2T[:, :], HID[:, j:j + 1], start=True, stop=True)
                last.then_inc(ring_full, 1)
                pe.wait_ge(pe_ready, pe_need.add())
                for j in range(H):
                    for t in range(CT):
                        for half in range(2):
                            mm(bank(), CW3[D * j:D * j + D, P * t:P * t + P],
                               PRB[D * j:D * j + D, HALF * half:HALF * half + HALF],
                               start=True, stop=True).then_inc(ring_full, 1)
            for k in range(2):
                group_sums(k, 0)
            for which in range(2):
                for half in range(2):
                    qk_product(which, half, 0, 0)
            for part in range(2):
                v_product(2, part, 0, 0)
            for h in range(H):
                for t in range(MT):
                    for half in range(2):
                        max_scores(2, 0, h, t, half)
            for which in range(2):
                for half in range(2):
                    qk_product(which, half, 0, 1)
            window(2, 0, window_jobs(prep=True, gn=True), 0, trail=False)
            window(3, 1, window_jobs(prep=True), 0)
            with pe.Fori(1, B - 1) as i:
                assert ring.now() % 2 == 0
                ring.enter(i - 1, RING_PER)
                iteration(i, window, None)
                ring.leave(TURNS)
            iteration(B - 1, window, None)
            values(2 * B + 1, 1, STEPS - 1)
            sums(2 * B + 1, STEPS - 1)
            for o in range(CT):
                for half in range(2):
                    output_product(o, half, B - 1)

            def project3(half):
                for o in range(CT):
                    dst = bank()
                    for t in range(CT):
                        last = mm(dst, WP3[:, t, P * o:P * o + P], OT[:, t, HALF * half:HALF * half + HALF],
                                  start=(t == 0), stop=(t == CT - 1))
                    last.then_inc(ring_full, 1)

            def transpose3(n):
                wait(pe, o_ready3, n + 1)
                wait(pe, ot_done3, n - 1)
                at = n if isinstance(n, int) else tile_at[0]
                dst, src = (AV, SUM)[at % 2], O3[at % 2]
                for t in range(CT):
                    last = nc.tensor.transpose(dst[:, P * t:P * t + P], src[:, P * t:P * t + P], IDENT)
                last.then_inc(tr_done3, 1)

            tile_at = [0]

            def slot(b, t):
                n = MT * b + t
                first = isinstance(b, int) and b == 0
                if t == 0:
                    wait(pe, xn_ready, CT * (B + b + 1))
                wait(pe, copied3, 2 * (n - 1))
                wait(pe, k_used3, n - 1)
                for c0, c1, dst in ((0, 2 * C, ST[:, t % 2, 0:HALF]), (2 * C, 3 * C, ST[:, t % 2, HALF:HALF + C])):
                    for ct in range(CT):
                        mm(dst, XN[:, ct, P * t:P * t + P], W3[:, ct, c0:c1], start=(ct == 0), stop=False)
                    last = mm(dst, ONES[0:1, :], B3[:, c0:c1], start=False, stop=True)
                last.then_inc(qkv3, 1)
                if not (first and t < 4) and t % 4 == 3:
                    wait(pe, ot_done3, n - 3)
                    project3((t // 4 + 1) % 2)
                if not (first and t < 3):
                    tile_at[0] = (t - 3) % MT
                    transpose3(n - 3)
                if t in (5, 6) and not (isinstance(b, int) and b == B - 1):
                    group_sums(t - 5, B + b + 1)

            pe.wait_ge(w3_in, 16 * 3)
            for k in range(2):
                group_sums(k, B)
            tile_slots(0, slot)
            with pe.Fori(1, B - 1) as b:
                assert ring.now() % 2 == 0
                ring.enter(b - 1, 6)
                tile_slots(b, slot)
                ring.leave(TURNS)
            tile_slots(B - 1, slot)
            for n in range(MT * B - 3, MT * B):
                transpose3(n)
            pe.wait_ge(ot_done3, MT * B)
            project3(1)

        @block.scalar
        def _(act):
            cs = Tally()

            def keep_half(u, par, half):
                wait(act, half_done, 2 * u + half + 1)
                wait(act, norm_done, NORM_PARTS * (2 * u + half))
                nc.scalar.activation(RC[:, :], SUM[:, :], ACT.Copy).then_inc(half_kept, 1)
                nc.scalar.activation(OH[par][half], AV[:, :], ACT.Copy).then_inc(half_kept, 1)

            def window(u, par, jobs, i, trail=True):
                for s in range(STEPS):
                    for pair in range(2):
                        wait(act, st_full, PAIRS * u + 2 * s + pair + 1)
                        wait(act, av_done, STEPS * u + s - 1)
                        if (s - 2) % MT in POOL_TILES:
                            wait(act, pool_used, 2 * POOL_SUMS * (2 * u + (s - 2) // MT)
                                 + 2 * max(POOL_TILES.index((s - 2) % MT) - 1, 0) + pair + 1)
                        nc.scalar.activation(PR[:, (2 * s + pair) % 4, :], ST[:, pair, :], ACT.Exp,
                                             scale=1.0 if i is None else float(D) ** -0.5
                                             ).then_inc(exp_done, 1)
                    if s == 0 and trail:
                        keep_half(u - 1, 1 - par, 1)
                    if s == MT:
                        keep_half(u, par, 0)

            act.wait_ge(cs_ready, cs.add())
            nc.scalar.activation(RWS[:, :], RW[:, :], ACT.Sqrt).then_inc(act_done, 1)
            window(0, 0, None, None, trail=False)
            window(1, 1, None, None)
            keep_half(1, 1, 1)
            for g in range(2):
                for half in range(2):
                    act.wait_ge(cs_ready, cs.add())
                    nc.scalar.activation(E, E, ACT.Exp).then_inc(act_done, 1)
                act.wait_ge(cs_ready, cs.add())
                nc.scalar.activation(NRM, NRM, ACT.Sqrt).then_inc(act_done, 1)
                act.wait_ge(cs_ready, cs.add())
                nc.scalar.activation(ZE[:, :], ZE[:, :], ACT.Sigmoid).then_inc(act_done, 1)
            window(2, 0, None, 0, trail=False)
            window(3, 1, None, 0)
            with act.Fori(1, B - 1) as i:
                iteration(i, window, None)
            iteration(B - 1, window, None)
            keep_half(2 * B + 1, 1, 1)

            def apply3(batch):
                wait(act, pool_gn, 4 * (batch + 1))
                for t in range(CT):
                    nc.scalar.activation(XN[:, t], XIN[:, t], ACT.Identity, bias=GB[:, t:t + 1],
                                         scale=GA[:, t:t + 1]).then_inc(xn_ready, 1)

            def exp3(n, at):
                wait(act, s_ready3, n + 1)
                nc.scalar.activation(S3[at % 2][:, :, :], S3[at % 2][:, :, :], ACT.Exp,
                                     scale=float(D) ** -0.5).then_inc(e_done3, 1)

            def keep3(n, at):
                wait(act, tr_done3, n + 1)
                nc.scalar.activation(OT[:, :, P * at:P * at + P],
                                     (AV, SUM)[at % 2][:, 0:C].rearrange("p (t q) -> p t q", t=CT),
                                     ACT.Copy).then_inc(ot_done3, 1)

            def slot(b, t):
                n = MT * b + t
                first = isinstance(b, int) and b == 0
                wait(act, qkv3, n + 1)
                wait(act, k_used3, n - 1)
                nc.scalar.activation(QC[t % 2], ST[:, t % 2, 0:C], ACT.Copy).then_inc(copied3, 1)
                wait(act, pv_done3, n - 3)
                nc.scalar.activation(VC[t % 4], ST[:, t % 2, HALF:HALF + C], ACT.Copy).then_inc(copied3, 1)
                if not (first and t < 1):
                    exp3(n - 1, (t - 1) % MT)
                if not (first and t < 3):
                    keep3(n - 3, (t - 3) % MT)
                if t == MT - 1 and not (isinstance(b, int) and b == B - 1):
                    apply3(B + b + 1)

            apply3(B)
            tile_slots(0, slot)
            with act.Fori(1, B - 1) as b:
                tile_slots(b, slot)
            tile_slots(B - 1, slot)
            exp3(MT * B - 1, MT - 1)
            for n in range(MT * B - 3, MT * B):
                keep3(n, n % MT)

        @block.gpsimd
        def _(pool):
            gn = Tally()

            def norm_factors(batch, scale, bias):
                wait(pool, var_ready, batch + 1)

                def link(ins):
                    ins.then_inc(pool_gn, 1)
                    wait_apart(pool, pool_gn, gn.add(), passed)

                link(nc.gpsimd.tensor_tensor(RSTD[:, :], VE[:, :], MHALF[:, :], ALU.pow))
                link(nc.gpsimd.tensor_tensor(GA[:, :], RSTD[:, :], scale, ALU.mult))
                link(nc.gpsimd.tensor_tensor(GT[:, :], MG[:, :], GA[:, :], ALU.mult))
                link(nc.gpsimd.tensor_tensor(GB[:, :], bias, GT[:, :], ALU.subtract))

            def norm_apply(batch):
                pool.wait_ge(wqk_in, 16)
                norm_factors(batch, GNS, GNB)
                for t in range(CT):
                    nc.gpsimd.tensor_scalar(XN[:, t], XIN[:, t], GA[:, t:t + 1], GB[:, t:t + 1],
                                            ALU.mult, ALU.add).then_inc(xn_ready, 1)

            def window(u, par, jobs, i):
                for s in range(STEPS):
                    half, mt = s // MT, s % MT
                    if mt in POOL_TILES[1:]:
                        rank = POOL_TILES.index(mt)
                        for pair in range(2):
                            wait_apart(pool, exp_done, PAIRS * u + 2 * s + pair + 1, passed)
                            if rank == 1:
                                wait_apart(pool, half_done, 2 * u + half, passed)
                                so_far = PR[:, (2 * (s - 1) + pair) % 4, :]
                            else:
                                wait_apart(pool, pool_used, 2 * POOL_SUMS * (2 * u + half) + 2 * (rank - 2)
                                           + pair + 1, passed)
                                so_far = ACC[:, pair, :]
                            nc.gpsimd.tensor_tensor(ACC[:, pair, :], so_far, PR[:, (2 * s + pair) % 4, :],
                                                    ALU.add).then_inc(pool_used, 1)
                    if jobs and ("gn", 1) in jobs[s]:
                        norm_apply(i + 1)

            nc.gpsimd.memset(MHALF[:, :], -0.5)
            window(0, 0, None, None)
            window(1, 1, None, None)
            norm_apply(0)
            window(2, 0, window_jobs(prep=True, gn=True), 0)
            window(3, 1, None, 0)
            with pool.Fori(1, B - 1) as i:
                gn.enter(i - 1, 4)
                iteration(i, window, None)
                gn.leave(TURNS)
            iteration(B - 1, window, None)

            def products(n, at):
                wait(pool, p_ready3, n + 1)
                wait(pool, copied3, 2 * n + 2)
                wait(pool, o_ready3, n - 1)
                nc.gpsimd.tensor_tensor(
                    PV[at % 2].rearrange("p (h d g) -> p h d g", h=NHEAD, d=D),
                    S3[at % 2][:, :, :].unsqueeze(2).broadcast_to([P, NHEAD, D, NHEAD]),
                    VC[at % 4].rearrange("p (g d) -> p d g", d=D).unsqueeze(1).broadcast_to(
                        [P, NHEAD, D, NHEAD]), ALU.mult).then_inc(pv_done3, 1)

            def slot(b, t):
                n = MT * b + t
                if not (isinstance(b, int) and b == 0 and t < 1):
                    products(n - 1, (t - 1) % MT)
                if t == 6 and not (isinstance(b, int) and b == B - 1):
                    norm_factors(B + b + 1, GNS3, GNB3)

            pool.wait_ge(w3_in, 16 * 3)
            norm_factors(B, GNS3, GNB3)
            tile_slots(0, slot)
            with pool.Fori(1, B - 1) as b:
                gn.enter(b - 1, 4)
                tile_slots(b, slot)
                gn.leave(TURNS)
            tile_slots(B - 1, slot)
            products(MT * B - 1, MT - 1)

        @block.vector
        def _(dve):
            ring = Tally()
            steps = Tally()
            acts = Tally()

            def link(ins, alone=False):
                ins.then_inc(dve_step, 1)
                if alone:
                    wait_apart(dve, dve_step, steps.add(), passed)
                else:
                    dve.wait_ge(dve_step, steps.add())

            def bank():
                wait(dve, ring_full, ring.add())
                return RING[:, ring.slot(), :]

            def own():
                dve.wait_ge(ring_free, ring.now())

            def split_qk(bias, which, half, u, done):
                src = bank()
                cols = slice(HALF * half, HALF * half + HALF)
                if which == 0 and half == 0:
                    for h in range(H):
                        wait(dve, stk[h], 96 * u)
                link(nc.vector.tensor_scalar(HI[:, which, cols], src, bias, None, ALU.add))
                nc.vector.scalar_tensor_tensor(out=LO[:, which, cols], in0=src, scalar=bias,
                                               in1=HI[:, which, cols].bitcast(f32), op0=ALU.add,
                                               op1=ALU.subtract).then_inc(ring_free, 1)
                if done:
                    own()
                    dve.sem_inc(stage_ready, 1)

            def keep_v(u, par, part, bias):
                src = bank()
                wait(dve, half_done, 2 * (u - 1))
                nc.vector.tensor_tensor(VT[par][:, 4 * part:4 * part + 4, :],
                                        src.rearrange("p (m c) -> p m c", c=P),
                                        bias.unsqueeze(1).broadcast_to([P, 4, P]),
                                        ALU.add).then_inc(ring_free, 1)
                own()
                dve.sem_inc(v_ready, 1)

            def row_max(u, par, h, t, half):
                nc.vector.tensor_reduce(out=MX[:, h, t, half:half + 1], in_=bank(), op=ALU.max,
                                        axis=AX.X).then_inc(ring_free, 1)
                if t == MT - 1 and half == 1:
                    own()
                    if h == 0:
                        wait(dve, rows_in, 2 * H * 16 * u)
                    link(nc.vector.tensor_reduce(out=NM[:, h, :], in_=MX[:, h], op=ALU.max, axis=AX.X,
                                                 negate=True))
                    link(nc.vector.tensor_copy(NMH[:, h, :], NM[:, h, :]))
                    nc.vector.tensor_tensor(NML[:, h, :], NM[:, h, :], NMH[:, h, :].bitcast(f32),
                                            ALU.subtract).then_inc(negmax_ready, 1)

            def normalise(u, par, half, part):
                if part == 0:
                    wait(dve, half_kept, 2 * (2 * u + half + 1))
                w = HALF // NORM_PARTS
                cols = slice(w * part, w * part + w)
                link(nc.vector.reciprocal(RC[:, cols], RC[:, cols]))
                nc.vector.tensor_tensor(OH[par][half][:, cols], OH[par][half][:, cols], RC[:, cols],
                                        ALU.mult).then_inc(norm_done, 1)

            def statistics(batch):
                wait(dve, xin_in, 16 * (batch + 1))
                for t in range(CT):
                    for half in range(2):
                        last = nc.vector.bn_stats(BN6[:, t, half, :], XIN[:, t, HALF * half:HALF * half + HALF])
                link(last, alone=True)
                link(nc.vector.bn_aggr(MV[:, 0, :], BN6[:, 0]), alone=True)
                link(nc.vector.bn_aggr(MV[:, 1, :], BN6[:, 1]))
                dve.sem_inc(gn_ready, 1)

            def group_stats(k, batch):
                src = bank()
                if k == 0:
                    nc.vector.tensor_copy(MG[:, :], src[:, 0:CT]).then_inc(ring_free, 1)
                    own()
                    link(nc.vector.tensor_tensor(DEV[:, :], MV[:, :, 0], MG[:, :], ALU.subtract))
                    link(nc.vector.tensor_tensor(S2[:, :], DEV[:, :], DEV[:, :], ALU.mult))
                    link(nc.vector.tensor_tensor(S2[:, :], S2[:, :], MV[:, :, 1], ALU.add))
                    dve.sem_inc(gn_ready, 1)
                else:
                    nc.vector.tensor_scalar(VE[:, :], src[:, 0:CT], EPS, None, ALU.add).then_inc(ring_free, 1)
                    own()
                    dve.sem_inc(var_ready, 1)

            def residual(o, half, batch, bias):
                src = bank()
                cols = slice(HALF * half, HALF * half + HALF)
                if o == 0 and half == 0:
                    wait(dve, xres_in, 16 * (batch + 1))
                nc.vector.scalar_tensor_tensor(out=XRES[:, o, cols], in0=src, scalar=bias[:, o:o + 1],
                                               in1=XRES[:, o, cols], op0=ALU.add,
                                               op1=ALU.add).then_inc(ring_free, 1)
                if o == CT - 1 and half == 1:
                    own()
                    dve.sem_inc(y_ready, 1)

            def window(u, par, jobs, i, trail=True):
                def run(todo):
                    for job in todo:
                        if job[0] == "max":
                            row_max(u + 1, 1 - par, *job[1:])
                        elif job[0] == "v" and i is None:
                            keep_v(1, 1, job[1], ZB[:, :])
                        elif job[0] == "v":
                            keep_v(u + 1, 1 - par, job[1], BV[:, P * (1 - par):P * (1 - par) + P])
                        elif job[0] == "qk":
                            split_qk(BQK[:, par, job[1]:job[1] + 1], *job[1:], u + 2, job[1:] == (1, 1))
                        elif job[0] == "stats":
                            statistics(i + 1)
                        elif job[0] == "gn":
                            group_stats(job[1], i + 1)
                        elif job[0] == "post":
                            residual(*job[1:], i - 1, BP)

                for s in range(STEPS):
                    run(jobs[s][0:3])
                    if 1 <= s <= NORM_PARTS and trail:
                        normalise(u - 1, 1 - par, 1, s - 1)
                    if MT + 1 <= s <= MT + NORM_PARTS:
                        normalise(u, par, 0, s - MT - 1)
                    run(jobs[s][3:])

            nc.vector.memset(WO[:, :, :], 0.0)
            nc.vector.memset(CONT[:, :, :], 0.0)
            nc.vector.memset(CWT[:, :, :], 0.0)
            nc.vector.memset(L1T[:, :], 0.0)
            nc.vector.memset(L2T[:, :], 0.0)
            nc.vector.memset(CB[:, :], 0.0)
            nc.vector.memset(ZB[:, :], 0.0)
            nc.vector.memset(CW[:, :], 1.0)
            nc.vector.memset(ONES[:, :], 1.0)
            for par in range(2):
                link(nc.vector.memset(KS[par][3 * D:3 * D + 2, :, :].bitcast(f32), 1.0))
            dve.sem_inc(zeroed, 1)
            dve.wait_ge(w_in, 16 * (6 + 5 * H))
            nc.vector.tensor_scalar(WL0[:, :, :], WL0[:, :, :], float(C) ** -0.5, None, ALU.mult)
            nc.vector.tensor_scalar(WO[:, :, :], WO[:, :, :], float(D) ** -0.5, None, ALU.mult)
            link(nc.vector.tensor_tensor(CW3[:, :], CW[:, :], CW[:, :], ALU.mult))
            dve.sem_inc(scaled, 1)
            link(nc.vector.tensor_reduce(out=RW[:, :], in_=CW3[:, :], op=ALU.add, axis=AX.X))
            dve.sem_inc(cs_ready, 1)
            dve.wait_ge(act_done, acts.add())
            link(nc.vector.reciprocal(RW[:, :], RWS[:, :]))
            for which in range(2):
                for half in range(2):
                    split_qk(ZB[:, 0:1], which, half, 0, (which, half) == (1, 1))
            for part in range(2):
                keep_v(0, 0, part, ZB[:, :])
            for h in range(H):
                for t in range(MT):
                    for half in range(2):
                        row_max(0, 0, h, t, half)
            for which in range(2):
                for half in range(2):
                    split_qk(ZB[:, 0:1], which, half, 1, (which, half) == (1, 1))
            window(0, 0, window_jobs(), None, trail=False)
            window(1, 1, window_jobs(nxt=False), None)
            for part in range(NORM_PARTS):
                normalise(1, 1, 1, part)
            def reread(dst, src):
                link(nc.vector.transpose(dst.rearrange("p (a c) -> p a c", c=D),
                                         src.rearrange("p (l a) -> p a l", a=D)))
                dve.sem_inc(pe_ready, 1)

            def add_to_x(g, half, gamma):
                for j in range(H):
                    for t in range(CT):
                        xs = X[:, H * g + j, t, HALF * half:HALF * half + HALF]
                        nc.vector.scalar_tensor_tensor(out=xs, in0=bank(), scalar=gamma, in1=xs,
                                                       op0=ALU.mult, op1=ALU.add).then_inc(ring_free, 1)

            for g in range(2):
                reread(LAT1, OHU[g][:, :, :].rearrange("p h q -> p (h q)"))
                for half in range(2):
                    cols = slice(HALF * half, HALF * half + HALF)
                    add_to_x(g, half, GAM[:, 0:1])
                    nc.vector.tensor_copy(ENC, bank()).then_inc(ring_free, 1)
                    for n in range(4):
                        src = bank().rearrange("p (j q) -> p j q", q=P)
                        link(nc.vector.tensor_reduce(out=CM4[:, n, :], in_=src, op=ALU.max, axis=AX.X))
                        nc.vector.tensor_tensor(E[:, H * n:H * n + H, :], src,
                                                CM4[:, n, :].unsqueeze(2).broadcast_to([P, H, P]),
                                                ALU.subtract).then_inc(ring_free, 1)
                    own()
                    dve.sem_inc(cs_ready, 1)
                    dve.wait_ge(act_done, acts.add())
                    link(nc.vector.tensor_reduce(out=CS[:, :], in_=E, op=ALU.add, axis=AX.X))
                    link(nc.vector.reciprocal(CR[:, :], CS[:, :]))
                    link(nc.vector.tensor_tensor(E, E, CR[:, :].unsqueeze(2).broadcast_to([P, 4 * H, P]),
                                                 ALU.mult))
                    dve.sem_inc(pe_ready, 1)
                    for n in range(4):
                        nc.vector.tensor_copy(PT[:, :, P * n:P * n + P],
                                              bank().rearrange("p (j q) -> p j q", q=P)).then_inc(ring_free, 1)
                    nc.vector.tensor_copy(LATC[:, cols], bank()).then_inc(ring_free, 1)
                own()
                reread(LAT2, LATC)
                for half in range(2):
                    add_to_x(g, half, GAM[:, 1:2])
                for half in range(2):
                    cols = slice(HALF * half, HALF * half + HALF)
                    nc.vector.tensor_scalar(OM[:, cols], bank(), CB[:, :], None, ALU.add).then_inc(ring_free, 1)
                    own()
                    link(nc.vector.tensor_tensor(SQ[:, cols], OM[:, cols], OM[:, cols], ALU.mult))
                dve.sem_inc(pe_ready, 1)
                for half in range(2):
                    nc.vector.tensor_copy(NRM[:, HALF * half:HALF * half + HALF], bank()).then_inc(ring_free, 1)
                own()
                dve.sem_inc(cs_ready, 1)
                dve.wait_ge(act_done, acts.add())
                link(nc.vector.reciprocal(NRI, NRM))
                link(nc.vector.scalar_tensor_tensor(out=PRB, in0=OM, scalar=RW[:, :], in1=NRI,
                                                    op0=ALU.mult, op1=ALU.mult))
                link(nc.vector.tensor_reduce(out=POOLED[:, :], in_=PRB, op=ALU.add, axis=AX.X))
                link(nc.vector.tensor_scalar(PM[:, :], BMASK, POOLED[:, :], 1.0 / N, ALU.mult, ALU.mult))
                dve.sem_inc(pe_ready, 1)
                nc.vector.tensor_scalar(HID[:, :], bank()[0:4 * K, 0:H], 0.0, None,
                                        ALU.max).then_inc(ring_free, 1)
                nc.vector.tensor_copy(ZE[:, :], bank()[:, 0:1]).then_inc(ring_free, 1)
                own()
                dve.sem_inc(cs_ready, 1)
                dve.wait_ge(act_done, acts.add())
                link(nc.vector.tensor_tensor(RG[:, :], ZE[:, :], GAM[:, 2:3], ALU.mult))
                link(nc.vector.tensor_scalar(CW3[:, :], CW[:, :], RG[:, :], None, ALU.mult))
                dve.sem_inc(pe_ready, 1)
                for j in range(H):
                    for t in range(CT):
                        for half in range(2):
                            xs = X[:, H * g + j, t, HALF * half:HALF * half + HALF]
                            nc.vector.tensor_tensor(xs, bank(), xs, ALU.add).then_inc(ring_free, 1)
                own()
                dve.sem_inc(x_final, 1)
            statistics(0)
            for k in range(2):
                group_stats(k, 0)
            dve.wait_ge(wqk_in, 16)
            for which in range(2):
                for half in range(2):
                    split_qk(BQK[:, 0, which:which + 1], which, half, 2, (which, half) == (1, 1))
            dve.wait_ge(wv_in, 16)
            dve.wait_ge(wp_in, 16)
            for part in range(2):
                keep_v(2, 0, part, BV[:, 0:P])
            for h in range(H):
                for t in range(MT):
                    for half in range(2):
                        row_max(2, 0, h, t, half)
            for which in range(2):
                for half in range(2):
                    split_qk(BQK[:, 1, which:which + 1], which, half, 3, (which, half) == (1, 1))
            window(2, 0, window_jobs(prep=True, gn=True), 0, trail=False)
            window(3, 1, window_jobs(prep=True), 0)
            with dve.Fori(1, B - 1) as i:
                assert ring.now() % 2 == 0
                ring.enter(i - 1, RING_PER)
                steps.enter(i - 1, 8 + 16 + 4 * NORM_PARTS + 6)
                iteration(i, window, None)
                ring.leave(TURNS)
                steps.leave(TURNS)
            iteration(B - 1, window, None)
            for part in range(NORM_PARTS):
                normalise(2 * B + 1, 1, 1, part)
            for o in range(CT):
                for half in range(2):
                    residual(o, half, B - 1, BP)

            def scores3(n, t):
                wait(dve, copied3, 2 * n + 1)
                grid = [P, NHEAD, NHEAD, D]
                ins = nc.vector.tensor_tensor(
                    PQ.rearrange("p (h g d) -> p h g d", h=NHEAD, g=NHEAD),
                    ST[:, t % 2, C:2 * C].rearrange("p (g d) -> p g d", d=D).unsqueeze(1).broadcast_to(grid),
                    QC[t % 2].rearrange("p (h d) -> p h d", d=D).unsqueeze(2).broadcast_to(grid),
                    ALU.mult)
                ins.then_inc(k_used3, 1)
                wait(dve, k_used3, n + 1)
                wait(dve, pv_done3, n - 1)
                link(nc.vector.tensor_reduce(out=S3[t % 2][:, :, :],
                                             in_=PQ.rearrange("p (h g d) -> p h g d", h=NHEAD, g=NHEAD),
                                             op=ALU.add, axis=AX.X))
                link(nc.vector.tensor_reduce(out=M3[:, :], in_=S3[t % 2][:, :, :], op=ALU.max, axis=AX.X))
                nc.vector.tensor_tensor(S3[t % 2][:, :, :], S3[t % 2][:, :, :],
                                        M3[:, :].unsqueeze(2).broadcast_to([P, NHEAD, NHEAD]),
                                        ALU.subtract).then_inc(s_ready3, 1)
                wait(dve, s_ready3, n + 1)

            def probabilities3(n, at):
                wait(dve, e_done3, n + 1)
                link(nc.vector.tensor_reduce(out=R3[:, 0, :], in_=S3[at % 2][:, :, :], op=ALU.add, axis=AX.X))
                link(nc.vector.reciprocal(R3[:, 1, :], R3[:, 0, :]))
                nc.vector.tensor_tensor(S3[at % 2][:, :, :], S3[at % 2][:, :, :],
                                        R3[:, 1, :].unsqueeze(2).broadcast_to([P, NHEAD, NHEAD]),
                                        ALU.mult).then_inc(p_ready3, 1)
                wait(dve, p_ready3, n + 1)

            def outputs3(n, at):
                wait(dve, pv_done3, n + 1)
                wait(dve, tr_done3, n - 1)
                nc.vector.tensor_reduce(out=O3[at % 2],
                                        in_=PV[at % 2].rearrange("p (c g) -> p c g", g=NHEAD),
                                        op=ALU.add, axis=AX.X).then_inc(o_ready3, 1)

            def slot(b, t):
                n = MT * b + t
                first, last = isinstance(b, int) and b == 0, isinstance(b, int) and b == B - 1
                scores3(n, t)
                if not (first and t < 1):
                    probabilities3(n - 1, (t - 1) % MT)
                if not (first and t < 2):
                    outputs3(n - 2, (t - 2) % MT)
                if t == 3 and not first:
                    for o in range(CT):
                        residual(o, 1, B + b - 1, BP3)
                if t == 7:
                    for o in range(CT):
                        residual(o, 0, B + b, BP3)
                if t == 4 and not last:
                    statistics(B + b + 1)
                if t in (5, 6) and not last:
                    group_stats(t - 5, B + b + 1)

            dve.wait_ge(w3_in, 16 * 3)
            statistics(B)
            for k in range(2):
                group_stats(k, B)
            tile_slots(0, slot)
            with dve.Fori(1, B - 1) as b:
                assert ring.now() % 2 == 0
                ring.enter(b - 1, 6)
                steps.enter(b - 1, 16 + 16 + 6)
                tile_slots(b, slot)
                ring.leave(TURNS)
                steps.leave(TURNS)
            tile_slots(B - 1, slot)
            probabilities3(MT * B - 1, MT - 1)
            for n in range(MT * B - 2, MT * B):
                outputs3(n, n % MT)
            for o in range(CT):
                residual(o, 1, 2 * B - 1, BP3)


def kernel(**inputs):
    import numpy as np
    import concourse.bacc as bacc
    from concourse.bass_utils import run_bass_kernel_spmd

    a = {k: np.asarray(v) for k, v in inputs.items()}

    def column(v):
        return v.reshape(CT, P).T

    def rows(w):
        return w.T.reshape(CT, P, C).transpose(1, 0, 2)

    def packs(wq, wk, wv, wp, bq, bk, bv, bp, scale, bias):
        qk = np.stack([rows(wq).reshape(P, CT, 2, P), rows(wk).reshape(P, CT, 2, P)], axis=3)
        bqk = np.stack([column(bq), column(bk)], axis=2)
        return (np.concatenate([qk.reshape(P, -1), bqk.reshape(P, -1), column(scale), column(bias)], axis=1),
                np.concatenate([rows(wv).reshape(P, -1), np.broadcast_to(bv[None], (P, C))], axis=1),
                np.concatenate([rows(wp).reshape(P, -1), column(bp)], axis=1))

    w2 = a["L2_conv_w_qkv"].reshape(C // D, 3, D, C)
    b2 = a["L2_conv_b_qkv"].reshape(C // D, 3, D)
    p2 = packs(*(w2[:, n].reshape(C, C) for n in range(3)), a["L2_conv_w_proj"],
               *(b2[:, n].reshape(C) for n in range(3)), a["L2_conv_b_proj"],
               a["L2_conv_gn_scale"], a["L2_conv_gn_bias"])
    eye = np.eye(P)
    block = np.kron(np.eye(H), np.ones((D, D)))
    consts = np.concatenate([eye, np.kron(np.eye(P // 8), np.full((8, 8), 0.125)), block, block[:, ::D]],
                            axis=1).astype(np.float32)
    arrays = {
        "x": a["x"].reshape(B, C, N),
        "w_l0": np.concatenate([a["L0_conv_w_theta"], a["L0_conv_w_phi"], a["L0_conv_w_g"]], axis=0).T,
        "w_o": a["L0_conv_w_o"].T,
        "concepts": a["L0_conv_concepts"],
        "concepts_t": a["L0_conv_concepts"].T,
        "gammas": np.concatenate([a["L0_conv_gamma_sa"].reshape(1, 1), a["L0_conv_gamma_moca"].reshape(1, 1),
                                  a["L1_conv_gamma"].reshape(1, 1)], axis=1),
        "conv_w": a["L1_conv_conv_w"],
        "conv_wt": a["L1_conv_conv_w"].T,
        "conv_b": a["L1_conv_conv_b"].reshape(K, 1),
        "lin1_t": a["L1_conv_lin1_w"].T,
        "lin2_t": a["L1_conv_lin2_w"].T,
        "qk_pack": p2[0],
        "v_pack": p2[1],
        "p_pack": p2[2],
        "w3_pack": a["L3_conv_qkv_w"].T.reshape(CT, P, 3 * C).transpose(1, 0, 2).reshape(P, -1),
        "b3_row": a["L3_conv_qkv_b"].reshape(1, 3 * C),
        "p3_pack": np.concatenate([rows(a["L3_conv_proj_w"]).reshape(P, -1), column(a["L3_conv_proj_b"]),
                                   column(a["L3_conv_norm_w"]), column(a["L3_conv_norm_b"])], axis=1),
        "consts": consts,
    }
    nc = bacc.Bacc("TRN2", target_bir_lowering=False, num_devices=1)
    args, fed = [], {}
    for name, v in arrays.items():
        v = np.ascontiguousarray(v)
        fed[f"in_{name}"] = v
        args.append(nc.dram_tensor(f"in_{name}", v.shape, mybir.dt.from_np(v.dtype), kind="ExternalInput").ap())
    args.append(nc.dram_tensor("out_y", (B, C, N), mybir.dt.float32, kind="ExternalOutput").ap())
    program(nc, *args)
    r = run_bass_kernel_spmd(nc, [fed], core_ids=[0])
    return r.results[0]["out_y"].reshape(B, C, 32, 32)
```

```python
from contextlib import ExitStack

import concourse.bass as bass
from concourse import mybir

B, C, N, P = 8, 256, 1024, 128
CT = C // P
HALF = 512
MT = N // P
D = 32
H = P // D
K = 10
STEPS = 2 * MT
EXPS = H * STEPS
BANKS = 3
POOL_TILES = (0, 1, 3, 5)
POOL_SUMS = len(POOL_TILES) - 1
FIRST_SUMMED = 2
NORM_PARTS = 4
NHEAD = C // D
EPS = 1e-5
QK_COLS = CT * 2 * 2 * P
V_COLS = CT * C
P_COLS = CT * C
W3_COLS = CT * 3 * C


class Tally:

    def __init__(self, banks=BANKS):
        self.base, self.k, self.banks = 0, 0, banks

    def add(self, n=1):
        self.k += n
        return self.base + self.k

    def now(self):
        return self.base + self.k

    def slot(self):
        return (self.k - 1) % self.banks

    def restart(self, banks):
        self.base, self.k, self.banks = self.base + self.k, 0, banks

    def enter(self, turn, per):
        self.start, self.per = self.base + self.k, per
        self.base, self.k = self.start + turn * per, 0

    def leave(self, turns):
        assert self.k == self.per
        self.base, self.k = self.start + turns * self.per, 0


def wait(eng, sem, value):
    if isinstance(value, int) and value <= 0:
        return
    eng.wait_ge(sem, value)


def wait_apart(eng, sem, value, passed):
    if isinstance(value, int) and value <= 0:
        return
    eng.wait_ge(sem, value)
    if not isinstance(value, int):
        eng.sem_inc(passed, 1)


DVE_COST = {"v": 7, "post": 6, "stats": 25, "gn": 6, "qk": 15, "max": 6}


def window_jobs(post=False, prep=False, nxt=True, gn=False):
    jobs = [[] for _ in range(STEPS)]
    if nxt:
        jobs[0].append(("v", 0))
        jobs[1].append(("v", 1))
    if gn:
        jobs[1].append(("stats",))
        jobs[3].append(("gn", 0))
        jobs[5].append(("gn", 1))
    if post:
        for n in range(4):
            jobs[6 + n // 2].append(("post", n // 2, n % 2))
    if prep:
        for n in range(4):
            jobs[9 + 2 * (n // 2) + n % 2].append(("qk", n // 2, n % 2))
    if nxt:
        tiles = [("max", h, t, half) for h in range(H) for t in range(MT) for half in range(2)]
        load = [sum(DVE_COST[j[0]] for j in step) + 9 * (s % MT in range(1, 1 + NORM_PARTS))
                for s, step in enumerate(jobs)]
        steps = range(2, STEPS - 1)
        room = min(r for r in range(200)
                   if sum(max(0, r - load[s]) // DVE_COST["max"] for s in steps) >= len(tiles))
        for s in steps:
            n = max(0, room - load[s]) // DVE_COST["max"]
            jobs[s] += tiles[:n]
            tiles = tiles[n:]
        assert not tiles
    return jobs


AFTER = [("reread", 0)]
for _half in range(2):
    AFTER += [("add", 0, _half), ("encode", _half), ("concepts", _half), ("softmax", _half),
              ("turn", _half), ("mix", _half)]
AFTER += [("reread", 1), ("add", 1, 0), ("add", 1, 1), ("classes",), ("norms",), ("pool",), ("hidden",),
          ("gates",), ("regate",)] + [("write", _j) for _j in range(H)]


def after_jobs():
    jobs = [[] for _ in range(STEPS)]
    for n, stage in enumerate(AFTER):
        jobs[2 + n // 2].append(stage)
    return jobs


def first_jobs():
    maxima = [("max", h, t, half) for h in range(H) for t in range(MT) for half in range(2)]
    jobs = {("concepts", 1): [("stats",)], ("softmax", 1): [("gn", 0)], ("turn", 1): [("gn", 1)],
            ("add", 1, 0): [("qk", n // 2, n % 2, 0) for n in range(4)],
            ("add", 1, 1): [("v", 0), ("v", 1)]}
    for stage, n in ((("classes",), 4), (("norms",), 6), (("pool",), 2), (("hidden",), 3), (("gates",), 4),
                     (("regate",), 2), (("write", 0), 6), (("write", 1), 6), (("write", 2), 6),
                     (("write", 3), 6)):
        jobs[stage] = maxima[:n]
        maxima = maxima[n:]
    return jobs, maxima + [("qk", n // 2, n % 2, 1) for n in range(4)]


def program(nc, x, w_l0, w_o, concepts, concepts_t, gammas, conv_w, conv_wt, conv_b, lin1_t, lin2_t,
            qk_pack, v_pack, p_pack, w3_pack, b3_row, p3_pack, consts, out):
    f32, f32r = mybir.dt.float32, mybir.dt.float32r
    ALU, ACT, AX = mybir.AluOpType, mybir.ActivationFunctionType, mybir.AxisListType

    x_d = x.rearrange("b (t p) n -> b p t n", p=P)
    out_d = out.rearrange("b (t p) n -> b p t n", p=P)

    ctx = ExitStack()
    with ctx:
        def sb(name, shape, dt=f32):
            return ctx.enter_context(nc.sbuf_tensor(name, shape, dt))

        def sem(name):
            return ctx.enter_context(nc.semaphore(name))

        X = sb("X", [P, B, CT, N])
        QS = [sb(f"QS{i}", [3 * D + 2, H, N], f32r) for i in range(2)]
        KS = [sb(f"KS{i}", [3 * D + 2, H, N], f32r) for i in range(2)]
        HI = sb("HI", [P, 2, N], f32r)
        LO = sb("LO", [P, 2, N], f32r)
        VT = [sb(f"VT{i}", [P, MT, P]) for i in range(2)]
        PR = sb("PR", [P, 4, 2 * HALF])
        ACC = sb("ACC", [P, 2, 2 * HALF])
        OHU = [sb(f"OHU{i}", [P, 2, HALF]) for i in range(2)]
        OH = [[OHU[i][:, h, :] for h in range(2)] for i in range(2)]
        RC = sb("RC", [P, HALF])
        MX = sb("MX", [P, H, MT, 2])
        NM = sb("NM", [P, H, MT])
        NMH = sb("NMH", [P, H, MT], f32r)
        NML = sb("NML", [P, H, MT], f32r)
        ONES = sb("ONES", [P, P])
        XIN, XRES, XN = X[:, 0], X[:, 1], X[:, 2]
        WREG = X[:, 3].rearrange("p t n -> p (t n)")
        WREG2 = X[:, 4].rearrange("p t n -> p (t n)")
        WREG3 = X[:, 6].rearrange("p t n -> p (t n)")
        WQK_ALL = WREG[:, 0:QK_COLS + 8]
        WQK = WQK_ALL[:, 0:QK_COLS].rearrange("p (t u w c) -> p t u w c", t=CT, u=2, w=2)
        BQK = WQK_ALL[:, QK_COLS:QK_COLS + 4].rearrange("p (u w) -> p u w", u=2)
        GNS = WQK_ALL[:, QK_COLS + 4:QK_COLS + 6]
        GNB = WQK_ALL[:, QK_COLS + 6:QK_COLS + 8]
        WV_ALL = WREG[:, 1152:1152 + V_COLS + C]
        WV = WV_ALL[:, 0:V_COLS].rearrange("p (t c) -> p t c", t=CT)
        BV = WV_ALL[:, V_COLS:V_COLS + C]
        WP_ALL = WREG2[:, 0:P_COLS + CT]
        WP = WP_ALL[:, 0:P_COLS].rearrange("p (t c) -> p t c", t=CT)
        BP = WP_ALL[:, P_COLS:P_COLS + CT]
        P3_ALL = WREG2[:, 1024:1024 + P_COLS + 3 * CT]
        WP3 = P3_ALL[:, 0:P_COLS].rearrange("p (t c) -> p t c", t=CT)
        BP3 = P3_ALL[:, P_COLS:P_COLS + CT]
        GNS3 = P3_ALL[:, P_COLS + CT:P_COLS + 2 * CT]
        GNB3 = P3_ALL[:, P_COLS + 2 * CT:P_COLS + 3 * CT]
        W3_ALL = WREG3[:, 0:W3_COLS]
        W3 = W3_ALL.rearrange("p (t c) -> p t c", t=CT)
        TWO = slice(3 * D, 3 * D + 2)
        B3 = X[TWO, 7].rearrange("p t n -> p (t n)")[:, 0:3 * C]
        B3N = QS[0][TWO, 1, 0:3 * C]
        B3S = QS[0][TWO, 0, 0:3 * C]
        PQ = X[:, 5].rearrange("p t n -> p (t n)")
        PV = [PR[:, 2 * n:2 * n + 2, :].rearrange("p a q -> p (a q)") for n in range(2)]
        QC = [HI[:, 0, C * n:C * n + C].bitcast(f32) for n in range(2)]
        VC = [HI[:, 1, C * n:C * n + C].bitcast(f32) for n in range(4)]
        S3 = [sb(f"S3{n}", [P, NHEAD, NHEAD]) for n in range(2)]
        M3 = sb("M3", [P, NHEAD])
        R3 = sb("R3", [P, 2, NHEAD])
        O3 = [LO[:, 1, C * n:C * n + C].bitcast(f32) for n in range(2)]
        OT = ACC[:, :, :]
        BN6 = sb("BN6", [P, CT, 2, 6])
        MV = sb("MV", [P, CT, 2])
        MG = sb("MG", [P, CT])
        DEV = sb("DEV", [P, CT])
        S2 = sb("S2", [P, CT])
        VE = sb("VE", [P, CT])
        RSTD = sb("RSTD", [P, CT])
        GA = sb("GA", [P, CT])
        GT = sb("GT", [P, CT])
        GB = sb("GB", [P, CT])
        MHALF = sb("MHALF", [P, CT])
        CST = sb("CST", [P, 3 * P + H])
        IDENT, GROUP, BLOCK, BMASK = (CST[:, 0:P], CST[:, P:2 * P], CST[:, 2 * P:3 * P], CST[:, 3 * P:3 * P + H])
        WL0 = sb("WL0", [P, CT, 3 * D])
        WO = sb("WO", [P, H, C])
        CON = sb("CON", [P, D])
        CONT = sb("CONT", [P, H, P])
        GAM = sb("GAM", [P, 3])
        CW = sb("CW", [P, C])
        CW3 = sb("CW3", [P, C])
        CWT = sb("CWT", [P, CT, D])
        CB = sb("CB", [P, 1])
        L1T = sb("L1T", [P, 4 * K])
        L2T = sb("L2T", [4 * K, D])
        ZB = sb("ZB", [P, P])
        RW = sb("RW", [P, 1])
        RWS = sb("RWS", [P, 1])
        WORK = [(HI.rearrange("p a n -> p (a n)").bitcast(f32), LO.rearrange("p a n -> p (a n)").bitcast(f32)),
                (PR[:, 0:2, :].rearrange("p a n -> p (a n)"), PR[:, 2:4, :].rearrange("p a n -> p (a n)"))]
        LATC = [OHU[g].rearrange("p h q -> p (h q)") for g in range(2)]
        LAT = [VT[g].rearrange("p t c -> p (t c)") for g in range(2)]
        ENC = sb("ENC", [P, HALF])
        E = [WORK[g][0].rearrange("p (j q) -> p j q", q=P) for g in range(2)]
        PT = [WORK[g][1].rearrange("p (j q) -> p j q", q=HALF) for g in range(2)]
        OM = [WORK[g][0][:, 0:N] for g in range(2)]
        SQ = [WORK[g][0][:, N:2 * N] for g in range(2)]
        NRM = [WORK[g][1][:, 0:N] for g in range(2)]
        NRI = [WORK[g][1][:, N:2 * N] for g in range(2)]
        PRB = LAT
        CW4 = [LATC[g].rearrange("p (j c) -> p j c", j=H) for g in range(2)]
        CM4 = sb("CM4", [P, 4, H])
        CS = sb("CS", [P, 4 * H])
        CR = sb("CR", [P, 4 * H])
        PSM = sb("PSM", [P, 2])
        POOLED = sb("POOLED", [P, 1])
        PM = sb("PM", [P, H])
        HID = sb("HID", [4 * K, H])
        ZE = sb("ZE", [P, 1])
        RG = sb("RG", [P, 1])

        ST = ctx.enter_context(nc.psum_tensor("ST", [P, BANKS, HALF], f32))
        RING = ctx.enter_context(nc.psum_tensor("RING", [P, BANKS, HALF], f32))
        AV = ctx.enter_context(nc.psum_tensor("AV", [P, HALF], f32))
        SUM = ctx.enter_context(nc.psum_tensor("SUM", [P, HALF], f32))

        V3 = [ST[:, 2, 0:C], RING[:, 2, 0:C]]

        x_in = [sem(f"x_in{b}") for b in range(2)]
        w_in = sem("w_in")
        zeroed = sem("zeroed")
        scaled = sem("scaled")
        ring_full = sem("ring_full")
        ring_free = sem("ring_free")
        dve_step = sem("dve_step")
        stage_ready = sem("stage_ready")
        stk = [sem(f"stk{h}") for h in range(H)]
        v_ready = sem("v_ready")
        negmax_ready = sem("negmax_ready")
        rows_in = sem("rows_in")
        st_full = sem("st_full")
        exp_done = sem("exp_done")
        pool_used = sem("pool_used")
        av_done = sem("av_done")
        half_done = sem("half_done")
        half_kept = sem("half_kept")
        norm_done = sem("norm_done")
        cs_ready = sem("cs_ready")
        act_done = sem("act_done")
        pe_ready = sem("pe_ready")
        x_final = sem("x_final")
        x_out = sem("x_out")
        xin_in = sem("xin_in")
        xres_in = sem("xres_in")
        wqk_in = sem("wqk_in")
        wv_in = sem("wv_in")
        wp_in = sem("wp_in")
        gn_ready = sem("gn_ready")
        var_ready = sem("var_ready")
        pool_gn = sem("pool_gn")
        xn_ready = sem("xn_ready")
        y_ready = sem("y_ready")
        passed = sem("passed")
        y_out = sem("y_out")

        w3_in = sem("w3_in")
        qkv3 = sem("qkv3")
        copied3 = sem("copied3")
        k_used3 = sem("k_used3")
        s_ready3 = sem("s_ready3")
        e_done3 = sem("e_done3")
        p_ready3 = sem("p_ready3")
        pv_done3 = sem("pv_done3")
        o_ready3 = sem("o_ready3")
        tr_done3 = sem("tr_done3")
        ot_done3 = sem("ot_done3")

        block = ctx.enter_context(nc.Block())

        def iteration(i, window, tallies, turns=None):
            u = 2 * i + 2
            last = isinstance(i, int) and i == B - 1
            first = isinstance(i, int) and i == 0
            window(u, 0, window_jobs(post=not first, prep=not last, gn=not last), i)
            window(u + 1, 1, window_jobs(prep=not last, nxt=not last), i)

        RING_PER = 2 + 4 + 2 + 4 + 64 + 2 + 4 + 64
        TURNS = B - 2

        def tile_slots(b, slot):
            for t in range(MT):
                slot(b, t)

        @block.sync
        def _(sp):
            def load(dst, src, s):
                sp.dma_start(dst, src).then_inc(s, 16)

            def stacks(u, par):
                wait_apart(sp, stage_ready, u + 1, passed)
                wait(sp, st_full, EXPS * (u - 1))
                for h in range(H):
                    rows = slice(D * h, D * h + D)
                    for j, (q, k) in enumerate(((HI, HI), (LO, HI), (HI, LO))):
                        load(QS[par][D * j:D * j + D, h, :].bitcast(f32), q[rows, 0, :].bitcast(f32), stk[h])
                        load(KS[par][D * j:D * j + D, h, :].bitcast(f32), k[rows, 1, :].bitcast(f32), stk[h])

            def rows(u, par):
                for h in range(H):
                    wait(sp, negmax_ready, H * u + h + 1)
                    for r, src in ((3 * D, NMH), (3 * D + 1, NML)):
                        load(QS[par][r:r + 1, h, :].rearrange("o (p t) -> o p t", t=MT).bitcast(f32),
                             src[:, h, :].bitcast(f32), rows_in)

            load(CST[:, :], consts, w_in)
            load(WL0[:, :, :], w_l0.rearrange("(t p) o -> p t o", p=P), w_in)
            for b in range(H):
                load(X[:, b], x_d[b], x_in[0])
            load(GAM[:, :], gammas.broadcast_to([P, 3]), w_in)
            load(CON[:, :], concepts, w_in)
            sp.wait_ge(zeroed, 1)
            load(CWT[:, :, 0:K], conv_wt.rearrange("(t p) o -> p t o", p=P), w_in)
            load(L2T[:, 0:K], lin2_t, w_in)
            for j in range(H):
                load(WO[D * j:D * j + D, j, :], w_o, w_in)
                load(CONT[D * j:D * j + D, j, :], concepts_t, w_in)
                load(CW[D * j:D * j + K, :], conv_w, w_in)
                load(CB[D * j:D * j + K, :], conv_b, w_in)
                load(L1T[D * j:D * j + K, :], lin1_t, w_in)
            for b in range(H, B):
                load(X[:, b], x_d[b], x_in[1])
            stacks(0, 0)
            rows(0, 0)
            stacks(1, 1)
            rows(1, 1)
            for g in range(2):
                sp.wait_ge(x_final, g + 1)
                for b in range(H * g, H * g + H):
                    load(out_d[b], X[:, b], x_out)
                if g == 0:
                    sp.wait_ge(x_out, 16 * H)
                    load(XIN, out_d[0], xin_in)
                    load(WQK_ALL, qk_pack, wqk_in)
                    load(WV_ALL, v_pack, wv_in)
                    stacks(2, 0)
            rows(2, 0)

            def sp_iteration(i):
                u = 2 * i + 2
                first, last = isinstance(i, int) and i == 0, isinstance(i, int) and i == B - 1
                if not last:
                    wait_apart(sp, xn_ready, CT * (i + 1), passed)
                    load(XIN, out_d[i + 1] if isinstance(i, int) else out_d[bass.ds(i + 1, 1)][0], xin_in)
                stacks(u + 1, 1)
                if first:
                    sp.wait_ge(x_out, 16 * B)
                    load(WP_ALL, p_pack, wp_in)
                    load(P3_ALL, p3_pack, w3_in)
                    load(W3_ALL, w3_pack, w3_in)
                    load(B3, b3_row.broadcast_to([2, 3 * C]), w3_in)
                if not first:
                    wait_apart(sp, y_ready, i, passed)
                    load(out_d[i - 1] if isinstance(i, int) else out_d[bass.ds(i - 1, 1)][0], XRES, y_out)
                rows(u + 1, 1)
                if not last:
                    stacks(u + 2, 0)
                wait_apart(sp, y_out, 16 * i, passed)
                load(XRES, out_d[i] if isinstance(i, int) else out_d[bass.ds(i, 1)][0], xres_in)
                if not last:
                    rows(u + 2, 0)

            sp_iteration(0)
            with sp.Fori(1, B - 1) as i:
                sp_iteration(i)
            sp_iteration(B - 1)
            sp.wait_ge(xn_ready, CT * B)
            load(XIN, out_d[0], xin_in)
            sp.wait_ge(y_ready, B)
            load(out_d[B - 1], XRES, y_out)
            sp.wait_ge(y_out, 16 * B)
            load(XRES, out_d[0], xres_in)

            def sp_batch(b):
                wait_apart(sp, xn_ready, CT * (B + b + 1), passed)
                load(XIN, out_d[b + 1] if isinstance(b, int) else out_d[bass.ds(b + 1, 1)][0], xin_in)

            def sp_store(b):
                wait_apart(sp, y_ready, B + b + 1, passed)
                load(out_d[b] if isinstance(b, int) else out_d[bass.ds(b, 1)][0], XRES, y_out)
                wait_apart(sp, y_out, 16 * (B + b + 1), passed)
                load(XRES, out_d[b + 1] if isinstance(b, int) else out_d[bass.ds(b + 1, 1)][0], xres_in)

            sp_batch(0)
            with sp.Fori(1, B - 1) as b:
                sp_batch(b)
                sp_store(b - 1)
            sp_store(B - 2)
            sp.wait_ge(y_ready, 2 * B)
            load(out_d[B - 1], XRES, y_out)
            sp.wait_ge(y_out, 16 * 2 * B)

        @block.tensor
        def _(pe):
            ring = Tally()
            pe_need = Tally()
            mm = nc.tensor.matmul

            def bank():
                wait(pe, ring_free, ring.add() - ring.banks)
                return RING[:, ring.slot(), :]

            def all_read():
                wait(pe, ring_free, ring.now())

            def qk_l0(g, which, half):
                dst = bank()
                for t in range(CT):
                    for j in range(H):
                        last = mm(dst[D * j:D * j + D, :], WL0[:, t, D * which:D * which + D],
                                  X[:, H * g + j, t, HALF * half:HALF * half + HALF],
                                  start=(t == 0), stop=(t == CT - 1))
                last.then_inc(ring_full, 1)

            def v_l0(g, part):
                dst = bank()
                for m in range(4):
                    mt = 4 * part + m
                    for j in range(H):
                        for t in range(CT):
                            last = mm(dst[:, P * m + D * j:P * m + D * j + D],
                                      X[:, H * g + j, t, P * mt:P * mt + P], WL0[:, t, 2 * D:3 * D],
                                      start=(t == 0), stop=(t == CT - 1))
                last.then_inc(ring_full, 1)

            def max_scores(u, par, h, t, half):
                if t == 0 and half == 0:
                    wait(pe, stk[h], 96 * (u + 1))
                mm(bank(), QS[par][0:3 * D, h, t:N:MT], KS[par][0:3 * D, h, HALF * half:HALF * half + HALF],
                   start=True, stop=True).then_inc(ring_full, 1)

            def scores(u, par, s, heads):
                half, mt = s // MT, s % MT
                for h in heads:
                    if s == 0 and h == 0:
                        wait(pe, rows_in, 2 * H * 16 * (u + 1))
                        wait(pe, exp_done, EXPS * u)
                    else:
                        wait(pe, exp_done, EXPS * u + H * s + h + 1 - BANKS)
                    mm(ST[:, (H * s + h) % BANKS, :], KS[par][:, h, P * mt:P * mt + P],
                       QS[par][:, h, HALF * half:HALF * half + HALF],
                       start=True, stop=True).then_inc(st_full, 1)

            def values(u, par, s):
                half, mt = s // MT, s % MT
                if mt == 0:
                    wait(pe, half_kept, 2 * (2 * u + half))
                    wait(pe, v_ready, 2 * (u + 1))
                wait(pe, exp_done, EXPS * u + H * s + H)
                for h in range(H):
                    last = mm(AV[D * h:D * h + D, :], VT[par][:, mt, D * h:D * h + D],
                              PR[:, (2 * s + h // 2) % 4, HALF * (h % 2):HALF * (h % 2) + HALF],
                              start=(mt == 0), stop=(mt == MT - 1))
                if mt in POOL_TILES:
                    last.then_inc(av_done, 1)

            def sums(u, s):
                half, mt = s // MT, s % MT
                if mt not in POOL_TILES:
                    for h in range(H):
                        last = mm(SUM[D * h:D * h + D, :], ONES[:, 0:D],
                                  PR[:, (2 * s + h // 2) % 4, HALF * (h % 2):HALF * (h % 2) + HALF],
                                  start=(mt == FIRST_SUMMED), stop=False)
                    last.then_inc(av_done, 1)
                if mt == MT - 1:
                    wait(pe, pool_used, 2 * POOL_SUMS * (2 * u + half + 1))
                    for h in range(H):
                        last = mm(SUM[D * h:D * h + D, :], ONES[:, 0:D],
                                  ACC[:, h // 2, HALF * (h % 2):HALF * (h % 2) + HALF], start=False, stop=True)
                    last.then_inc(half_done, 1)

            def v_product(u, part, batch, unit):
                dst = bank()
                if part == 0:
                    pe.wait_ge(wv_in, 16)
                for m in range(4):
                    mt = 4 * part + m
                    for t in range(CT):
                        last = mm(dst[:, P * m:P * m + P], XN[:, t, P * mt:P * mt + P],
                                  WV[:, t, P * unit:P * unit + P], start=(t == 0), stop=(t == CT - 1))
                last.then_inc(ring_full, 1)

            def qk_product(which, half, batch, unit):
                dst = bank()
                if which == 0 and half == 0:
                    pe.wait_ge(wqk_in, 16)
                    wait(pe, xn_ready, CT * (batch + 1))
                for t in range(CT):
                    last = mm(dst, WQK[:, t, unit, which, :], XN[:, t, HALF * half:HALF * half + HALF],
                              start=(t == 0), stop=(t == CT - 1))
                last.then_inc(ring_full, 1)

            def group_sums(k, batch):
                dst = bank()
                wait(pe, gn_ready, 2 * batch + k + 1)
                mm(dst[:, 0:CT], GROUP, MV[:, :, 0] if k == 0 else S2[:, :],
                   start=True, stop=True).then_inc(ring_full, 1)

            def output_product(o, half, batch):
                dst = bank()
                if o == 0 and half == 0:
                    pe.wait_ge(wp_in, 16)
                    wait(pe, norm_done, 2 * NORM_PARTS * (2 * batch + 4))
                for t in range(CT):
                    last = mm(dst, WP[:, t, P * o:P * o + P], OH[t][half],
                              start=(t == 0), stop=(t == CT - 1))
                last.then_inc(ring_full, 1)

            def window(u, par, jobs, i, trail=True):
                def run(todo):
                    for job in todo:
                        if job[0] == "max":
                            max_scores(u + 1, 1 - par, *job[1:])
                        elif job[0] == "v" and i is None:
                            v_l0(1, job[1])
                        elif job[0] == "v":
                            v_product(u + 1, job[1], i + par, 1 - par)
                        elif job[0] == "qk":
                            qk_product(*job[1:], i + 1, par)
                        elif job[0] == "gn":
                            group_sums(job[1], i + 1)
                        elif job[0] == "post":
                            output_product(*job[1:], i - 1)
                        else:
                            after(0, job)

                for s in range(STEPS):
                    scores(u, par, s, (0,))
                    run(jobs[s][0:1])
                    scores(u, par, s, (1, 2))
                    run(jobs[s][1:2])
                    if s:
                        values(u, par, s - 1)
                    elif trail:
                        values(u - 1, 1 - par, STEPS - 1)
                    scores(u, par, s, (3,))
                    run(jobs[s][2:3])
                    if s:
                        sums(u, s - 1)
                    elif trail:
                        sums(u - 1, STEPS - 1)
                    run(jobs[s][3:])

            def after(g, stage):
                what, half = stage[0], stage[-1]
                if what == "add":
                    src = LAT[g]
                    if stage[1] == 0 or half == 0:
                        all_read()
                    if half == 0:
                        pe.wait_ge(pe_ready, pe_need.add())
                    for j in range(H):
                        for t in range(CT):
                            mm(bank(), WO[:, j, P * t:P * t + P], src[:, HALF * half:HALF * half + HALF],
                               start=True, stop=True).then_inc(ring_full, 1)
                elif what == "encode":
                    all_read()
                    qk_l0(g, 0, half)
                elif what == "concepts":
                    all_read()
                    for n in range(4):
                        mm(bank(), ENC[:, P * n:P * n + P], CONT[:, :, :].rearrange("p j q -> p (j q)"),
                           start=True, stop=True).then_inc(ring_full, 1)
                elif what == "turn":
                    pe.wait_ge(pe_ready, pe_need.add())
                    for n in range(4):
                        dst = bank()
                        for j in range(H):
                            last = nc.tensor.transpose(dst[:, P * j:P * j + P], E[g][:, H * n + j, :], IDENT)
                        last.then_inc(ring_full, 1)
                elif what == "mix":
                    all_read()
                    dst = bank()
                    for j in range(H):
                        last = mm(dst[D * j:D * j + D, :], CON[:, :], PT[g][:, j, :], start=True, stop=True)
                    last.then_inc(ring_full, 1)
                elif what == "classes":
                    all_read()
                    for part in range(2):
                        cols = slice(HALF * part, HALF * part + HALF)
                        dst = bank()
                        for t in range(CT):
                            for j in range(H):
                                last = mm(dst[D * j:D * j + D, :], CWT[:, t, :], X[:, H * g + j, t, cols],
                                          start=(t == 0), stop=(t == CT - 1))
                        last.then_inc(ring_full, 1)
                elif what == "norms":
                    pe.wait_ge(pe_ready, pe_need.add())
                    for part in range(2):
                        mm(bank(), BLOCK, SQ[g][:, HALF * part:HALF * part + HALF],
                           start=True, stop=True).then_inc(ring_full, 1)
                elif what == "hidden":
                    pe.wait_ge(pe_ready, pe_need.add())
                    mm(bank()[0:4 * K, 0:H], L1T[:, :], PM[:, :], start=True, stop=True).then_inc(ring_full, 1)
                elif what == "gates":
                    all_read()
                    dst = bank()
                    for j in range(H):
                        last = mm(dst[D * j:D * j + D, 0:1], L2T[:, :], HID[:, j:j + 1],
                                  start=True, stop=True)
                    last.then_inc(ring_full, 1)
                elif what == "write":
                    j = stage[1]
                    if j == 0:
                        pe.wait_ge(pe_ready, pe_need.add())
                    for t in range(CT):
                        for part in range(2):
                            mm(bank(), CW4[g][:, j, P * t:P * t + P],
                               PRB[g][:, HALF * part:HALF * part + HALF],
                               start=True, stop=True).then_inc(ring_full, 1)

            def prepare(jobs):
                for job in jobs:
                    if job[0] == "gn":
                        group_sums(job[1], 0)
                    elif job[0] == "qk":
                        qk_product(job[1], job[2], 0, job[3])
                    elif job[0] == "v":
                        v_product(2, job[1], 0, 0)
                    elif job[0] == "max":
                        max_scores(2, 0, *job[1:])

            pe.wait_ge(scaled, 1)
            pe.wait_ge(x_in[0], 16 * H)
            for which in range(2):
                for half in range(2):
                    qk_l0(0, which, half)
            for part in range(2):
                v_l0(0, part)
            for h in range(H):
                for t in range(MT):
                    for half in range(2):
                        max_scores(0, 0, h, t, half)
            pe.wait_ge(x_in[1], 16 * H)
            for which in range(2):
                for half in range(2):
                    qk_l0(1, which, half)
            window(0, 0, window_jobs(), None, trail=False)
            window(1, 1, after_jobs(), None)
            values(1, 1, STEPS - 1)
            sums(1, STEPS - 1)
            between, rest = first_jobs()
            for stage in AFTER:
                after(1, stage)
                prepare(between.get(stage, ()))
            prepare(rest)
            window(2, 0, window_jobs(prep=True, gn=True), 0, trail=False)
            window(3, 1, window_jobs(prep=True), 0)
            with pe.Fori(1, B - 1) as i:
                ring.enter(i - 1, RING_PER)
                all_read()
                iteration(i, window, None)
                ring.leave(TURNS)
            all_read()
            iteration(B - 1, window, None)
            values(2 * B + 1, 1, STEPS - 1)
            sums(2 * B + 1, STEPS - 1)
            for o in range(CT):
                for half in range(2):
                    output_product(o, half, B - 1)

            def project3(half):
                for o in range(CT):
                    dst = bank()
                    for t in range(CT):
                        last = mm(dst, WP3[:, t, P * o:P * o + P], OT[:, t, HALF * half:HALF * half + HALF],
                                  start=(t == 0), stop=(t == CT - 1))
                    last.then_inc(ring_full, 1)

            def transpose3(n):
                wait(pe, o_ready3, n + 1)
                wait(pe, ot_done3, n - 1)
                at = n if isinstance(n, int) else tile_at[0]
                dst, src = (AV, SUM)[at % 2], O3[at % 2]
                for t in range(CT):
                    last = nc.tensor.transpose(dst[:, P * t:P * t + P], src[:, P * t:P * t + P], IDENT)
                last.then_inc(tr_done3, 1)

            tile_at = [0]

            def slot(b, t):
                n = MT * b + t
                first = isinstance(b, int) and b == 0
                if t == 0:
                    wait(pe, xn_ready, CT * (B + b + 1))
                wait(pe, copied3, 2 * (n - 1))
                wait(pe, k_used3, n - 1)
                for c0, c1, dst in ((0, 2 * C, ST[:, t % 2, :]), (2 * C, 3 * C, V3[t % 2])):
                    for ct in range(CT):
                        mm(dst, XN[:, ct, P * t:P * t + P], W3[:, ct, c0:c1], start=(ct == 0), stop=False)
                    last = mm(dst, KS[0][TWO, 0, 0:P], B3S[:, c0:c1], start=False, stop=True)
                last.then_inc(qkv3, 1)
                if not (first and t < 4) and t % 4 == 3:
                    wait(pe, ot_done3, n - 3)
                    project3((t // 4 + 1) % 2)
                if not (first and t < 3):
                    tile_at[0] = (t - 3) % MT
                    transpose3(n - 3)
                if t in (5, 6) and not (isinstance(b, int) and b == B - 1):
                    group_sums(t - 5, B + b + 1)

            all_read()
            ring.restart(2)
            pe.wait_ge(w3_in, 16 * 3)
            pe.wait_ge(pe_ready, pe_need.add())
            for k in range(2):
                group_sums(k, B)
            tile_slots(0, slot)
            with pe.Fori(1, B - 1) as b:
                ring.enter(b - 1, 6)
                all_read()
                tile_slots(b, slot)
                ring.leave(TURNS)
            all_read()
            tile_slots(B - 1, slot)
            for n in range(MT * B - 3, MT * B):
                transpose3(n)
            pe.wait_ge(ot_done3, MT * B)
            project3(1)

        @block.scalar
        def _(act):
            cs = Tally()

            def keep_half(u, par, half):
                wait(act, half_done, 2 * u + half + 1)
                wait(act, norm_done, NORM_PARTS * (2 * u + half))
                nc.scalar.activation(RC[:, :], SUM[:, :], ACT.Copy).then_inc(half_kept, 1)
                nc.scalar.activation(OH[par][half], AV[:, :], ACT.Copy).then_inc(half_kept, 1)

            def window(u, par, jobs, i, trail=True):
                for s in range(STEPS):
                    for h in range(H):
                        pair, one = h // 2, h % 2
                        wait(act, st_full, EXPS * u + H * s + h + 1)
                        if one == 0:
                            wait(act, av_done, STEPS * u + s - 1)
                            if (s - 2) % MT in POOL_TILES:
                                wait(act, pool_used, 2 * POOL_SUMS * (2 * u + (s - 2) // MT)
                                     + 2 * max(POOL_TILES.index((s - 2) % MT) - 1, 0) + pair + 1)
                        nc.scalar.activation(PR[:, (2 * s + pair) % 4, HALF * one:HALF * one + HALF],
                                             ST[:, (H * s + h) % BANKS, :], ACT.Exp,
                                             scale=1.0 if i is None else float(D) ** -0.5
                                             ).then_inc(exp_done, 1)
                    if s == 0 and trail:
                        keep_half(u - 1, 1 - par, 1)
                    if s == MT:
                        keep_half(u, par, 0)
                    if par == 1 and i is None:
                        for stage in jobs[s]:
                            after(0, stage)

            def after(g, stage):
                if stage[0] == "concepts":
                    act.wait_ge(cs_ready, cs.add())
                    nc.scalar.activation(E[g], E[g], ACT.Exp).then_inc(act_done, 1)
                elif stage[0] == "norms":
                    act.wait_ge(cs_ready, cs.add())
                    nc.scalar.activation(NRM[g], NRM[g], ACT.Sqrt).then_inc(act_done, 1)
                elif stage[0] == "gates":
                    act.wait_ge(cs_ready, cs.add())
                    nc.scalar.activation(ZE[:, :], ZE[:, :], ACT.Sigmoid).then_inc(act_done, 1)

            act.wait_ge(cs_ready, cs.add())
            nc.scalar.activation(RWS[:, :], RW[:, :], ACT.Sqrt).then_inc(act_done, 1)
            window(0, 0, None, None, trail=False)
            window(1, 1, after_jobs(), None)
            keep_half(1, 1, 1)
            for stage in AFTER:
                after(1, stage)
            window(2, 0, None, 0, trail=False)
            window(3, 1, None, 0)
            with act.Fori(1, B - 1) as i:
                iteration(i, window, None)
            iteration(B - 1, window, None)
            keep_half(2 * B + 1, 1, 1)

            def apply3(batch):
                wait(act, pool_gn, 4 * (batch + 1))
                for t in range(CT):
                    nc.scalar.activation(XN[:, t], XIN[:, t], ACT.Identity, bias=GB[:, t:t + 1],
                                         scale=GA[:, t:t + 1]).then_inc(xn_ready, 1)

            def exp3(n, at):
                wait(act, s_ready3, n + 1)
                nc.scalar.activation(S3[at % 2][:, :, :], S3[at % 2][:, :, :], ACT.Exp,
                                     scale=float(D) ** -0.5).then_inc(e_done3, 1)

            def keep3(n, at):
                wait(act, tr_done3, n + 1)
                nc.scalar.activation(OT[:, :, P * at:P * at + P],
                                     (AV, SUM)[at % 2][:, 0:C].rearrange("p (t q) -> p t q", t=CT),
                                     ACT.Copy).then_inc(ot_done3, 1)

            def slot(b, t):
                n = MT * b + t
                first = isinstance(b, int) and b == 0
                wait(act, qkv3, n + 1)
                wait(act, k_used3, n - 1)
                nc.scalar.activation(QC[t % 2], ST[:, t % 2, 0:C], ACT.Copy).then_inc(copied3, 1)
                wait(act, pv_done3, n - 3)
                nc.scalar.activation(VC[t % 4], V3[t % 2], ACT.Copy).then_inc(copied3, 1)
                if not (first and t < 1):
                    exp3(n - 1, (t - 1) % MT)
                if not (first and t < 3):
                    keep3(n - 3, (t - 3) % MT)
                if t == MT - 1 and not (isinstance(b, int) and b == B - 1):
                    apply3(B + b + 1)

            apply3(B)
            tile_slots(0, slot)
            with act.Fori(1, B - 1) as b:
                tile_slots(b, slot)
            tile_slots(B - 1, slot)
            exp3(MT * B - 1, MT - 1)
            for n in range(MT * B - 3, MT * B):
                keep3(n, n % MT)

        @block.gpsimd
        def _(pool):
            gn = Tally()

            def norm_factors(batch, scale, bias):
                wait(pool, var_ready, batch + 1)

                def link(ins):
                    ins.then_inc(pool_gn, 1)
                    wait_apart(pool, pool_gn, gn.add(), passed)

                link(nc.gpsimd.tensor_tensor(RSTD[:, :], VE[:, :], MHALF[:, :], ALU.pow))
                link(nc.gpsimd.tensor_tensor(GA[:, :], RSTD[:, :], scale, ALU.mult))
                link(nc.gpsimd.tensor_tensor(GT[:, :], MG[:, :], GA[:, :], ALU.mult))
                link(nc.gpsimd.tensor_tensor(GB[:, :], bias, GT[:, :], ALU.subtract))

            def norm_apply(batch):
                pool.wait_ge(wqk_in, 16)
                norm_factors(batch, GNS, GNB)
                for t in range(CT):
                    nc.gpsimd.tensor_scalar(XN[:, t], XIN[:, t], GA[:, t:t + 1], GB[:, t:t + 1],
                                            ALU.mult, ALU.add).then_inc(xn_ready, 1)

            def window(u, par, jobs, i):
                for s in range(STEPS):
                    half, mt = s // MT, s % MT
                    if mt in POOL_TILES[1:]:
                        rank = POOL_TILES.index(mt)
                        for pair in range(2):
                            wait_apart(pool, exp_done, EXPS * u + H * s + 2 * pair + 2, passed)
                            if rank == 1:
                                wait_apart(pool, half_done, 2 * u + half, passed)
                                so_far = PR[:, (2 * (s - 1) + pair) % 4, :]
                            else:
                                wait_apart(pool, pool_used, 2 * POOL_SUMS * (2 * u + half) + 2 * (rank - 2)
                                           + pair + 1, passed)
                                so_far = ACC[:, pair, :]
                            nc.gpsimd.tensor_tensor(ACC[:, pair, :], so_far, PR[:, (2 * s + pair) % 4, :],
                                                    ALU.add).then_inc(pool_used, 1)
                    if jobs and ("gn", 1) in jobs[s]:
                        norm_apply(i + 1)

            nc.gpsimd.memset(MHALF[:, :], -0.5)
            window(0, 0, None, None)
            window(1, 1, None, None)
            norm_apply(0)
            window(2, 0, window_jobs(prep=True, gn=True), 0)
            window(3, 1, None, 0)
            with pool.Fori(1, B - 1) as i:
                gn.enter(i - 1, 4)
                iteration(i, window, None)
                gn.leave(TURNS)
            iteration(B - 1, window, None)

            def products(n, at):
                wait(pool, p_ready3, n + 1)
                wait(pool, copied3, 2 * n + 2)
                wait(pool, o_ready3, n - 1)
                nc.gpsimd.tensor_tensor(
                    PV[at % 2].rearrange("p (h d g) -> p h d g", h=NHEAD, d=D),
                    S3[at % 2][:, :, :].unsqueeze(2).broadcast_to([P, NHEAD, D, NHEAD]),
                    VC[at % 4].rearrange("p (g d) -> p d g", d=D).unsqueeze(1).broadcast_to(
                        [P, NHEAD, D, NHEAD]), ALU.mult).then_inc(pv_done3, 1)

            def slot(b, t):
                n = MT * b + t
                if not (isinstance(b, int) and b == 0 and t < 1):
                    products(n - 1, (t - 1) % MT)
                if t == 6 and not (isinstance(b, int) and b == B - 1):
                    norm_factors(B + b + 1, GNS3, GNB3)

            pool.wait_ge(w3_in, 16 * 3)
            norm_factors(B, GNS3, GNB3)
            tile_slots(0, slot)
            with pool.Fori(1, B - 1) as b:
                gn.enter(b - 1, 4)
                tile_slots(b, slot)
                gn.leave(TURNS)
            tile_slots(B - 1, slot)
            products(MT * B - 1, MT - 1)

        @block.vector
        def _(dve):
            ring = Tally()
            steps = Tally()
            acts = Tally()

            def link(ins, alone=False):
                ins.then_inc(dve_step, 1)
                if alone:
                    wait_apart(dve, dve_step, steps.add(), passed)
                else:
                    dve.wait_ge(dve_step, steps.add())

            def bank():
                wait(dve, ring_full, ring.add())
                return RING[:, ring.slot(), :]

            def own():
                dve.wait_ge(ring_free, ring.now())

            def split_qk(bias, which, half, u, done):
                src = bank()
                cols = slice(HALF * half, HALF * half + HALF)
                if which == 0 and half == 0:
                    for h in range(H):
                        wait(dve, stk[h], 96 * u)
                link(nc.vector.tensor_scalar(HI[:, which, cols], src, bias, None, ALU.add))
                nc.vector.scalar_tensor_tensor(out=LO[:, which, cols], in0=src, scalar=bias,
                                               in1=HI[:, which, cols].bitcast(f32), op0=ALU.add,
                                               op1=ALU.subtract).then_inc(ring_free, 1)
                if done:
                    own()
                    dve.sem_inc(stage_ready, 1)

            def keep_v(u, par, part, bias):
                src = bank()
                wait(dve, half_done, 2 * (u - 1))
                nc.vector.tensor_tensor(VT[par][:, 4 * part:4 * part + 4, :],
                                        src.rearrange("p (m c) -> p m c", c=P),
                                        bias.unsqueeze(1).broadcast_to([P, 4, P]),
                                        ALU.add).then_inc(ring_free, 1)
                own()
                dve.sem_inc(v_ready, 1)

            def row_max(u, par, h, t, half):
                nc.vector.tensor_reduce(out=MX[:, h, t, half:half + 1], in_=bank(), op=ALU.max,
                                        axis=AX.X).then_inc(ring_free, 1)
                if t == MT - 1 and half == 1:
                    own()
                    if h == 0:
                        wait(dve, rows_in, 2 * H * 16 * u)
                    link(nc.vector.tensor_reduce(out=NM[:, h, :], in_=MX[:, h], op=ALU.max, axis=AX.X,
                                                 negate=True))
                    link(nc.vector.tensor_copy(NMH[:, h, :], NM[:, h, :]))
                    nc.vector.tensor_tensor(NML[:, h, :], NM[:, h, :], NMH[:, h, :].bitcast(f32),
                                            ALU.subtract).then_inc(negmax_ready, 1)

            def normalise(u, par, half, part):
                if part == 0:
                    wait(dve, half_kept, 2 * (2 * u + half + 1))
                w = HALF // NORM_PARTS
                cols = slice(w * part, w * part + w)
                link(nc.vector.reciprocal(RC[:, cols], RC[:, cols]))
                nc.vector.tensor_tensor(OH[par][half][:, cols], OH[par][half][:, cols], RC[:, cols],
                                        ALU.mult).then_inc(norm_done, 1)

            def statistics(batch):
                wait(dve, xin_in, 16 * (batch + 1))
                for t in range(CT):
                    for half in range(2):
                        last = nc.vector.bn_stats(BN6[:, t, half, :], XIN[:, t, HALF * half:HALF * half + HALF])
                link(last, alone=True)
                link(nc.vector.bn_aggr(MV[:, 0, :], BN6[:, 0]), alone=True)
                link(nc.vector.bn_aggr(MV[:, 1, :], BN6[:, 1]))
                dve.sem_inc(gn_ready, 1)

            def group_stats(k, batch):
                src = bank()
                if k == 0:
                    nc.vector.tensor_copy(MG[:, :], src[:, 0:CT]).then_inc(ring_free, 1)
                    own()
                    link(nc.vector.tensor_tensor(DEV[:, :], MV[:, :, 0], MG[:, :], ALU.subtract))
                    link(nc.vector.tensor_tensor(S2[:, :], DEV[:, :], DEV[:, :], ALU.mult))
                    link(nc.vector.tensor_tensor(S2[:, :], S2[:, :], MV[:, :, 1], ALU.add))
                    dve.sem_inc(gn_ready, 1)
                else:
                    nc.vector.tensor_scalar(VE[:, :], src[:, 0:CT], EPS, None, ALU.add).then_inc(ring_free, 1)
                    own()
                    dve.sem_inc(var_ready, 1)

            def residual(o, half, batch, bias):
                src = bank()
                cols = slice(HALF * half, HALF * half + HALF)
                if o == 0 and half == 0:
                    wait(dve, xres_in, 16 * (batch + 1))
                nc.vector.scalar_tensor_tensor(out=XRES[:, o, cols], in0=src, scalar=bias[:, o:o + 1],
                                               in1=XRES[:, o, cols], op0=ALU.add,
                                               op1=ALU.add).then_inc(ring_free, 1)
                if o == CT - 1 and half == 1:
                    own()
                    dve.sem_inc(y_ready, 1)

            def window(u, par, jobs, i, trail=True):
                def run(todo):
                    for job in todo:
                        if job[0] == "max":
                            row_max(u + 1, 1 - par, *job[1:])
                        elif job[0] == "v" and i is None:
                            keep_v(1, 1, job[1], ZB[:, :])
                        elif job[0] == "v":
                            keep_v(u + 1, 1 - par, job[1], BV[:, P * (1 - par):P * (1 - par) + P])
                        elif job[0] == "qk":
                            split_qk(BQK[:, par, job[1]:job[1] + 1], *job[1:], u + 2, job[1:] == (1, 1))
                        elif job[0] == "stats":
                            statistics(i + 1)
                        elif job[0] == "gn":
                            group_stats(job[1], i + 1)
                        elif job[0] == "post":
                            residual(*job[1:], i - 1, BP)
                        else:
                            after(0, job)

                for s in range(STEPS):
                    run(jobs[s][0:3])
                    if par == 1 and i is None:
                        for part in range(NORM_PARTS if s == 1 else 0):
                            normalise(u - 1, 1 - par, 1, part)
                    elif 1 <= s <= NORM_PARTS and trail:
                        normalise(u - 1, 1 - par, 1, s - 1)
                    if MT + 1 <= s <= MT + NORM_PARTS:
                        normalise(u, par, 0, s - MT - 1)
                    run(jobs[s][3:])

            def reread(dst, src):
                link(nc.vector.transpose(dst.rearrange("p (a c) -> p a c", c=D),
                                         src.rearrange("p (l a) -> p a l", a=D)))
                dve.sem_inc(pe_ready, 1)

            def after(g, stage):
                what, half = stage[0], stage[-1]
                if what == "reread":
                    own()
                    if half == 0:
                        dve.wait_ge(norm_done, 2 * NORM_PARTS * (g + 1))
                    reread(LAT[g], LATC[g])
                elif what == "add":
                    for j in range(H):
                        for t in range(CT):
                            xs = X[:, H * g + j, t, HALF * half:HALF * half + HALF]
                            nc.vector.scalar_tensor_tensor(out=xs, in0=bank(),
                                                           scalar=GAM[:, stage[1]:stage[1] + 1], in1=xs,
                                                           op0=ALU.mult, op1=ALU.add).then_inc(ring_free, 1)
                elif what == "encode":
                    nc.vector.tensor_copy(ENC[:, :], bank()).then_inc(ring_free, 1)
                elif what == "concepts":
                    for n in range(4):
                        src = bank().rearrange("p (j q) -> p j q", q=P)
                        link(nc.vector.tensor_reduce(out=CM4[:, n, :], in_=src, op=ALU.max, axis=AX.X))
                        nc.vector.tensor_tensor(E[g][:, H * n:H * n + H, :], src,
                                                CM4[:, n, :].unsqueeze(2).broadcast_to([P, H, P]),
                                                ALU.subtract).then_inc(ring_free, 1)
                    own()
                    dve.sem_inc(cs_ready, 1)
                elif what == "softmax":
                    dve.wait_ge(act_done, acts.add())
                    link(nc.vector.tensor_reduce(out=CS[:, :], in_=E[g], op=ALU.add, axis=AX.X))
                    link(nc.vector.reciprocal(CR[:, :], CS[:, :]))
                    link(nc.vector.tensor_tensor(E[g], E[g], CR[:, :].unsqueeze(2).broadcast_to([P, 4 * H, P]),
                                                 ALU.mult))
                    dve.sem_inc(pe_ready, 1)
                elif what == "turn":
                    for n in range(4):
                        nc.vector.tensor_copy(PT[g][:, :, P * n:P * n + P],
                                              bank().rearrange("p (j q) -> p j q", q=P)).then_inc(ring_free, 1)
                elif what == "mix":
                    nc.vector.tensor_copy(LATC[g][:, HALF * half:HALF * half + HALF],
                                          bank()).then_inc(ring_free, 1)
                elif what == "classes":
                    for part in range(2):
                        cols = slice(HALF * part, HALF * part + HALF)
                        nc.vector.tensor_scalar(OM[g][:, cols], bank(), CB[:, :], None,
                                                ALU.add).then_inc(ring_free, 1)
                        own()
                        link(nc.vector.tensor_tensor(SQ[g][:, cols], OM[g][:, cols], OM[g][:, cols], ALU.mult))
                    dve.sem_inc(pe_ready, 1)
                elif what == "norms":
                    for part in range(2):
                        nc.vector.tensor_copy(NRM[g][:, HALF * part:HALF * part + HALF],
                                              bank()).then_inc(ring_free, 1)
                    own()
                    dve.sem_inc(cs_ready, 1)
                elif what == "pool":
                    dve.wait_ge(act_done, acts.add())
                    link(nc.vector.reciprocal(NRI[g], NRM[g]))
                    link(nc.vector.scalar_tensor_tensor(out=PRB[g], in0=OM[g], scalar=RW[:, :], in1=NRI[g],
                                                        op0=ALU.mult, op1=ALU.mult))
                    link(nc.vector.tensor_reduce(out=POOLED[:, :], in_=PRB[g], op=ALU.add, axis=AX.X))
                    link(nc.vector.tensor_scalar(PM[:, :], BMASK, POOLED[:, :], 1.0 / N, ALU.mult, ALU.mult))
                    dve.sem_inc(pe_ready, 1)
                elif what == "hidden":
                    nc.vector.tensor_scalar(HID[:, :], bank()[0:4 * K, 0:H], 0.0, None,
                                            ALU.max).then_inc(ring_free, 1)
                elif what == "gates":
                    nc.vector.tensor_copy(ZE[:, :], bank()[:, 0:1]).then_inc(ring_free, 1)
                    own()
                    dve.sem_inc(cs_ready, 1)
                elif what == "regate":
                    dve.wait_ge(act_done, acts.add())
                    link(nc.vector.tensor_tensor(RG[:, :], ZE[:, :], GAM[:, 2:3], ALU.mult))
                    for j in range(H):
                        last = nc.vector.tensor_scalar(CW4[g][:, j, :], CW[:, :], RG[:, :], BMASK[:, j:j + 1],
                                                       ALU.mult, ALU.mult)
                    link(last)
                    dve.sem_inc(pe_ready, 1)
                elif what == "write":
                    j = stage[1]
                    for t in range(CT):
                        for part in range(2):
                            xs = X[:, H * g + j, t, HALF * part:HALF * part + HALF]
                            nc.vector.tensor_tensor(xs, bank(), xs, ALU.add).then_inc(ring_free, 1)
                    if j == H - 1:
                        own()
                        dve.sem_inc(x_final, 1)

            def prepare(jobs):
                for job in jobs:
                    if job[0] == "stats":
                        statistics(0)
                    elif job[0] == "gn":
                        group_stats(job[1], 0)
                    elif job[0] == "qk":
                        if job[1:] == (0, 0, 0):
                            dve.wait_ge(wqk_in, 16)
                        split_qk(BQK[:, job[3], job[1]:job[1] + 1], job[1], job[2], 2 + job[3],
                                 job[1:3] == (1, 1))
                    elif job[0] == "v":
                        dve.wait_ge(wv_in, 16)
                        keep_v(2, 0, job[1], BV[:, 0:P])
                    elif job[0] == "max":
                        row_max(2, 0, *job[1:])

            nc.vector.memset(WO[:, :, :], 0.0)
            nc.vector.memset(CONT[:, :, :], 0.0)
            nc.vector.memset(CWT[:, :, :], 0.0)
            nc.vector.memset(L1T[:, :], 0.0)
            nc.vector.memset(L2T[:, :], 0.0)
            nc.vector.memset(CB[:, :], 0.0)
            nc.vector.memset(ZB[:, :], 0.0)
            nc.vector.memset(CW[:, :], 1.0)
            nc.vector.memset(ONES[:, :], 1.0)
            for par in range(2):
                link(nc.vector.memset(KS[par][3 * D:3 * D + 2, :, :].bitcast(f32), 1.0))
            dve.sem_inc(zeroed, 1)
            dve.wait_ge(w_in, 16 * (6 + 5 * H))
            nc.vector.tensor_scalar(WL0[:, :, :], WL0[:, :, :], float(C) ** -0.5, None, ALU.mult)
            nc.vector.tensor_scalar(WO[:, :, :], WO[:, :, :], float(D) ** -0.5, None, ALU.mult)
            link(nc.vector.tensor_tensor(CW3[:, :], CW[:, :], CW[:, :], ALU.mult))
            dve.sem_inc(scaled, 1)
            link(nc.vector.tensor_reduce(out=RW[:, :], in_=CW3[:, :], op=ALU.add, axis=AX.X))
            dve.sem_inc(cs_ready, 1)
            dve.wait_ge(act_done, acts.add())
            link(nc.vector.reciprocal(RW[:, :], RWS[:, :]))
            for which in range(2):
                for half in range(2):
                    split_qk(ZB[:, 0:1], which, half, 0, (which, half) == (1, 1))
            for part in range(2):
                keep_v(0, 0, part, ZB[:, :])
            for h in range(H):
                for t in range(MT):
                    for half in range(2):
                        row_max(0, 0, h, t, half)
            for which in range(2):
                for half in range(2):
                    split_qk(ZB[:, 0:1], which, half, 1, (which, half) == (1, 1))
            window(0, 0, window_jobs(), None, trail=False)
            window(1, 1, after_jobs(), None)
            for part in range(NORM_PARTS):
                normalise(1, 1, 1, part)
            between, rest = first_jobs()
            for stage in AFTER:
                after(1, stage)
                prepare(between.get(stage, ()))
            prepare(rest)
            window(2, 0, window_jobs(prep=True, gn=True), 0, trail=False)
            window(3, 1, window_jobs(prep=True), 0)
            dve.wait_ge(wp_in, 16)
            with dve.Fori(1, B - 1) as i:
                ring.enter(i - 1, RING_PER)
                steps.enter(i - 1, 8 + 16 + 4 * NORM_PARTS + 6)
                iteration(i, window, None)
                ring.leave(TURNS)
                steps.leave(TURNS)
            iteration(B - 1, window, None)
            for part in range(NORM_PARTS):
                normalise(2 * B + 1, 1, 1, part)
            for o in range(CT):
                for half in range(2):
                    residual(o, half, B - 1, BP)

            ring.restart(2)

            def step(ins):
                ins.then_inc(dve_step, 1)
                return steps.add()

            def scores3(n, t, prior):
                grid = [P, NHEAD, NHEAD, D]
                if n is not None:
                    S = S3[t % 2][:, :, :]
                    products = PQ.rearrange("p (h g d) -> p h g d", h=NHEAD, g=NHEAD)
                    wait(dve, copied3, 2 * n + 1)
                    nc.vector.tensor_tensor(
                        products,
                        ST[:, t % 2, C:2 * C].rearrange("p (g d) -> p g d", d=D).unsqueeze(1).broadcast_to(grid),
                        QC[t % 2].rearrange("p (h d) -> p h d", d=D).unsqueeze(2).broadcast_to(grid),
                        ALU.mult).then_inc(k_used3, 1)
                if prior is not None:
                    E3 = S3[(t - 1) % 2][:, :, :]
                    wait(dve, e_done3, prior + 1)
                    summed = step(nc.vector.tensor_reduce(out=R3[:, 0, :], in_=E3, op=ALU.add, axis=AX.X))
                if n is not None:
                    wait(dve, k_used3, n + 1)
                    wait(dve, pv_done3, n - 1)
                    scored = step(nc.vector.tensor_reduce(out=S, in_=products, op=ALU.add, axis=AX.X))
                if prior is not None:
                    wait(dve, dve_step, summed)
                    inverted = step(nc.vector.reciprocal(R3[:, 1, :], R3[:, 0, :]))
                if n is not None:
                    wait(dve, dve_step, scored)
                    largest = step(nc.vector.tensor_reduce(out=M3[:, :], in_=S, op=ALU.max, axis=AX.X))
                if prior is not None:
                    wait(dve, dve_step, inverted)
                    nc.vector.tensor_tensor(E3, E3, R3[:, 1, :].unsqueeze(2).broadcast_to([P, NHEAD, NHEAD]),
                                            ALU.mult).then_inc(p_ready3, 1)
                if n is not None:
                    wait(dve, dve_step, largest)
                    nc.vector.tensor_tensor(S, S, M3[:, :].unsqueeze(2).broadcast_to([P, NHEAD, NHEAD]),
                                            ALU.subtract).then_inc(s_ready3, 1)

            def outputs3(n, at):
                wait(dve, pv_done3, n + 1)
                wait(dve, tr_done3, n - 1)
                nc.vector.tensor_reduce(out=O3[at % 2],
                                        in_=PV[at % 2].rearrange("p (c g) -> p c g", g=NHEAD),
                                        op=ALU.add, axis=AX.X).then_inc(o_ready3, 1)

            def slot(b, t):
                n = MT * b + t
                first, last = isinstance(b, int) and b == 0, isinstance(b, int) and b == B - 1
                scores3(n, t, None if first and t < 1 else n - 1)
                if not (first and t < 2):
                    outputs3(n - 2, (t - 2) % MT)
                if t == 3 and not first:
                    for o in range(CT):
                        residual(o, 1, B + b - 1, BP3)
                if t == 7:
                    for o in range(CT):
                        residual(o, 0, B + b, BP3)
                if t == 4 and not last:
                    statistics(B + b + 1)
                if t in (5, 6) and not last:
                    group_stats(t - 5, B + b + 1)

            dve.wait_ge(w3_in, 16 * 3)
            link(nc.vector.tensor_scalar(B3N, B3, -1.0, None, ALU.mult))
            link(nc.vector.scalar_tensor_tensor(out=B3S, in0=B3N.bitcast(f32),
                                                scalar=IDENT[TWO, 3 * D + 1:3 * D + 2],
                                                in1=B3, op0=ALU.mult, op1=ALU.add))
            dve.sem_inc(pe_ready, 1)
            statistics(B)
            for k in range(2):
                group_stats(k, B)
            tile_slots(0, slot)
            with dve.Fori(1, B - 1) as b:
                ring.enter(b - 1, 6)
                steps.enter(b - 1, 16 + 16 + 6)
                tile_slots(b, slot)
                ring.leave(TURNS)
                steps.leave(TURNS)
            tile_slots(B - 1, slot)
            scores3(None, MT, MT * B - 1)
            for n in range(MT * B - 2, MT * B):
                outputs3(n, n % MT)
            for o in range(CT):
                residual(o, 1, 2 * B - 1, BP3)


def kernel(**inputs):
    import numpy as np
    import concourse.bacc as bacc
    from concourse.bass_utils import run_bass_kernel_spmd

    a = {k: np.asarray(v) for k, v in inputs.items()}

    def column(v):
        return v.reshape(CT, P).T

    def rows(w):
        return w.T.reshape(CT, P, C).transpose(1, 0, 2)

    def packs(wq, wk, wv, wp, bq, bk, bv, bp, scale, bias):
        qk = np.stack([rows(wq).reshape(P, CT, 2, P), rows(wk).reshape(P, CT, 2, P)], axis=3)
        bqk = np.stack([column(bq), column(bk)], axis=2)
        return (np.concatenate([qk.reshape(P, -1), bqk.reshape(P, -1), column(scale), column(bias)], axis=1),
                np.concatenate([rows(wv).reshape(P, -1), np.broadcast_to(bv[None], (P, C))], axis=1),
                np.concatenate([rows(wp).reshape(P, -1), column(bp)], axis=1))

    w2 = a["L2_conv_w_qkv"].reshape(C // D, 3, D, C)
    b2 = a["L2_conv_b_qkv"].reshape(C // D, 3, D)
    p2 = packs(*(w2[:, n].reshape(C, C) for n in range(3)), a["L2_conv_w_proj"],
               *(b2[:, n].reshape(C) for n in range(3)), a["L2_conv_b_proj"],
               a["L2_conv_gn_scale"], a["L2_conv_gn_bias"])
    eye = np.eye(P)
    block = np.kron(np.eye(H), np.ones((D, D)))
    consts = np.concatenate([eye, np.kron(np.eye(P // 8), np.full((8, 8), 0.125)), block, block[:, ::D]],
                            axis=1).astype(np.float32)
    arrays = {
        "x": a["x"].reshape(B, C, N),
        "w_l0": np.concatenate([a["L0_conv_w_theta"], a["L0_conv_w_phi"], a["L0_conv_w_g"]], axis=0).T,
        "w_o": a["L0_conv_w_o"].T,
        "concepts": a["L0_conv_concepts"],
        "concepts_t": a["L0_conv_concepts"].T,
        "gammas": np.concatenate([a["L0_conv_gamma_sa"].reshape(1, 1), a["L0_conv_gamma_moca"].reshape(1, 1),
                                  a["L1_conv_gamma"].reshape(1, 1)], axis=1),
        "conv_w": a["L1_conv_conv_w"],
        "conv_wt": a["L1_conv_conv_w"].T,
        "conv_b": a["L1_conv_conv_b"].reshape(K, 1),
        "lin1_t": a["L1_conv_lin1_w"].T,
        "lin2_t": a["L1_conv_lin2_w"].T,
        "qk_pack": p2[0],
        "v_pack": p2[1],
        "p_pack": p2[2],
        "w3_pack": a["L3_conv_qkv_w"].T.reshape(CT, P, 3 * C).transpose(1, 0, 2).reshape(P, -1),
        "b3_row": a["L3_conv_qkv_b"].reshape(1, 3 * C),
        "p3_pack": np.concatenate([rows(a["L3_conv_proj_w"]).reshape(P, -1), column(a["L3_conv_proj_b"]),
                                   column(a["L3_conv_norm_w"]), column(a["L3_conv_norm_b"])], axis=1),
        "consts": consts,
    }
    nc = bacc.Bacc("TRN2", target_bir_lowering=False, num_devices=1)
    args, fed = [], {}
    for name, v in arrays.items():
        v = np.ascontiguousarray(v)
        fed[f"in_{name}"] = v
        args.append(nc.dram_tensor(f"in_{name}", v.shape, mybir.dt.from_np(v.dtype), kind="ExternalInput").ap())
    args.append(nc.dram_tensor("out_y", (B, C, N), mybir.dt.float32, kind="ExternalOutput").ap())
    program(nc, *args)
    r = run_bass_kernel_spmd(nc, [fed], core_ids=[0])
    return r.results[0]["out_y"].reshape(B, C, 32, 32)
```

```python
from contextlib import ExitStack

import concourse.bass as bass
from concourse import mybir

B, C, N, P = 8, 256, 1024, 128
CT = C // P
HALF = 512
MT = N // P
D = 32
H = P // D
K = 10
STEPS = 2 * MT
EXPS = H * STEPS
BANKS = 3
POOL_TILES = (0, 1, 2, 4, 5)
POOL_SUMS = len(POOL_TILES) - 1
FIRST_SUMMED = 3
INVERT_AT = 2
SPREAD_AT = 5
NHEAD = C // D
EPS = 1e-5
QK_COLS = CT * 2 * 2 * P
V_COLS = CT * C
P_COLS = CT * C
W3_COLS = CT * 3 * C


class Tally:

    def __init__(self, banks=BANKS):
        self.base, self.k, self.banks = 0, 0, banks

    def add(self, n=1):
        self.k += n
        return self.base + self.k

    def now(self):
        return self.base + self.k

    def slot(self):
        return (self.k - 1) % self.banks

    def restart(self, banks):
        self.base, self.k, self.banks = self.base + self.k, 0, banks

    def enter(self, turn, per):
        self.start, self.per = self.base + self.k, per
        self.base, self.k = self.start + turn * per, 0

    def leave(self, turns):
        assert self.k == self.per
        self.base, self.k = self.start + turns * self.per, 0


def wait(eng, sem, value):
    if isinstance(value, int) and value <= 0:
        return
    eng.wait_ge(sem, value)


def wait_apart(eng, sem, value, passed):
    if isinstance(value, int) and value <= 0:
        return
    eng.wait_ge(sem, value)
    if not isinstance(value, int):
        eng.sem_inc(passed, 1)


DVE_SHARE = {"v": 7, "post": 6, "stats": 25, "gn": 6, "qk": 15, "max": 6, "spread": 6}


def window_jobs(post=False, prep=False, nxt=True, gn=False, trail=True):
    jobs = [[] for _ in range(STEPS)]
    if trail:
        jobs[SPREAD_AT].append(("spread", -1))
    jobs[MT + SPREAD_AT].append(("spread", 0))
    if nxt:
        jobs[0].append(("v", 0))
        jobs[1].append(("v", 1))
    if gn:
        jobs[1].append(("stats",))
        jobs[3].append(("gn", 0))
        jobs[5].append(("gn", 1))
    if post:
        for n in range(4):
            jobs[6 + n // 2].append(("post", n // 2, n % 2))
    if prep:
        for n in range(4):
            jobs[9 + 2 * (n // 2) + n % 2].append(("qk", n // 2, n % 2))
    if nxt:
        tiles = [("max", h, t, half) for h in range(H) for t in range(MT) for half in range(2)]
        load = [sum(DVE_SHARE[j[0]] for j in step) for step in jobs]
        steps = range(1, STEPS)
        room = min(r for r in range(200)
                   if sum(max(0, r - load[s]) // DVE_SHARE["max"] for s in steps) >= len(tiles))
        for s in steps:
            n = max(0, room - load[s]) // DVE_SHARE["max"]
            jobs[s] += tiles[:n]
            tiles = tiles[n:]
        assert not tiles
    return jobs


AFTER = [("reread", 0), ("add", 0, 0), ("encode", 0), ("concepts", 0), ("add", 0, 1), ("softmax", 0),
         ("encode", 1), ("turn", 0), ("mix", 0), ("concepts", 1), ("softmax", 1), ("turn", 1), ("mix", 1)]
AFTER += [("reread", 1), ("add", 1, 0), ("add", 1, 1), ("classes",), ("norms",), ("pool",), ("hidden",),
          ("gates",), ("regate",)] + [("write", _j) for _j in range(H)]


START = []
for _h in range(H):
    START += [("max", _h, _t, _half) for _t in range(MT) for _half in range(2)]
    START += [[("v", 1)], [("qk", 0, 0)], [("qk", 0, 1), ("qk", 1, 0)], [("qk", 1, 1)]][_h]


def after_jobs():
    jobs = [[] for _ in range(STEPS)]
    jobs[2].append(("spread", -1))
    jobs[MT + SPREAD_AT].append(("spread", 0))
    for n, stage in enumerate(AFTER[:-H]):
        jobs[3 + n // 2].append(stage)
    return jobs


def first_jobs():
    maxima = [("max", h, t, half) for h in range(H) for t in range(MT) for half in range(2)]
    jobs = {("concepts", 1): [("stats",)], ("softmax", 1): [("gn", 0)], ("turn", 1): [("gn", 1)],
            ("add", 1, 0): [("qk", n // 2, n % 2, 0) for n in range(4)],
            ("add", 1, 1): [("v", 0), ("v", 1)]}
    for stage, n in ((("classes",), 4), (("norms",), 6), (("pool",), 2), (("hidden",), 3), (("gates",), 4),
                     (("regate",), 2), (("write", 0), 6), (("write", 1), 6), (("write", 2), 6),
                     (("write", 3), 6)):
        jobs[stage] = maxima[:n]
        maxima = maxima[n:]
    return jobs, maxima + [("qk", n // 2, n % 2, 1) for n in range(4)]


def program(nc, x, w_l0, w_o, concepts, concepts_t, gammas, conv_w, conv_wt, conv_b, lin1_t, lin2_t,
            qk_pack, v_pack, p_pack, w3_pack, b3_row, p3_pack, consts, out):
    f32, f32r = mybir.dt.float32, mybir.dt.float32r
    ALU, ACT, AX = mybir.AluOpType, mybir.ActivationFunctionType, mybir.AxisListType

    x_d = x.rearrange("b (t p) n -> b p t n", p=P)
    out_d = out.rearrange("b (t p) n -> b p t n", p=P)

    ctx = ExitStack()
    with ctx:
        def sb(name, shape, dt=f32):
            return ctx.enter_context(nc.sbuf_tensor(name, shape, dt))

        def sem(name):
            return ctx.enter_context(nc.semaphore(name))

        X = sb("X", [P, B, CT, N])
        QS = [sb(f"QS{i}", [3 * D + 2, H, N], f32r) for i in range(2)]
        KS = [sb(f"KS{i}", [3 * D + 2, H, N], f32r) for i in range(2)]
        HI = sb("HI", [P, 2, N], f32r)
        LO = sb("LO", [P, 2, N], f32r)
        VT = [sb(f"VT{i}", [P, MT, P]) for i in range(2)]
        PR = sb("PR", [P, 4, 2 * HALF])
        ACC = sb("ACC", [P, 2, 2 * HALF])
        OHU = [sb(f"OHU{i}", [P, 2, HALF]) for i in range(2)]
        OH = [[OHU[i][:, h, :] for h in range(2)] for i in range(2)]
        RC = sb("RC", [P, HALF])
        R16 = sb("R16", [P, HALF // D])
        MX = sb("MX", [P, H, MT, 2])
        NM = sb("NM", [P, H, MT])
        NMH = sb("NMH", [P, H, MT], f32r)
        NML = sb("NML", [P, H, MT], f32r)
        ONES = sb("ONES", [P, P])
        XIN, XRES, XN = X[:, 0], X[:, 1], X[:, 2]
        WREG = X[:, 3].rearrange("p t n -> p (t n)")
        WREG2 = X[:, 4].rearrange("p t n -> p (t n)")
        WREG3 = X[:, 6].rearrange("p t n -> p (t n)")
        WQK_ALL = WREG[:, 0:QK_COLS + 8]
        WQK = WQK_ALL[:, 0:QK_COLS].rearrange("p (t u w c) -> p t u w c", t=CT, u=2, w=2)
        BQK = WQK_ALL[:, QK_COLS:QK_COLS + 4].rearrange("p (u w) -> p u w", u=2)
        GNS = WQK_ALL[:, QK_COLS + 4:QK_COLS + 6]
        GNB = WQK_ALL[:, QK_COLS + 6:QK_COLS + 8]
        V_AT = QK_COLS + P
        WV_ALL = WREG[:, V_AT:V_AT + V_COLS + C]
        WV = WV_ALL[:, 0:V_COLS].rearrange("p (t c) -> p t c", t=CT)
        BV = WV_ALL[:, V_COLS:V_COLS + C]
        WP_ALL = WREG2[:, 0:P_COLS + CT]
        WP = WP_ALL[:, 0:P_COLS].rearrange("p (t c) -> p t c", t=CT)
        BP = WP_ALL[:, P_COLS:P_COLS + CT]
        P3_ALL = WREG2[:, 1024:1024 + P_COLS + 3 * CT]
        WP3 = P3_ALL[:, 0:P_COLS].rearrange("p (t c) -> p t c", t=CT)
        BP3 = P3_ALL[:, P_COLS:P_COLS + CT]
        GNS3 = P3_ALL[:, P_COLS + CT:P_COLS + 2 * CT]
        GNB3 = P3_ALL[:, P_COLS + 2 * CT:P_COLS + 3 * CT]
        W3_ALL = WREG3[:, 0:W3_COLS]
        W3 = W3_ALL.rearrange("p (t c) -> p t c", t=CT)
        TWO = slice(3 * D, 3 * D + 2)
        B3 = X[TWO, 7].rearrange("p t n -> p (t n)")[:, 0:3 * C]
        B3N = QS[0][TWO, 1, 0:3 * C]
        B3S = QS[0][TWO, 0, 0:3 * C]
        DEEP = [PR[:, n, :] for n in range(4)] + [X[:, b, n, :] for b in (5, 7) for n in range(2)]

        def exps(i, s, pair):
            return DEEP[(2 * s + pair) % (4 if i is None else 8)]

        PQ = X[:, 5].rearrange("p t n -> p (t n)")
        PV = [PR[:, 2 * n:2 * n + 2, :].rearrange("p a q -> p (a q)") for n in range(2)]
        QC = [HI[:, 0, C * n:C * n + C].bitcast(f32) for n in range(2)]
        VC = [HI[:, 1, C * n:C * n + C].bitcast(f32) for n in range(4)]
        S3 = [sb(f"S3{n}", [P, NHEAD, NHEAD]) for n in range(4)]
        M3 = sb("M3", [P, NHEAD])
        R3 = sb("R3", [P, 2, NHEAD])
        O3 = [LO[:, 1, C * n:C * n + C].bitcast(f32) for n in range(2)]
        OT = ACC[:, :, :]
        BN6 = sb("BN6", [P, CT, 2, 6])
        MV = sb("MV", [P, CT, 2])
        MG = sb("MG", [P, CT])
        DEV = sb("DEV", [P, CT])
        S2 = sb("S2", [P, CT])
        VE = sb("VE", [P, CT])
        RSTD = sb("RSTD", [P, CT])
        GA = sb("GA", [P, CT])
        GT = sb("GT", [P, CT])
        GB = sb("GB", [P, CT])
        MHALF = sb("MHALF", [P, CT])
        CST = sb("CST", [P, 4 * P + H])
        IDENT, GROUP, BLOCK, BMASK = (CST[:, 0:P], CST[:, P:2 * P], CST[:, 2 * P:3 * P], CST[:, 3 * P:3 * P + H])
        SPREAD = CST[:, 3 * P + H:4 * P + H]
        WL0 = sb("WL0", [P, CT, 3 * D])
        WO = sb("WO", [P, H, C])
        CON = sb("CON", [P, D])
        CONT = sb("CONT", [P, H, P])
        GAM = sb("GAM", [P, 3])
        CW = sb("CW", [P, C])
        CW3 = sb("CW3", [P, C])
        CWT = sb("CWT", [P, CT, D])
        CB = sb("CB", [P, 1])
        L1T = sb("L1T", [P, 4 * K])
        L2T = sb("L2T", [4 * K, D])
        ZB = sb("ZB", [P, P])
        RW = sb("RW", [P, 1])
        RWS = sb("RWS", [P, 1])
        WORK = [(HI.rearrange("p a n -> p (a n)").bitcast(f32), LO.rearrange("p a n -> p (a n)").bitcast(f32)),
                (PR[:, 0:2, :].rearrange("p a n -> p (a n)"), PR[:, 2:4, :].rearrange("p a n -> p (a n)"))]
        LATC = [OHU[g].rearrange("p h q -> p (h q)") for g in range(2)]
        LAT = [VT[g].rearrange("p t c -> p (t c)") for g in range(2)]
        ENC = sb("ENC", [P, HALF])
        E = [WORK[g][0].rearrange("p (j q) -> p j q", q=P) for g in range(2)]
        PT = [WORK[g][1].rearrange("p (j q) -> p j q", q=HALF) for g in range(2)]
        OM = [WORK[g][0][:, 0:N] for g in range(2)]
        SQ = [WORK[g][0][:, N:2 * N] for g in range(2)]
        NRM = [WORK[g][1][:, 0:N] for g in range(2)]
        NRI = [WORK[g][1][:, N:2 * N] for g in range(2)]
        PRB = LAT
        CW4 = [LATC[g].rearrange("p (j c) -> p j c", j=H) for g in range(2)]
        CM4 = sb("CM4", [P, 4, H])
        CS = sb("CS", [P, 4 * H])
        CR = sb("CR", [P, 4 * H])
        POOLED = sb("POOLED", [P, 1])
        PM = sb("PM", [P, H])
        HID = sb("HID", [4 * K, H])
        ZE = sb("ZE", [P, 1])
        RG = sb("RG", [P, 1])

        ST = ctx.enter_context(nc.psum_tensor("ST", [P, BANKS, HALF], f32))
        RING = ctx.enter_context(nc.psum_tensor("RING", [P, BANKS, HALF], f32))
        AV = ctx.enter_context(nc.psum_tensor("AV", [P, HALF], f32))
        SUM = ctx.enter_context(nc.psum_tensor("SUM", [P, HALF], f32))

        V3 = [ST[:, 2, 0:C], RING[:, 2, 0:C]]

        x_in = [sem(f"x_in{b}") for b in range(2)]
        w_first = sem("w_first")
        cst_in = sem("cst_in")
        w_in = sem("w_in")
        zeroed = sem("zeroed")
        scaled = sem("scaled")
        ring_full = sem("ring_full")
        ring_free = sem("ring_free")
        dve_step = sem("dve_step")
        stage_ready = sem("stage_ready")
        stk = [sem(f"stk{h}") for h in range(H)]
        v_ready = sem("v_ready")
        negmax_ready = sem("negmax_ready")
        rows_in = [sem(f"rows_in{h}") for h in range(H)]
        st_full = sem("st_full")
        exp_done = sem("exp_done")
        pool_used = sem("pool_used")
        av_done = sem("av_done")
        half_done = sem("half_done")
        half_kept = sem("half_kept")
        sums_in = sem("sums_in")
        inverted = sem("inverted")
        inverse_in = sem("inverse_in")
        norm_done = sem("norm_done")
        cs_ready = sem("cs_ready")
        act_done = sem("act_done")
        pe_ready = sem("pe_ready")
        x_final = sem("x_final")
        x_out = sem("x_out")
        xin_in = sem("xin_in")
        xres_in = sem("xres_in")
        wqk_in = sem("wqk_in")
        wv_in = sem("wv_in")
        wp_in = sem("wp_in")
        gn_ready = sem("gn_ready")
        var_ready = sem("var_ready")
        pool_gn = sem("pool_gn")
        xn_ready = sem("xn_ready")
        y_ready = sem("y_ready")
        passed = sem("passed")
        y_out = sem("y_out")

        w3_in = sem("w3_in")
        qkv3 = sem("qkv3")
        copied3 = sem("copied3")
        k_used3 = sem("k_used3")
        s_ready3 = sem("s_ready3")
        e_done3 = sem("e_done3")
        p_ready3 = sem("p_ready3")
        pv_done3 = sem("pv_done3")
        o_ready3 = sem("o_ready3")
        tr_done3 = sem("tr_done3")
        ot_done3 = sem("ot_done3")

        block = ctx.enter_context(nc.Block())

        def iteration(i, window, tallies, turns=None):
            u = 2 * i + 2
            last = isinstance(i, int) and i == B - 1
            first = isinstance(i, int) and i == 0
            window(u, 0, window_jobs(post=not first, prep=not last, gn=not last), i)
            window(u + 1, 1, window_jobs(prep=not last, nxt=not last, gn=last), i)

        RING_PER = 2 + 2 + 4 + 2 + 4 + 64 + 2 + 2 + 4 + 64
        TURNS = B - 2

        def tile_slots(b, slot):
            for t in range(MT):
                slot(b, t)

        @block.sync
        def _(sp):
            def load(dst, src, s):
                sp.dma_start(dst, src).then_inc(s, 16)

            def stacks(u, par):
                wait_apart(sp, stage_ready, u + 1, passed)
                wait(sp, st_full, EXPS * (u - 1))
                for h in range(H):
                    rows = slice(D * h, D * h + D)
                    for j, (q, k) in enumerate(((HI, HI), (LO, HI), (HI, LO))):
                        load(QS[par][D * j:D * j + D, h, :].bitcast(f32), q[rows, 0, :].bitcast(f32), stk[h])
                        load(KS[par][D * j:D * j + D, h, :].bitcast(f32), k[rows, 1, :].bitcast(f32), stk[h])

            def rows(u, par):
                for h in range(H):
                    wait(sp, negmax_ready, H * u + h + 1)
                    for r, src in ((3 * D, NMH), (3 * D + 1, NML)):
                        load(QS[par][r:r + 1, h, :].rearrange("o (p t) -> o p t", t=MT).bitcast(f32),
                             src[:, h, :].bitcast(f32), rows_in[h])

            load(WL0[:, :, :], w_l0.rearrange("(t p) o -> p t o", p=P), w_first)
            for b in range(H):
                load(X[:, b], x_d[b], x_in[0])
            load(CST[:, :], consts, cst_in)
            load(GAM[:, :], gammas.broadcast_to([P, 3]), w_in)
            load(CON[:, :], concepts, w_in)
            sp.wait_ge(zeroed, 1)
            load(CWT[:, :, 0:K], conv_wt.rearrange("(t p) o -> p t o", p=P), w_in)
            load(L2T[:, 0:K], lin2_t, w_in)
            for j in range(H):
                load(WO[D * j:D * j + D, j, :], w_o, w_in)
                load(CONT[D * j:D * j + D, j, :], concepts_t, w_in)
                load(CW[D * j:D * j + K, :], conv_w, w_in)
                load(CB[D * j:D * j + K, :], conv_b, w_in)
                load(L1T[D * j:D * j + K, :], lin1_t, w_in)
            stacks(0, 0)
            for b in range(H, B):
                load(X[:, b], x_d[b], x_in[1])
            rows(0, 0)
            stacks(1, 1)
            rows(1, 1)
            for g in range(2):
                sp.wait_ge(x_final, g + 1)
                for b in range(H * g, H * g + H):
                    load(out_d[b], X[:, b], x_out)
                if g == 0:
                    sp.wait_ge(x_out, 16 * H)
                    load(XIN, out_d[0], xin_in)
                    load(WQK_ALL, qk_pack, wqk_in)
                    load(WV_ALL, v_pack, wv_in)
                    stacks(2, 0)
            rows(2, 0)

            def sp_iteration(i):
                u = 2 * i + 2
                first, last = isinstance(i, int) and i == 0, isinstance(i, int) and i == B - 1
                wait_apart(sp, xn_ready, CT * (i + 1), passed)
                load(XIN, out_d[(i + 1) % B] if isinstance(i, int) else out_d[bass.ds(i + 1, 1)][0], xin_in)
                stacks(u + 1, 1)
                if first:
                    sp.wait_ge(x_out, 16 * B)
                    load(WP_ALL, p_pack, wp_in)
                    load(P3_ALL, p3_pack, w3_in)
                    load(W3_ALL, w3_pack, w3_in)
                if not first:
                    wait_apart(sp, y_ready, i, passed)
                    load(out_d[i - 1] if isinstance(i, int) else out_d[bass.ds(i - 1, 1)][0], XRES, y_out)
                rows(u + 1, 1)
                if not last:
                    stacks(u + 2, 0)
                wait_apart(sp, y_out, 16 * i, passed)
                load(XRES, out_d[i] if isinstance(i, int) else out_d[bass.ds(i, 1)][0], xres_in)
                if not last:
                    rows(u + 2, 0)

            sp_iteration(0)
            with sp.Fori(1, B - 1) as i:
                sp_iteration(i)
            sp_iteration(B - 1)
            sp.wait_ge(half_done, 2 * (2 * B + 2))
            load(B3, b3_row.broadcast_to([2, 3 * C]), w3_in)
            sp.wait_ge(y_ready, B)
            load(out_d[B - 1], XRES, y_out)
            sp.wait_ge(y_out, 16 * B)
            load(XRES, out_d[0], xres_in)

            def sp_batch(b):
                wait_apart(sp, xn_ready, CT * (B + b + 1), passed)
                load(XIN, out_d[b + 1] if isinstance(b, int) else out_d[bass.ds(b + 1, 1)][0], xin_in)

            def sp_store(b):
                wait_apart(sp, y_ready, B + b + 1, passed)
                load(out_d[b] if isinstance(b, int) else out_d[bass.ds(b, 1)][0], XRES, y_out)
                wait_apart(sp, y_out, 16 * (B + b + 1), passed)
                load(XRES, out_d[b + 1] if isinstance(b, int) else out_d[bass.ds(b + 1, 1)][0], xres_in)

            sp_batch(0)
            with sp.Fori(1, B - 1) as b:
                sp_batch(b)
                sp_store(b - 1)
            sp_store(B - 2)
            sp.wait_ge(y_ready, 2 * B)
            load(out_d[B - 1], XRES, y_out)
            sp.wait_ge(y_out, 16 * 2 * B)

        @block.tensor
        def _(pe):
            ring = Tally()
            pe_need = Tally()
            mm = nc.tensor.matmul

            def bank():
                wait(pe, ring_free, ring.add() - ring.banks)
                return RING[:, ring.slot(), :]

            def all_read():
                wait(pe, ring_free, ring.now())

            def qk_l0(g, which, half):
                dst = bank()
                for t in range(CT):
                    for j in range(H):
                        last = mm(dst[D * j:D * j + D, :], WL0[:, t, D * which:D * which + D],
                                  X[:, H * g + j, t, HALF * half:HALF * half + HALF],
                                  start=(t == 0), stop=(t == CT - 1))
                last.then_inc(ring_full, 1)

            def v_l0(g, part):
                qk_l0(g, 2, part)
                all_read()
                dst = bank()
                for m in range(4):
                    last = nc.tensor.transpose(dst[:, P * m:P * m + P], ENC[:, P * m:P * m + P], IDENT)
                last.then_inc(ring_full, 1)

            def max_scores(u, par, h, t, half):
                if t == 0 and half == 0:
                    wait(pe, stk[h], 96 * (u + 1))
                mm(bank(), QS[par][0:3 * D, h, t:N:MT], KS[par][0:3 * D, h, HALF * half:HALF * half + HALF],
                   start=True, stop=True).then_inc(ring_full, 1)

            def scores(u, par, s, heads):
                half, mt = s // MT, s % MT
                for h in heads:
                    if s == 0:
                        wait(pe, rows_in[h], 2 * 16 * (u + 1))
                    if s == 0 and h == 0:
                        wait(pe, exp_done, EXPS * u)
                    else:
                        wait(pe, exp_done, EXPS * u + H * s + h + 1 - BANKS)
                    mm(ST[:, (H * s + h) % BANKS, :], KS[par][:, h, P * mt:P * mt + P],
                       QS[par][:, h, HALF * half:HALF * half + HALF],
                       start=True, stop=True).then_inc(st_full, 1)

            def values(u, par, s, i):
                half, mt = s // MT, s % MT
                if mt == 0:
                    wait(pe, half_kept, 2 * (2 * u + half))
                    wait(pe, v_ready, 2 * (u + 1))
                wait(pe, exp_done, EXPS * u + H * s + H)
                for h in range(H):
                    last = mm(AV[D * h:D * h + D, :], VT[par][:, mt, D * h:D * h + D],
                              exps(i, s, h // 2)[:, HALF * (h % 2):HALF * (h % 2) + HALF],
                              start=(mt == 0), stop=(mt == MT - 1))
                if mt in POOL_TILES:
                    last.then_inc(av_done, 1)

            def sums(u, s, i):
                half, mt = s // MT, s % MT
                if mt not in POOL_TILES:
                    for h in range(H):
                        last = mm(SUM[D * h:D * h + D, :], ONES[:, 0:D],
                                  exps(i, s, h // 2)[:, HALF * (h % 2):HALF * (h % 2) + HALF],
                                  start=(mt == FIRST_SUMMED), stop=False)
                    last.then_inc(av_done, 1)
                if mt == MT - 1:
                    wait(pe, pool_used, 2 * POOL_SUMS * (2 * u + half + 1))
                    for h in range(H):
                        last = mm(SUM[D * h:D * h + D, :], ONES[:, 0:D],
                                  ACC[:, h // 2, HALF * (h % 2):HALF * (h % 2) + HALF], start=False, stop=True)
                    last.then_inc(half_done, 1)

            def v_product(u, part, batch, unit):
                dst = bank()
                if part == 0:
                    pe.wait_ge(wv_in, 16)
                for m in range(4):
                    mt = 4 * part + m
                    for t in range(CT):
                        last = mm(dst[:, P * m:P * m + P], XN[:, t, P * mt:P * mt + P],
                                  WV[:, t, P * unit:P * unit + P], start=(t == 0), stop=(t == CT - 1))
                last.then_inc(ring_full, 1)

            def qk_product(which, half, batch, unit):
                dst = bank()
                if which == 0 and half == 0:
                    pe.wait_ge(wqk_in, 16)
                    wait(pe, xn_ready, CT * (batch + 1))
                for t in range(CT):
                    last = mm(dst, WQK[:, t, unit, which, :], XN[:, t, HALF * half:HALF * half + HALF],
                              start=(t == 0), stop=(t == CT - 1))
                last.then_inc(ring_full, 1)

            def group_sums(k, batch):
                dst = bank()
                wait(pe, gn_ready, 2 * batch + k + 1)
                mm(dst[:, 0:CT], GROUP, MV[:, :, 0] if k == 0 else S2[:, :],
                   start=True, stop=True).then_inc(ring_full, 1)

            def output_product(o, half, batch):
                dst = bank()
                if o == 0 and half == 0:
                    pe.wait_ge(wp_in, 16)
                    wait(pe, norm_done, 2 * (2 * batch + 4))
                for t in range(CT):
                    last = mm(dst, WP[:, t, P * o:P * o + P], OH[t][half],
                              start=(t == 0), stop=(t == CT - 1))
                last.then_inc(ring_full, 1)

            def spread(n):
                wait(pe, inverse_in, 16 * (n + 1))
                mm(bank(), SPREAD, RC[:, :], start=True, stop=True).then_inc(ring_full, 1)

            def window(u, par, jobs, i, trail=True):
                def run(todo):
                    for job in todo:
                        if job[0] == "spread":
                            spread(2 * u + job[1])
                        elif job[0] == "max":
                            max_scores(u + 1, 1 - par, *job[1:])
                        elif job[0] == "v" and i is None:
                            v_l0(1, job[1])
                        elif job[0] == "v":
                            v_product(u + 1, job[1], i + par, 1 - par)
                        elif job[0] == "qk":
                            qk_product(*job[1:], i + 1, par)
                        elif job[0] == "gn":
                            group_sums(job[1], i + 1)
                        elif job[0] == "post":
                            output_product(*job[1:], i - 1)
                        else:
                            after(0, job)

                for s in range(STEPS):
                    scores(u, par, s, (0,))
                    run(jobs[s][0:1])
                    scores(u, par, s, (1, 2))
                    run(jobs[s][1:3])
                    if s:
                        values(u, par, s - 1, i)
                    elif trail:
                        values(u - 1, 1 - par, STEPS - 1, i)
                    run(jobs[s][3:4])
                    scores(u, par, s, (3,))
                    run(jobs[s][4:5])
                    if s:
                        sums(u, s - 1, i)
                    elif trail:
                        sums(u - 1, STEPS - 1, i)
                    run(jobs[s][5:])

            def after(g, stage):
                what, half = stage[0], stage[-1]
                if what == "add":
                    src = LAT[g]
                    if stage[1] == 0 or half == 0:
                        all_read()
                    if half == 0:
                        pe.wait_ge(pe_ready, pe_need.add())
                    for j in range(H):
                        for t in range(CT):
                            mm(bank(), WO[:, j, P * t:P * t + P], src[:, HALF * half:HALF * half + HALF],
                               start=True, stop=True).then_inc(ring_full, 1)
                elif what == "encode":
                    all_read()
                    qk_l0(g, 0, half)
                elif what == "concepts":
                    all_read()
                    for n in range(4):
                        mm(bank(), ENC[:, P * n:P * n + P], CONT[:, :, :].rearrange("p j q -> p (j q)"),
                           start=True, stop=True).then_inc(ring_full, 1)
                elif what == "turn":
                    pe.wait_ge(pe_ready, pe_need.add())
                    for n in range(4):
                        dst = bank()
                        for j in range(H):
                            last = nc.tensor.transpose(dst[:, P * j:P * j + P], E[g][:, H * n + j, :], IDENT)
                        last.then_inc(ring_full, 1)
                elif what == "mix":
                    all_read()
                    dst = bank()
                    for j in range(H):
                        last = mm(dst[D * j:D * j + D, :], CON[:, :], PT[g][:, j, :], start=True, stop=True)
                    last.then_inc(ring_full, 1)
                elif what == "classes":
                    all_read()
                    for part in range(2):
                        cols = slice(HALF * part, HALF * part + HALF)
                        dst = bank()
                        for t in range(CT):
                            for j in range(H):
                                last = mm(dst[D * j:D * j + D, :], CWT[:, t, :], X[:, H * g + j, t, cols],
                                          start=(t == 0), stop=(t == CT - 1))
                        last.then_inc(ring_full, 1)
                elif what == "norms":
                    pe.wait_ge(pe_ready, pe_need.add())
                    for part in range(2):
                        mm(bank(), BLOCK, SQ[g][:, HALF * part:HALF * part + HALF],
                           start=True, stop=True).then_inc(ring_full, 1)
                elif what == "hidden":
                    pe.wait_ge(pe_ready, pe_need.add())
                    mm(bank()[0:4 * K, 0:H], L1T[:, :], PM[:, :], start=True, stop=True).then_inc(ring_full, 1)
                elif what == "gates":
                    all_read()
                    dst = bank()
                    for j in range(H):
                        last = mm(dst[D * j:D * j + D, 0:1], L2T[:, :], HID[:, j:j + 1],
                                  start=True, stop=True)
                    last.then_inc(ring_full, 1)
                elif what == "write":
                    j = stage[1]
                    if j == 0:
                        pe.wait_ge(pe_ready, pe_need.add())
                    for t in range(CT):
                        for part in range(2):
                            mm(bank(), CW4[g][:, j, P * t:P * t + P],
                               PRB[g][:, HALF * part:HALF * part + HALF],
                               start=True, stop=True).then_inc(ring_full, 1)

            def prepare(jobs):
                for job in jobs:
                    if job[0] == "gn":
                        group_sums(job[1], 0)
                    elif job[0] == "qk":
                        qk_product(job[1], job[2], 0, job[3])
                    elif job[0] == "v":
                        v_product(2, job[1], 0, 0)
                    elif job[0] == "max":
                        max_scores(2, 0, *job[1:])

            pe.wait_ge(scaled, 1)
            pe.wait_ge(cst_in, 16)
            pe.wait_ge(x_in[0], 16 * H)
            for which in range(2):
                for half in range(2):
                    qk_l0(0, which, half)
            v_l0(0, 0)
            for job in START:
                if job[0] == "v":
                    v_l0(0, 1)
                elif job[0] == "qk":
                    if job[1:] == (0, 0):
                        pe.wait_ge(x_in[1], 16 * H)
                    qk_l0(1, job[1], job[2])
                else:
                    max_scores(0, 0, *job[1:])
            window(0, 0, window_jobs(trail=False), None, trail=False)
            window(1, 1, after_jobs(), None)
            values(1, 1, STEPS - 1, None)
            sums(1, STEPS - 1, None)
            for stage in AFTER[-H:]:
                after(0, stage)
            spread(3)
            between, rest = first_jobs()
            for stage in AFTER:
                after(1, stage)
                prepare(between.get(stage, ()))
            prepare(rest)
            window(2, 0, window_jobs(prep=True, gn=True, trail=False), 0, trail=False)
            window(3, 1, window_jobs(prep=True), 0)
            with pe.Fori(1, B - 1) as i:
                ring.enter(i - 1, RING_PER)
                all_read()
                iteration(i, window, None)
                ring.leave(TURNS)
            all_read()
            iteration(B - 1, window, None)
            values(2 * B + 1, 1, STEPS - 1, B - 1)
            sums(2 * B + 1, STEPS - 1, B - 1)
            spread(2 * (2 * B + 1) + 1)
            for o in range(CT):
                for half in range(2):
                    output_product(o, half, B - 1)

            def project3(half):
                for o in range(CT):
                    dst = bank()
                    for t in range(CT):
                        last = mm(dst, WP3[:, t, P * o:P * o + P], OT[:, t, HALF * half:HALF * half + HALF],
                                  start=(t == 0), stop=(t == CT - 1))
                    last.then_inc(ring_full, 1)

            def transpose3(n):
                wait(pe, o_ready3, n + 1)
                wait(pe, ot_done3, n - 1)
                at = n if isinstance(n, int) else tile_at[0]
                dst, src = (AV, SUM)[at % 2], O3[at % 2]
                for t in range(CT):
                    last = nc.tensor.transpose(dst[:, P * t:P * t + P], src[:, P * t:P * t + P], IDENT)
                last.then_inc(tr_done3, 1)

            tile_at = [0]

            def slot(b, t):
                n = MT * b + t
                first = isinstance(b, int) and b == 0
                if t == 0:
                    wait(pe, xn_ready, CT * (B + b + 1))
                wait(pe, copied3, 2 * (n - 1))
                wait(pe, k_used3, n - 1)
                for c0, c1, dst in ((0, 2 * C, ST[:, t % 2, :]), (2 * C, 3 * C, V3[t % 2])):
                    for ct in range(CT):
                        mm(dst, XN[:, ct, P * t:P * t + P], W3[:, ct, c0:c1], start=(ct == 0), stop=False)
                    last = mm(dst, KS[0][TWO, 0, 0:P], B3S[:, c0:c1], start=False, stop=True)
                last.then_inc(qkv3, 1)
                if not (first and t < 4) and t % 4 == 3:
                    wait(pe, ot_done3, n - 3)
                    project3((t // 4 + 1) % 2)
                if not (first and t < 3):
                    tile_at[0] = (t - 3) % MT
                    transpose3(n - 3)
                if t in (4, 5) and not (isinstance(b, int) and b == B - 1):
                    group_sums(t - 4, B + b + 1)

            all_read()
            ring.restart(2)
            pe.wait_ge(w3_in, 16 * 3)
            pe.wait_ge(pe_ready, pe_need.add())
            tile_slots(0, slot)
            with pe.Fori(1, B - 1) as b:
                ring.enter(b - 1, 6)
                tile_slots(b, slot)
                ring.leave(TURNS)
            tile_slots(B - 1, slot)
            for n in range(MT * B - 3, MT * B):
                transpose3(n)
            pe.wait_ge(ot_done3, MT * B)
            project3(1)

        @block.scalar
        def _(act):
            cs = Tally()

            def keep_half(u, par, half):
                wait(act, half_done, 2 * u + half + 1)
                wait(act, norm_done, 2 * u + half)
                nc.scalar.activation(RC[:, :], SUM[:, :], ACT.Copy).then_inc(half_kept, 1)
                nc.scalar.activation(OH[par][half], AV[:, :], ACT.Copy).then_inc(half_kept, 1)
                wait(act, half_kept, 2 * (2 * u + half) + 1)
                act.dma_start(R16[:, :],
                              RC[0:P:D, :].rearrange("h (p c) -> h p c", p=D)).then_inc(sums_in, 16)

            def return_inverse(n):
                wait(act, inverted, n + 1)
                act.dma_start(RC[0:P:D, :].rearrange("h (p c) -> h p c", p=D),
                              R16[:, :]).then_inc(inverse_in, 16)

            def window(u, par, jobs, i, trail=True):
                for s in range(STEPS):
                    for h in range(H):
                        pair, one = h // 2, h % 2
                        wait(act, st_full, EXPS * u + H * s + h + 1)
                        if one == 0:
                            prior = s - (2 if i is None else 4)
                            wait(act, av_done, STEPS * u + prior + 1)
                            if prior % MT in POOL_TILES:
                                wait(act, pool_used, 2 * POOL_SUMS * (2 * u + prior // MT)
                                     + 2 * max(POOL_TILES.index(prior % MT) - 1, 0) + pair + 1)
                        nc.scalar.activation(exps(i, s, pair)[:, HALF * one:HALF * one + HALF],
                                             ST[:, (H * s + h) % BANKS, :], ACT.Exp,
                                             scale=1.0 if i is None else float(D) ** -0.5
                                             ).then_inc(exp_done, 1)
                    if s == 0 and trail:
                        keep_half(u - 1, 1 - par, 1)
                    if s == MT:
                        keep_half(u, par, 0)
                    if s == (1 if par == 1 and i is None else INVERT_AT) and trail:
                        return_inverse(2 * u - 1)
                    if s == MT + INVERT_AT:
                        return_inverse(2 * u)
                    if par == 1 and i is None:
                        for stage in jobs[s]:
                            after(0, stage)

            def after(g, stage):
                if stage[0] == "concepts":
                    act.wait_ge(cs_ready, cs.add())
                    nc.scalar.activation(E[g], E[g], ACT.Exp).then_inc(act_done, 1)
                elif stage[0] == "norms":
                    act.wait_ge(cs_ready, cs.add())
                    nc.scalar.activation(NRM[g], NRM[g], ACT.Sqrt).then_inc(act_done, 1)
                elif stage[0] == "gates":
                    act.wait_ge(cs_ready, cs.add())
                    nc.scalar.activation(ZE[:, :], ZE[:, :], ACT.Sigmoid).then_inc(act_done, 1)

            def apply3(batch):
                wait(act, pool_gn, 4 * (batch + 1))
                for t in range(CT):
                    nc.scalar.activation(XN[:, t], XIN[:, t], ACT.Identity, bias=GB[:, t:t + 1],
                                         scale=GA[:, t:t + 1]).then_inc(xn_ready, 1)

            act.wait_ge(cs_ready, cs.add())
            nc.scalar.activation(RWS[:, :], RW[:, :], ACT.Sqrt).then_inc(act_done, 1)
            window(0, 0, None, None, trail=False)
            window(1, 1, after_jobs(), None)
            keep_half(1, 1, 1)
            return_inverse(3)
            for stage in AFTER:
                after(1, stage)
            window(2, 0, None, 0, trail=False)
            window(3, 1, None, 0)
            with act.Fori(1, B - 1) as i:
                iteration(i, window, None)
            iteration(B - 1, window, None)
            apply3(B)
            keep_half(2 * B + 1, 1, 1)
            return_inverse(2 * (2 * B + 1) + 1)

            def exp3(n, at):
                wait(act, s_ready3, n + 1)
                nc.scalar.activation(S3[at % 4][:, :, :], S3[at % 4][:, :, :], ACT.Exp,
                                     scale=float(D) ** -0.5).then_inc(e_done3, 1)

            def keep3(n, at):
                wait(act, tr_done3, n + 1)
                nc.scalar.activation(OT[:, :, P * at:P * at + P],
                                     (AV, SUM)[at % 2][:, 0:C].rearrange("p (t q) -> p t q", t=CT),
                                     ACT.Copy).then_inc(ot_done3, 1)

            def slot(b, t):
                n = MT * b + t
                first = isinstance(b, int) and b == 0
                wait(act, qkv3, n + 1)
                wait(act, k_used3, n - 1)
                nc.scalar.activation(QC[t % 2], ST[:, t % 2, 0:C], ACT.Copy).then_inc(copied3, 1)
                wait(act, pv_done3, n - 3)
                nc.scalar.activation(VC[t % 4], V3[t % 2], ACT.Copy).then_inc(copied3, 1)
                if not (first and t < 1):
                    exp3(n - 1, (t - 1) % MT)
                if t == MT - 1 and not (isinstance(b, int) and b == B - 1):
                    apply3(B + b + 1)
                if not (first and t < 3):
                    keep3(n - 3, (t - 3) % MT)

            tile_slots(0, slot)
            with act.Fori(1, B - 1) as b:
                tile_slots(b, slot)
            tile_slots(B - 1, slot)
            exp3(MT * B - 1, MT - 1)
            for n in range(MT * B - 3, MT * B):
                keep3(n, n % MT)

        @block.gpsimd
        def _(pool):
            gn = Tally()

            def norm_factors(batch, scale, bias):
                wait(pool, var_ready, batch + 1)

                def link(ins):
                    ins.then_inc(pool_gn, 1)
                    wait_apart(pool, pool_gn, gn.add(), passed)

                link(nc.gpsimd.tensor_tensor(RSTD[:, :], VE[:, :], MHALF[:, :], ALU.pow))
                link(nc.gpsimd.tensor_tensor(GA[:, :], RSTD[:, :], scale, ALU.mult))
                link(nc.gpsimd.tensor_tensor(GT[:, :], MG[:, :], GA[:, :], ALU.mult))
                link(nc.gpsimd.tensor_tensor(GB[:, :], bias, GT[:, :], ALU.subtract))

            def norm_apply(batch):
                pool.wait_ge(wqk_in, 16)
                norm_factors(batch, GNS, GNB)
                for t in range(CT):
                    nc.gpsimd.tensor_scalar(XN[:, t], XIN[:, t], GA[:, t:t + 1], GB[:, t:t + 1],
                                            ALU.mult, ALU.add).then_inc(xn_ready, 1)

            def window(u, par, jobs, i):
                for s in range(STEPS):
                    half, mt = s // MT, s % MT
                    if mt in POOL_TILES[1:]:
                        rank = POOL_TILES.index(mt)
                        for pair in range(2):
                            wait_apart(pool, exp_done, EXPS * u + H * s + 2 * pair + 2, passed)
                            if rank == 1:
                                wait_apart(pool, half_done, 2 * u + half, passed)
                                so_far = exps(i, s - 1, pair)
                            else:
                                wait_apart(pool, pool_used, 2 * POOL_SUMS * (2 * u + half) + 2 * (rank - 2)
                                           + pair + 1, passed)
                                so_far = ACC[:, pair, :]
                            nc.gpsimd.tensor_tensor(ACC[:, pair, :], so_far, exps(i, s, pair),
                                                    ALU.add).then_inc(pool_used, 1)
                    if jobs and ("gn", 1) in jobs[s]:
                        if par == 0:
                            norm_apply(i + 1)
                        else:
                            pool.wait_ge(w3_in, 16 * 2)
                            norm_factors(B, GNS3, GNB3)

            nc.gpsimd.memset(MHALF[:, :], -0.5)
            window(0, 0, None, None)
            window(1, 1, None, None)
            norm_apply(0)
            window(2, 0, window_jobs(prep=True, gn=True), 0)
            window(3, 1, None, 0)
            with pool.Fori(1, B - 1) as i:
                gn.enter(i - 1, 4)
                iteration(i, window, None)
                gn.leave(TURNS)
            iteration(B - 1, window, None)

            def products(n, at):
                wait(pool, p_ready3, n + 1)
                wait(pool, copied3, 2 * n + 2)
                wait(pool, o_ready3, n - 1)
                nc.gpsimd.tensor_tensor(
                    PV[at % 2].rearrange("p (h d g) -> p h d g", h=NHEAD, d=D),
                    S3[at % 4][:, :, :].unsqueeze(2).broadcast_to([P, NHEAD, D, NHEAD]),
                    VC[at % 4].rearrange("p (g d) -> p d g", d=D).unsqueeze(1).broadcast_to(
                        [P, NHEAD, D, NHEAD]), ALU.mult).then_inc(pv_done3, 1)

            def slot(b, t):
                n = MT * b + t
                if not (isinstance(b, int) and b == 0 and t < 1):
                    products(n - 1, (t - 1) % MT)
                if t == 5 and not (isinstance(b, int) and b == B - 1):
                    norm_factors(B + b + 1, GNS3, GNB3)

            tile_slots(0, slot)
            with pool.Fori(1, B - 1) as b:
                gn.enter(b - 1, 4)
                tile_slots(b, slot)
                gn.leave(TURNS)
            tile_slots(B - 1, slot)
            products(MT * B - 1, MT - 1)

        @block.vector
        def _(dve):
            ring = Tally()
            steps = Tally()
            acts = Tally()

            def link(ins, alone=False):
                ins.then_inc(dve_step, 1)
                if alone:
                    wait_apart(dve, dve_step, steps.add(), passed)
                else:
                    dve.wait_ge(dve_step, steps.add())

            def bank():
                wait(dve, ring_full, ring.add())
                return RING[:, ring.slot(), :]

            def own():
                dve.wait_ge(ring_free, ring.now())

            def split_qk(bias, which, half, u, done):
                src = bank()
                cols = slice(HALF * half, HALF * half + HALF)
                if which == 0 and half == 0:
                    for h in range(H):
                        wait(dve, stk[h], 96 * u)
                link(nc.vector.tensor_scalar(HI[:, which, cols], src, bias, None, ALU.add))
                nc.vector.scalar_tensor_tensor(out=LO[:, which, cols], in0=src, scalar=bias,
                                               in1=HI[:, which, cols].bitcast(f32), op0=ALU.add,
                                               op1=ALU.subtract).then_inc(ring_free, 1)
                if done:
                    own()
                    dve.sem_inc(stage_ready, 1)

            def keep_v(u, par, part, bias):
                src = bank()
                wait(dve, half_done, 2 * (u - 1))
                nc.vector.tensor_tensor(VT[par][:, 4 * part:4 * part + 4, :],
                                        src.rearrange("p (m c) -> p m c", c=P),
                                        bias.unsqueeze(1).broadcast_to([P, 4, P]),
                                        ALU.add).then_inc(ring_free, 1)
                own()
                dve.sem_inc(v_ready, 1)

            def keep_v_l0(u, part):
                nc.vector.tensor_copy(ENC[:, :], bank()).then_inc(ring_free, 1)
                keep_v(u, u, part, ZB[:, :])

            def row_max(u, par, h, t, half):
                nc.vector.tensor_reduce(out=MX[:, h, t, half:half + 1], in_=bank(), op=ALU.max,
                                        axis=AX.X).then_inc(ring_free, 1)
                if t == MT - 1 and half == 1:
                    own()
                    wait(dve, rows_in[h], 2 * 16 * u)
                    link(nc.vector.tensor_reduce(out=NM[:, h, :], in_=MX[:, h], op=ALU.max, axis=AX.X,
                                                 negate=True))
                    link(nc.vector.tensor_copy(NMH[:, h, :], NM[:, h, :]))
                    nc.vector.tensor_tensor(NML[:, h, :], NM[:, h, :], NMH[:, h, :].bitcast(f32),
                                            ALU.subtract).then_inc(negmax_ready, 1)

            def invert(n):
                wait(dve, half_kept, 2 * (n + 1))
                wait(dve, sums_in, 16 * (n + 1))
                nc.vector.reciprocal(R16[:, :], R16[:, :]).then_inc(inverted, 1)

            def normalise(par, half):
                nc.vector.tensor_tensor(OH[par][half], OH[par][half], bank(), ALU.mult).then_inc(ring_free, 1)
                own()
                dve.sem_inc(norm_done, 1)

            def statistics(batch):
                wait(dve, xin_in, 16 * (batch + 1))
                for t in range(CT):
                    for half in range(2):
                        last = nc.vector.bn_stats(BN6[:, t, half, :], XIN[:, t, HALF * half:HALF * half + HALF])
                link(last, alone=True)
                link(nc.vector.bn_aggr(MV[:, 0, :], BN6[:, 0]), alone=True)
                link(nc.vector.bn_aggr(MV[:, 1, :], BN6[:, 1]))
                dve.sem_inc(gn_ready, 1)

            def group_stats(k, batch):
                src = bank()
                if k == 0:
                    nc.vector.tensor_copy(MG[:, :], src[:, 0:CT]).then_inc(ring_free, 1)
                    own()
                    link(nc.vector.tensor_tensor(DEV[:, :], MV[:, :, 0], MG[:, :], ALU.subtract))
                    link(nc.vector.tensor_tensor(S2[:, :], DEV[:, :], DEV[:, :], ALU.mult))
                    link(nc.vector.tensor_tensor(S2[:, :], S2[:, :], MV[:, :, 1], ALU.add))
                    dve.sem_inc(gn_ready, 1)
                else:
                    nc.vector.tensor_scalar(VE[:, :], src[:, 0:CT], EPS, None, ALU.add).then_inc(ring_free, 1)
                    own()
                    dve.sem_inc(var_ready, 1)

            def residual(o, half, batch, bias):
                src = bank()
                cols = slice(HALF * half, HALF * half + HALF)
                if o == 0 and half == 0:
                    wait(dve, xres_in, 16 * (batch + 1))
                nc.vector.scalar_tensor_tensor(out=XRES[:, o, cols], in0=src, scalar=bias[:, o:o + 1],
                                               in1=XRES[:, o, cols], op0=ALU.add,
                                               op1=ALU.add).then_inc(ring_free, 1)
                if o == CT - 1 and half == 1:
                    own()
                    dve.sem_inc(y_ready, 1)

            def window(u, par, jobs, i, trail=True):
                def run(todo):
                    for job in todo:
                        if job[0] == "spread":
                            normalise(1 - par if job[1] else par, 1 if job[1] else 0)
                        elif job[0] == "max":
                            row_max(u + 1, 1 - par, *job[1:])
                        elif job[0] == "v" and i is None:
                            keep_v_l0(1, job[1])
                        elif job[0] == "v":
                            keep_v(u + 1, 1 - par, job[1], BV[:, P * (1 - par):P * (1 - par) + P])
                        elif job[0] == "qk":
                            split_qk(BQK[:, par, job[1]:job[1] + 1], *job[1:], u + 2, job[1:] == (1, 1))
                        elif job[0] == "stats":
                            statistics(i + 1)
                        elif job[0] == "gn":
                            group_stats(job[1], i + 1)
                        elif job[0] == "post":
                            residual(*job[1:], i - 1, BP)
                        else:
                            after(0, job)

                for s in range(STEPS):
                    run(jobs[s][0:3])
                    if s == (1 if par == 1 and i is None else INVERT_AT) and trail:
                        invert(2 * u - 1)
                    if s == MT + INVERT_AT:
                        invert(2 * u)
                    run(jobs[s][3:])

            def reread(dst, src):
                link(nc.vector.transpose(dst.rearrange("p (a c) -> p a c", c=D),
                                         src.rearrange("p (l a) -> p a l", a=D)))
                dve.sem_inc(pe_ready, 1)

            def after(g, stage):
                what, half = stage[0], stage[-1]
                if what == "reread":
                    own()
                    if half == 0:
                        dve.wait_ge(norm_done, 2 * (g + 1))
                    reread(LAT[g], LATC[g])
                elif what == "add":
                    for j in range(H):
                        for t in range(CT):
                            xs = X[:, H * g + j, t, HALF * half:HALF * half + HALF]
                            nc.vector.scalar_tensor_tensor(out=xs, in0=bank(),
                                                           scalar=GAM[:, stage[1]:stage[1] + 1], in1=xs,
                                                           op0=ALU.mult, op1=ALU.add).then_inc(ring_free, 1)
                elif what == "encode":
                    nc.vector.tensor_copy(ENC[:, :], bank()).then_inc(ring_free, 1)
                elif what == "concepts":
                    for n in range(4):
                        src = bank().rearrange("p (j q) -> p j q", q=P)
                        link(nc.vector.tensor_reduce(out=CM4[:, n, :], in_=src, op=ALU.max, axis=AX.X))
                        nc.vector.tensor_tensor(E[g][:, H * n:H * n + H, :], src,
                                                CM4[:, n, :].unsqueeze(2).broadcast_to([P, H, P]),
                                                ALU.subtract).then_inc(ring_free, 1)
                    own()
                    dve.sem_inc(cs_ready, 1)
                elif what == "softmax":
                    dve.wait_ge(act_done, acts.add())
                    link(nc.vector.tensor_reduce(out=CS[:, :], in_=E[g], op=ALU.add, axis=AX.X))
                    link(nc.vector.reciprocal(CR[:, :], CS[:, :]))
                    link(nc.vector.tensor_tensor(E[g], E[g], CR[:, :].unsqueeze(2).broadcast_to([P, 4 * H, P]),
                                                 ALU.mult))
                    dve.sem_inc(pe_ready, 1)
                elif what == "turn":
                    for n in range(4):
                        nc.vector.tensor_copy(PT[g][:, :, P * n:P * n + P],
                                              bank().rearrange("p (j q) -> p j q", q=P)).then_inc(ring_free, 1)
                elif what == "mix":
                    nc.vector.tensor_copy(LATC[g][:, HALF * half:HALF * half + HALF],
                                          bank()).then_inc(ring_free, 1)
                elif what == "classes":
                    for part in range(2):
                        cols = slice(HALF * part, HALF * part + HALF)
                        nc.vector.tensor_scalar(OM[g][:, cols], bank(), CB[:, :], None,
                                                ALU.add).then_inc(ring_free, 1)
                        own()
                        link(nc.vector.tensor_tensor(SQ[g][:, cols], OM[g][:, cols], OM[g][:, cols], ALU.mult))
                    dve.sem_inc(pe_ready, 1)
                elif what == "norms":
                    for part in range(2):
                        nc.vector.tensor_copy(NRM[g][:, HALF * part:HALF * part + HALF],
                                              bank()).then_inc(ring_free, 1)
                    own()
                    dve.sem_inc(cs_ready, 1)
                elif what == "pool":
                    dve.wait_ge(act_done, acts.add())
                    link(nc.vector.reciprocal(NRI[g], NRM[g]))
                    link(nc.vector.scalar_tensor_tensor(out=PRB[g], in0=OM[g], scalar=RW[:, :], in1=NRI[g],
                                                        op0=ALU.mult, op1=ALU.mult))
                    link(nc.vector.tensor_reduce(out=POOLED[:, :], in_=PRB[g], op=ALU.add, axis=AX.X))
                    link(nc.vector.tensor_scalar(PM[:, :], BMASK, POOLED[:, :], 1.0 / N, ALU.mult, ALU.mult))
                    dve.sem_inc(pe_ready, 1)
                elif what == "hidden":
                    nc.vector.tensor_scalar(HID[:, :], bank()[0:4 * K, 0:H], 0.0, None,
                                            ALU.max).then_inc(ring_free, 1)
                elif what == "gates":
                    nc.vector.tensor_copy(ZE[:, :], bank()[:, 0:1]).then_inc(ring_free, 1)
                    own()
                    dve.sem_inc(cs_ready, 1)
                elif what == "regate":
                    dve.wait_ge(act_done, acts.add())
                    link(nc.vector.tensor_tensor(RG[:, :], ZE[:, :], GAM[:, 2:3], ALU.mult))
                    for j in range(H):
                        last = nc.vector.tensor_scalar(CW4[g][:, j, :], CW[:, :], RG[:, :], BMASK[:, j:j + 1],
                                                       ALU.mult, ALU.mult)
                    link(last)
                    dve.sem_inc(pe_ready, 1)
                elif what == "write":
                    j = stage[1]
                    for t in range(CT):
                        for part in range(2):
                            xs = X[:, H * g + j, t, HALF * part:HALF * part + HALF]
                            nc.vector.tensor_tensor(xs, bank(), xs, ALU.add).then_inc(ring_free, 1)
                    if j == H - 1:
                        own()
                        dve.sem_inc(x_final, 1)

            def prepare(jobs):
                for job in jobs:
                    if job[0] == "stats":
                        statistics(0)
                    elif job[0] == "gn":
                        group_stats(job[1], 0)
                    elif job[0] == "qk":
                        if job[1:] == (0, 0, 0):
                            dve.wait_ge(wqk_in, 16)
                        split_qk(BQK[:, job[3], job[1]:job[1] + 1], job[1], job[2], 2 + job[3],
                                 job[1:3] == (1, 1))
                    elif job[0] == "v":
                        dve.wait_ge(wv_in, 16)
                        keep_v(2, 0, job[1], BV[:, 0:P])
                    elif job[0] == "max":
                        row_max(2, 0, *job[1:])

            dve.wait_ge(w_first, 16)
            link(nc.vector.tensor_scalar(WL0[:, :, :], WL0[:, :, :], float(C) ** -0.5, None, ALU.mult))
            dve.sem_inc(scaled, 1)
            nc.vector.memset(WO[:, :, :], 0.0)
            nc.vector.memset(CONT[:, :, :], 0.0)
            nc.vector.memset(CWT[:, :, :], 0.0)
            nc.vector.memset(L1T[:, :], 0.0)
            nc.vector.memset(L2T[:, :], 0.0)
            nc.vector.memset(CB[:, :], 0.0)
            nc.vector.memset(ZB[:, :], 0.0)
            nc.vector.memset(CW[:, :], 1.0)
            nc.vector.memset(ONES[:, :], 1.0)
            for par in range(2):
                link(nc.vector.memset(KS[par][3 * D:3 * D + 2, :, :].bitcast(f32), 1.0))
            dve.sem_inc(zeroed, 1)
            for which in range(2):
                for half in range(2):
                    split_qk(ZB[:, 0:1], which, half, 0, (which, half) == (1, 1))
            keep_v_l0(0, 0)
            dve.wait_ge(w_in, 16 * (4 + 5 * H))
            nc.vector.tensor_scalar(WO[:, :, :], WO[:, :, :], float(D) ** -0.5, None, ALU.mult)
            link(nc.vector.tensor_tensor(CW3[:, :], CW[:, :], CW[:, :], ALU.mult))
            link(nc.vector.tensor_reduce(out=RW[:, :], in_=CW3[:, :], op=ALU.add, axis=AX.X))
            dve.sem_inc(cs_ready, 1)
            for job in START:
                if job[0] == "v":
                    keep_v_l0(0, 1)
                elif job[0] == "qk":
                    split_qk(ZB[:, 0:1], job[1], job[2], 1, job[1:] == (1, 1))
                else:
                    row_max(0, 0, *job[1:])
            dve.wait_ge(act_done, acts.add())
            link(nc.vector.reciprocal(RW[:, :], RWS[:, :]))
            window(0, 0, window_jobs(trail=False), None, trail=False)
            window(1, 1, after_jobs(), None)
            for stage in AFTER[-H:-1]:
                after(0, stage)
            invert(3)
            after(0, AFTER[-1])
            normalise(1, 1)
            between, rest = first_jobs()
            for stage in AFTER:
                after(1, stage)
                prepare(between.get(stage, ()))
            prepare(rest)
            window(2, 0, window_jobs(prep=True, gn=True, trail=False), 0, trail=False)
            window(3, 1, window_jobs(prep=True), 0)
            dve.wait_ge(wp_in, 16)
            with dve.Fori(1, B - 1) as i:
                ring.enter(i - 1, RING_PER)
                steps.enter(i - 1, 8 + 16 + 6)
                iteration(i, window, None)
                ring.leave(TURNS)
                steps.leave(TURNS)
            iteration(B - 1, window, None)
            invert(2 * (2 * B + 1) + 1)
            normalise(1, 1)
            for o in range(CT):
                for half in range(2):
                    residual(o, half, B - 1, BP)

            ring.restart(2)

            def step(ins):
                ins.then_inc(dve_step, 1)
                return steps.add()

            def scores3(n, t, prior):
                grid = [P, NHEAD, NHEAD, D]
                if n is not None:
                    S = S3[t % 4][:, :, :]
                    products = PQ.rearrange("p (h g d) -> p h g d", h=NHEAD, g=NHEAD)
                    wait(dve, copied3, 2 * n + 1)
                    nc.vector.tensor_tensor(
                        products,
                        ST[:, t % 2, C:2 * C].rearrange("p (g d) -> p g d", d=D).unsqueeze(1).broadcast_to(grid),
                        QC[t % 2].rearrange("p (h d) -> p h d", d=D).unsqueeze(2).broadcast_to(grid),
                        ALU.mult).then_inc(k_used3, 1)
                if prior is not None:
                    E3 = S3[(t - 1) % 4][:, :, :]
                    wait(dve, e_done3, prior + 1)
                    summed = step(nc.vector.tensor_reduce(out=R3[:, 0, :], in_=E3, op=ALU.add, axis=AX.X))
                if n is not None:
                    wait(dve, k_used3, n + 1)
                    wait(dve, pv_done3, n - 3)
                    scored = step(nc.vector.tensor_reduce(out=S, in_=products, op=ALU.add, axis=AX.X))
                if prior is not None:
                    wait(dve, dve_step, summed)
                    inverted = step(nc.vector.reciprocal(R3[:, 1, :], R3[:, 0, :]))
                if n is not None:
                    wait(dve, dve_step, scored)
                    largest = step(nc.vector.tensor_reduce(out=M3[:, :], in_=S, op=ALU.max, axis=AX.X))
                if prior is not None:
                    wait(dve, dve_step, inverted)
                    nc.vector.tensor_tensor(E3, E3, R3[:, 1, :].unsqueeze(2).broadcast_to([P, NHEAD, NHEAD]),
                                            ALU.mult).then_inc(p_ready3, 1)
                if n is not None:
                    wait(dve, dve_step, largest)
                    nc.vector.tensor_tensor(S, S, M3[:, :].unsqueeze(2).broadcast_to([P, NHEAD, NHEAD]),
                                            ALU.subtract).then_inc(s_ready3, 1)

            def outputs3(n, at):
                wait(dve, pv_done3, n + 1)
                wait(dve, tr_done3, n - 1)
                nc.vector.tensor_reduce(out=O3[at % 2],
                                        in_=PV[at % 2].rearrange("p (c g) -> p c g", g=NHEAD),
                                        op=ALU.add, axis=AX.X).then_inc(o_ready3, 1)

            def slot(b, t):
                n = MT * b + t
                first, last = isinstance(b, int) and b == 0, isinstance(b, int) and b == B - 1
                scores3(n, t, None if first and t < 1 else n - 1)
                if not (first and t < 2):
                    outputs3(n - 2, (t - 2) % MT)
                if t == 3 and not first:
                    for o in range(CT):
                        residual(o, 1, B + b - 1, BP3)
                if t == 7:
                    for o in range(CT):
                        residual(o, 0, B + b, BP3)
                if t == 2 and not last:
                    statistics(B + b + 1)
                if t in (3, 4) and not last:
                    group_stats(t - 3, B + b + 1)

            dve.wait_ge(w3_in, 16 * 3)
            link(nc.vector.tensor_scalar(B3N, B3, -1.0, None, ALU.mult))
            link(nc.vector.scalar_tensor_tensor(out=B3S, in0=B3N.bitcast(f32),
                                                scalar=IDENT[TWO, 3 * D + 1:3 * D + 2],
                                                in1=B3, op0=ALU.mult, op1=ALU.add))
            dve.sem_inc(pe_ready, 1)
            tile_slots(0, slot)
            with dve.Fori(1, B - 1) as b:
                ring.enter(b - 1, 6)
                steps.enter(b - 1, 16 + 16 + 6)
                tile_slots(b, slot)
                ring.leave(TURNS)
                steps.leave(TURNS)
            tile_slots(B - 1, slot)
            scores3(None, MT, MT * B - 1)
            for n in range(MT * B - 2, MT * B):
                outputs3(n, n % MT)
            for o in range(CT):
                residual(o, 1, 2 * B - 1, BP3)


def kernel(**inputs):
    import numpy as np
    import concourse.bacc as bacc
    from concourse.bass_utils import run_bass_kernel_spmd

    a = {k: np.asarray(v) for k, v in inputs.items()}

    def column(v):
        return v.reshape(CT, P).T

    def rows(w):
        return w.T.reshape(CT, P, C).transpose(1, 0, 2)

    def packs(wq, wk, wv, wp, bq, bk, bv, bp, scale, bias):
        qk = np.stack([rows(wq).reshape(P, CT, 2, P), rows(wk).reshape(P, CT, 2, P)], axis=3)
        bqk = np.stack([column(bq), column(bk)], axis=2)
        return (np.concatenate([qk.reshape(P, -1), bqk.reshape(P, -1), column(scale), column(bias)], axis=1),
                np.concatenate([rows(wv).reshape(P, -1), np.broadcast_to(bv[None], (P, C))], axis=1),
                np.concatenate([rows(wp).reshape(P, -1), column(bp)], axis=1))

    w2 = a["L2_conv_w_qkv"].reshape(C // D, 3, D, C)
    b2 = a["L2_conv_b_qkv"].reshape(C // D, 3, D)
    p2 = packs(*(w2[:, n].reshape(C, C) for n in range(3)), a["L2_conv_w_proj"],
               *(b2[:, n].reshape(C) for n in range(3)), a["L2_conv_b_proj"],
               a["L2_conv_gn_scale"], a["L2_conv_gn_bias"])
    eye = np.eye(P)
    block = np.kron(np.eye(H), np.ones((D, D)))
    spread = block * (np.arange(P) % D == 0)[:, None]
    consts = np.concatenate([eye, np.kron(np.eye(P // 8), np.full((8, 8), 0.125)), block, block[:, ::D], spread],
                            axis=1).astype(np.float32)
    arrays = {
        "x": a["x"].reshape(B, C, N),
        "w_l0": np.concatenate([a["L0_conv_w_theta"], a["L0_conv_w_phi"], a["L0_conv_w_g"]], axis=0).T,
        "w_o": a["L0_conv_w_o"].T,
        "concepts": a["L0_conv_concepts"],
        "concepts_t": a["L0_conv_concepts"].T,
        "gammas": np.concatenate([a["L0_conv_gamma_sa"].reshape(1, 1), a["L0_conv_gamma_moca"].reshape(1, 1),
                                  a["L1_conv_gamma"].reshape(1, 1)], axis=1),
        "conv_w": a["L1_conv_conv_w"],
        "conv_wt": a["L1_conv_conv_w"].T,
        "conv_b": a["L1_conv_conv_b"].reshape(K, 1),
        "lin1_t": a["L1_conv_lin1_w"].T,
        "lin2_t": a["L1_conv_lin2_w"].T,
        "qk_pack": p2[0],
        "v_pack": p2[1],
        "p_pack": p2[2],
        "w3_pack": a["L3_conv_qkv_w"].T.reshape(CT, P, 3 * C).transpose(1, 0, 2).reshape(P, -1),
        "b3_row": a["L3_conv_qkv_b"].reshape(1, 3 * C),
        "p3_pack": np.concatenate([rows(a["L3_conv_proj_w"]).reshape(P, -1), column(a["L3_conv_proj_b"]),
                                   column(a["L3_conv_norm_w"]), column(a["L3_conv_norm_b"])], axis=1),
        "consts": consts,
    }
    nc = bacc.Bacc("TRN2", target_bir_lowering=False, num_devices=1)
    args, fed = [], {}
    for name, v in arrays.items():
        v = np.ascontiguousarray(v)
        fed[f"in_{name}"] = v
        args.append(nc.dram_tensor(f"in_{name}", v.shape, mybir.dt.from_np(v.dtype), kind="ExternalInput").ap())
    args.append(nc.dram_tensor("out_y", (B, C, N), mybir.dt.float32, kind="ExternalOutput").ap())
    program(nc, *args)
    r = run_bass_kernel_spmd(nc, [fed], core_ids=[0])
    return r.results[0]["out_y"].reshape(B, C, 32, 32)
```
